# Optimizing a Trainium2 kernel written in Bass

```python
import numpy as np
import jax
import jax.numpy as jnp

def _softmax(x, axis=-1):
    return jax.nn.softmax(x, axis=axis)

def _gelu(x):
    return jax.nn.gelu(x, approximate=True)

def _silu(x):
    return jax.nn.silu(x)

def _sigmoid(x):
    return jax.nn.sigmoid(x)

def _layernorm(x, axis=-1, eps=1e-05):
    m = jnp.mean(x, axis=axis, keepdims=True)
    v = jnp.var(x, axis=axis, keepdims=True)
    return (x - m) / jnp.sqrt(v + eps)

def _scatter_add(tgt, idx, src, axis=0):
    return tgt.at[idx].add(src)

def _segment_sum(src, seg, n):
    return jax.ops.segment_sum(src, seg, n)
kernel_name = 'mk_flamingo_gated_d1_seqx_r4_d23034'

def setup_inputs(seed: int=0):
    np.random.seed(seed)
    _w = jnp.asarray

    def _rec_inputs():
        import jax
        import jax.numpy as jnp
        _rk = jax.random.key(seed)
        x = 7.22e-05 + 1 * jax.random.normal(jax.random.fold_in(_rk, 1), (32, 128, 256), jnp.float32)
        _lenS = 128 - jax.random.randint(jax.random.fold_in(_rk, 7), (32,), 0, max(1, 128 // 4) + 1, jnp.int32)
        _lenS2 = 128 - jax.random.randint(jax.random.fold_in(_rk, 8), (32,), 0, max(1, 128 // 4) + 1, jnp.int32)
        _ctx_1024P = jax.random.normal(jax.random.fold_in(_rk, 11), (32, 16, 256), jnp.float32)
        _ctx_1024c = jax.random.dirichlet(jax.random.fold_in(_rk, 511), 0.3 * jnp.ones((16,), jnp.float32), (32, 128))
        _ctx_1024t = jnp.einsum('bsk,bkd->bsd', _ctx_1024c, _ctx_1024P)
        _ctx_1024t = _ctx_1024t * jax.lax.rsqrt(jnp.mean(jnp.square(_ctx_1024t)) + 1e-12) * 0.953939
        ctx_1024 = 4.13588e-05 + 0.999923 * (_ctx_1024t + 0.3 * jax.random.normal(jax.random.fold_in(_rk, 611), (32, 128, 256), jnp.float32))
        _g = jax.random.normal(jax.random.fold_in(_rk, 9001), (2, 1), jnp.float32)
        _g = jnp.sign(_g) * jnp.maximum(jnp.abs(_g), 1.0) + (_g == 0) * 1.0
        g_xattn = _g[0]
        g_ffn = _g[1]
        return (x, ctx_1024, g_xattn, g_ffn)
    x, ctx_1024, g_xattn, g_ffn = _rec_inputs()

    def _L0_xattn_setup():
        import jax, jax.numpy as jnp
        import numpy as np
        from jax import lax
        NUM_HEADS = 16
        DIM = 256
        BATCH = 4
        SEQ = 512
        key = jax.random.key(seed)
        ks = jax.random.split(key, 12)
        f32 = jnp.float32
        q = jax.random.normal(ks[0], (BATCH, SEQ, DIM), dtype=f32)
        k = jax.random.normal(ks[1], (BATCH, SEQ, DIM), dtype=f32)
        v = jax.random.normal(ks[2], (BATCH, SEQ, DIM), dtype=f32)
        lim = 1.0 / np.sqrt(DIM)
        Wi = jax.random.uniform(ks[3], (DIM, DIM), minval=-lim, maxval=lim, dtype=f32)
        bi = jax.random.uniform(ks[4], (DIM,), minval=-lim, maxval=lim, dtype=f32)
        Wg = jax.random.uniform(ks[5], (DIM, DIM), minval=-lim, maxval=lim, dtype=f32)
        bg = jax.random.uniform(ks[6], (DIM,), minval=-lim, maxval=lim, dtype=f32)
        Wo = jax.random.uniform(ks[7], (DIM, DIM), minval=-lim, maxval=lim, dtype=f32)
        bo = jax.random.uniform(ks[8], (DIM,), minval=-lim, maxval=lim, dtype=f32)
        A = jax.random.normal(ks[9], (DIM, DIM), dtype=f32) * 0.1
        Bm = jax.random.normal(ks[10], (DIM, DIM), dtype=f32) * 0.1
        decay = jnp.full((1, NUM_HEADS, 1), 0.9, dtype=f32)
        return dict(q=q, k=k, v=v, Wi=Wi, bi=bi, Wg=Wg, bg=bg, A=A, Bm=Bm, Wo=Wo, bo=bo, decay=decay)
    _L0_xattn_all = _L0_xattn_setup()
    _L0_xattn_in = {k: v for k, v in _L0_xattn_all.items() if k in ('Wi', 'bi', 'Wg', 'bg', 'A', 'Bm', 'Wo', 'bo', 'decay')}
    del _L0_xattn_all

    def _L0_ffn_setup():
        import jax, jax.numpy as jnp
        import numpy as np
        B, T, C, H, E, K = (4, 256, 256, 256, 8, 2)

        def _swiglu(x):
            a, b = jnp.split(x, 2, axis=-1)
            return jax.nn.silu(a) * b
        key = jax.random.key(seed)
        ks = jax.random.split(key, 6)
        s = 0.02
        x = jax.random.normal(ks[0], (B, T, C), jnp.float32)
        w_shared_in = jax.random.normal(ks[1], (C, 2 * H), jnp.float32) * s
        w_shared_out = jax.random.normal(ks[2], (H, C), jnp.float32) * s
        w1_shared = jax.random.normal(ks[3], (C, 2 * H), jnp.float32) * s
        w2 = jax.random.normal(ks[4], (E, H, C), jnp.float32) * s
        w_gate = jax.random.normal(ks[5], (C, E), jnp.float32) * s
        gate_bias = jnp.zeros((E,), jnp.float32)
        return {'x': x, 'w_shared_in': w_shared_in, 'w_shared_out': w_shared_out, 'w1_shared': w1_shared, 'w2': w2, 'w_gate': w_gate, 'gate_bias': gate_bias}
    _L0_ffn_all = _L0_ffn_setup()
    _L0_ffn_in = {k: v for k, v in _L0_ffn_all.items() if k in ('w_shared_in', 'w_shared_out', 'w1_shared', 'w2', 'w_gate', 'gate_bias')}
    del _L0_ffn_all
    return {'x': x, 'ctx_1024': ctx_1024, 'g_xattn': g_xattn, 'g_ffn': g_ffn, 'L0_xattn_Wi': _L0_xattn_in['Wi'], 'L0_xattn_bi': _L0_xattn_in['bi'], 'L0_xattn_Wg': _L0_xattn_in['Wg'], 'L0_xattn_bg': _L0_xattn_in['bg'], 'L0_xattn_A': _L0_xattn_in['A'], 'L0_xattn_Bm': _L0_xattn_in['Bm'], 'L0_xattn_Wo': _L0_xattn_in['Wo'], 'L0_xattn_bo': _L0_xattn_in['bo'], 'L0_xattn_decay': _L0_xattn_in['decay'], 'L0_ffn_w_shared_in': _L0_ffn_in['w_shared_in'], 'L0_ffn_w_shared_out': _L0_ffn_in['w_shared_out'], 'L0_ffn_w1_shared': _L0_ffn_in['w1_shared'], 'L0_ffn_w2': _L0_ffn_in['w2'], 'L0_ffn_w_gate': _L0_ffn_in['w_gate'], 'L0_ffn_gate_bias': _L0_ffn_in['gate_bias']}

def reference(x, ctx_1024, g_xattn, g_ffn, L0_xattn_Wi, L0_xattn_bi, L0_xattn_Wg, L0_xattn_bg, L0_xattn_A, L0_xattn_Bm, L0_xattn_Wo, L0_xattn_bo, L0_xattn_decay, L0_ffn_w_shared_in, L0_ffn_w_shared_out, L0_ffn_w1_shared, L0_ffn_w2, L0_ffn_w_gate, L0_ffn_gate_bias):
    import jax
    import jax.numpy as jnp

    def _L0_xattn_ref(q, k, v, Wi, bi, Wg, bg, A, Bm, Wo, bo, decay):
        import jax, jax.numpy as jnp
        import numpy as np
        from jax import lax
        NUM_HEADS = 16
        DIM = 256
        BATCH = 4
        SEQ = 512
        B, S, D = q.shape
        H = decay.shape[1]
        hd = D // H
        qh = jnp.moveaxis(q.reshape(B, S, H, hd), 1, 0)
        kh = jnp.moveaxis(k.reshape(B, S, H, hd), 1, 0)
        vh = jnp.moveaxis(v.reshape(B, S, H, hd), 1, 0)

        def step(carry, xs):
            r, state = carry
            qt, kt, vt = xs
            r = decay * r + kt * vt
            retained = (qt * r).reshape(B, D)
            inp = retained @ Wi.T + bi
            gate = jax.nn.sigmoid(inp @ Wg.T + bg)
            blended = gate * state + (1.0 - gate) * inp
            state = jnp.tanh(blended @ A.T + inp @ Bm.T)
            out = state @ Wo.T + bo
            return ((r, state), out)
        r0 = jnp.zeros((B, H, hd), dtype=q.dtype)
        s0 = jnp.zeros((B, D), dtype=q.dtype)
        _, outs = lax.scan(step, (r0, s0), (qh, kh, vh))
        return jnp.moveaxis(outs, 0, 1)

    def _L0_ffn_ref(x, w_shared_in, w_shared_out, w1_shared, w2, w_gate, gate_bias):
        import jax, jax.numpy as jnp
        import numpy as np
        B, T, C, H, E, K = (4, 256, 256, 256, 8, 2)

        def _swiglu(x):
            a, b = jnp.split(x, 2, axis=-1)
            return jax.nn.silu(a) * b
        Bx, Tx, Cx = x.shape
        S = Bx * Tx
        fx = x.reshape(S, Cx)
        shared_out = _swiglu(fx @ w_shared_in) @ w_shared_out
        logits = fx @ w_gate + gate_bias
        probs = jax.nn.softmax(logits, axis=-1)
        top_val, top_idx = jax.lax.top_k(probs, K)
        wdense = jnp.zeros((S, E), probs.dtype).at[jnp.arange(S)[:, None], top_idx].add(top_val)
        hid = _swiglu(fx @ w1_shared)
        routed_out = jnp.zeros_like(shared_out)
        for e in range(E):
            routed_out = routed_out + wdense[:, e:e + 1] * (hid @ w2[e])
        return (shared_out + routed_out).reshape(Bx, Tx, Cx)
    x = x + jnp.tanh(g_xattn[0]) * _L0_xattn_ref(_layernorm(x, axis=-1), ctx_1024, ctx_1024, L0_xattn_Wi, L0_xattn_bi, L0_xattn_Wg, L0_xattn_bg, L0_xattn_A, L0_xattn_Bm, L0_xattn_Wo, L0_xattn_bo, L0_xattn_decay)
    x = x + jnp.tanh(g_ffn[0]) * _L0_ffn_ref(_layernorm(x, axis=-1), L0_ffn_w_shared_in, L0_ffn_w_shared_out, L0_ffn_w1_shared, L0_ffn_w2, L0_ffn_w_gate, L0_ffn_gate_bias)
    return x

_drawn_inputs = setup_inputs


def setup_inputs(seed=0):
    import zlib

    import numpy as np

    out = dict(_drawn_inputs(seed))
    spreads = {'L0_xattn_decay': (0.8999999761581421, 0.2), 'L0_ffn_gate_bias': (0.0, 0.8)}
    factors = {'L0_xattn_bi': 8.0,
     'L0_xattn_bg': 8.0,
     'L0_ffn_w_shared_in': 3.861,
     'L0_ffn_w_shared_out': 3.861,
     'L0_ffn_w1_shared': 8.0,
     'L0_ffn_w2': 8.0,
     'L0_ffn_w_gate': 8.0}
    for name, (base, spread) in spreads.items():
        noise = np.random.default_rng([zlib.crc32(name.encode()), seed]).standard_normal(out[name].shape)
        drawn = base * np.exp(spread * noise) if base else spread * noise
        out[name] = jnp.asarray(drawn.astype(out[name].dtype))
    for name, factor in factors.items():
        out[name] = (out[name] * factor).astype(out[name].dtype)
    return out
```

```python
from contextlib import ExitStack

import concourse.bass as bass
from concourse import mybir

F32 = mybir.dt.float32
F32R = mybir.dt.float32r
F16 = mybir.dt.float16
ALU = mybir.AluOpType
ACT = mybir.ActivationFunctionType
AX_X = mybir.AxisListType.X

P = 128
B, S, D = 32, 128, 256
KC = D // P
HEADS = 16
E = 8
STEPS = 8
HALVES = 2
J = STEPS // HALVES
TOK = STEPS * B
TILES = S // STEPS
EPS = 1e-5
PSCALE = 256.0


def gated_layer(nc, x, ctx_in, g_xattn, g_ffn, Wi, bi, Wg, bg, A, Bm, Wo, bo, decay,
                w_shared_in, w_shared_out, w1_shared, w2, w_gate, gate_bias, out):
    with ExitStack() as stack:
        def sb(name, shape, dt=F32):
            return stack.enter_context(nc.sbuf_tensor(name, shape, dt))

        def two(name, shape, dt=F32):
            return [sb(f"{name}{n}", shape, dt) for n in range(2)]

        def one(name, shape, dt=F32):
            return [sb(name, shape, dt)] * 2

        def sem(name):
            return stack.enter_context(nc.semaphore(name))

        x_tiles = x.rearrange("b (u j s) d -> u b j (s d)", j=J, s=HALVES)
        c_tiles = ctx_in.rearrange("b (u j s) d -> u b j (s d)", j=J, s=HALVES)
        o_tiles = out.rearrange("b (u j s) d -> u b j (s d)", j=J, s=HALVES)

        raw_sq = {n: sb(f"raw_{n}", [P, KC, D]) for n in ("Wi", "Wg", "Bm", "A", "Wo", "so")}
        raw_wide = {n: sb(f"raw_{n}", [P, KC, 2 * D]) for n in ("sh", "w1")}
        raw_wgate = sb("raw_wgate", [P, KC, E])
        rows = sb("rows", [4, P])
        cols = sb("cols", [P, 4])
        bi_wide = sb("bi_wide", [P, KC, P])
        WgT = sb("WgT", [P, KC, D])
        BmT = sb("BmT", [P, KC, D])
        split = {}
        for n in ("inp", "gate", "bm", "a", "wo", "so"):
            split[n] = (sb(f"{n}_hi", [P, KC, D], F32R), sb(f"{n}_lo", [P, KC, D], F32R))
        for n in ("sh", "w1"):
            split[n] = (sb(f"{n}_hi", [P, KC, 2 * D], F32R), sb(f"{n}_lo", [P, KC, 2 * D], F32R))
        split["w2"] = (sb("w2_hi", [P, KC, E, D], F32R), sb("w2_lo", [P, KC, E, D], F32R))
        split["wgate"] = (sb("wgate_hi", [P, KC, P], F32R), sb("wgate_lo", [P, KC, P], F32R))
        tmp_w = sb("tmp_w", [P, KC * D])
        tmp_a = sb("tmp_a", [P, KC * D])
        tmp_s = sb("tmp_s", [P, KC * D])
        raw_w2 = [raw_sq[n] for n in ("Wi", "Wg", "Bm", "A", "Wo")] + [WgT, BmT, sb("raw_last", [P, KC, D])]
        a16 = (sb("a16_hi", [P, KC, D], F16), sb("a16_lo", [P, KC, D], F16))
        cp = sb("cp", [P, D], F32R)
        cp_row = sb("cp_row", [P, D])
        cp_hi = sb("cp_hi", [P, D], F32R)
        ones = sb("ones", [P, TOK], F32R)
        ident = sb("ident", [P, P])
        minus_half = sb("minus_half", [P, HALVES])
        half_gate_bias = sb("half_gate_bias", [P, KC])
        gx = sb("gx", [P, 1])
        gf = sb("gf", [P, 1])
        tgx = sb("tgx", [P, 1])
        tgf = sb("tgf", [P, 1])
        bo_all = sb("bo_all", [P, D])
        tgbo = sb("tgbo", [P, D])
        gb_all = sb("gb_all", [P, E])
        dec8 = sb("dec8", [2, HEADS // KC])
        dec_rows = sb("dec_rows", [2, P])
        dec_cols = sb("dec_cols", [P, KC])
        dmask = sb("dmask", [P, KC, B, STEPS + 1])
        tri = sb("tri", [P, E, E])

        x_sb = two("x_sb", [P, HALVES * D])
        c_sb = two("c_sb", [P, HALVES * D])
        xr_sb = two("xr_sb", [P, HALVES * D])
        xn1 = one("xn1", [P, HALVES, D])
        c2 = one("c2", [P, KC, B, STEPS + 1])
        r = two("r", [P, KC, B, STEPS + 1])
        ret = one("ret", [P, KC, TOK])
        ret_s = [(sb("ret_hi", [P, KC, TOK], F32R), sb("ret_lo", [P, KC, TOK], F32R))] * 2
        gt = two("gt", [P, KC, TOK])
        inp = one("inp_sb", [P, KC, TOK])
        cn = one("cn", [P, KC, TOK])
        cn_s = [(sb("cn_hi", [P, KC, TOK], F32R), sb("cn_lo", [P, KC, TOK], F32R))] * 2
        state = two("state", [P, KC, TOK])
        st_s = [(sb("st_hi", [P, KC, TOK], F32R), sb("st_lo", [P, KC, TOK], F32R))] * 2
        u_hi = two("u_hi", [P, KC, B], F16)
        u_lo = two("u_lo", [P, KC, B], F16)
        u_full = two("u_full", [P, KC, B])
        x1 = two("x1", [P, HALVES, D])
        xn2 = one("xn2", [P, HALVES, D])
        xn2_s = [(sb("xn2_hi", [P, KC, TOK], F32R), sb("xn2_lo", [P, KC, TOK], F32R))] * 2
        sil_s = sb("sil_s", [P, KC, TOK])
        sil_w = sb("sil_w", [P, KC, TOK])
        hs = sb("hs", [P, KC, TOK])
        hid = sb("hid", [P, KC, TOK])
        hs_s = (sb("hs_hi", [P, KC, TOK], F32R), sb("hs_lo", [P, KC, TOK], F32R))
        hid_s = [(sb(f"hid_hi{n}", [P, KC, TOK], F32R), sb(f"hid_lo{n}", [P, KC, TOK], F32R)) for n in range(2)]
        acc = two("acc", [P, HALVES, D])
        st1 = two("st1", [P, HALVES, 6])
        mv1 = two("mv1", [P, HALVES, 2])
        ve1 = two("ve1", [P, HALVES])
        nm1 = two("nm1", [P, HALVES])
        rs1 = two("rs1", [P, HALVES])
        nr1 = two("nr1", [P, HALVES])
        st2 = two("st2", [P, HALVES, 6])
        mv2 = two("mv2", [P, HALVES, 2])
        ve2 = two("ve2", [P, HALVES])
        nm2 = two("nm2", [P, HALVES])
        rs2 = two("rs2", [P, HALVES])
        nr2 = two("nr2", [P, HALVES])
        lg_f = sb("lg_f", [P, TOK])
        lg = sb("lg", [P, HALVES, E])
        lmax = sb("lmax", [P, HALVES])
        ld = sb("ld", [P, HALVES, E])
        lt = sb("lt", [P, HALVES, E])
        num = sb("num", [P, HALVES, E])
        den = sb("den", [P, HALVES, E])
        rden = sb("rden", [P, HALVES, E])
        ex = sb("ex", [P, HALVES, E])
        esum = sb("esum", [P, HALVES])
        rsum = sb("rsum", [P, HALVES])
        rsg = sb("rsg", [P, HALVES])
        more = sb("more", [P, HALVES, E, E])
        same = sb("same", [P, HALVES, E, E])
        same_l = sb("same_l", [P, HALVES, E, E])
        beat = sb("beat", [P, HALVES, E, E])
        b4 = sb("b4", [P, HALVES * E, 4])
        b2 = sb("b2", [P, HALVES * E, 2])
        rank = sb("rank", [P, HALVES, E])
        picked = sb("picked", [P, HALVES, E])
        wts = two("wts", [P, HALVES, E])

        rec = [stack.enter_context(nc.psum_tensor(f"rec{n}", [P, KC, TOK], F32)) for n in range(2)]
        bank = [stack.enter_context(nc.psum_tensor(f"bank{n}", [P, 512], F32)) for n in range(6)]

        load = {n: sem(f"load_{n}") for n in
                ("Wi", "Wg", "Bm", "A", "Wo", "so", "sh", "w1", "w2", "wgate", "small")}
        x_in = [sem("x_in0"), sem("x_in1")]
        c_in = [sem("c_in0"), sem("c_in1")]
        xr_in = [sem("xr_in0"), sem("xr_in1")]
        out_done = [sem("out_done0"), sem("out_done1")]
        consts = sem("consts")
        zeros = sem("zeros")
        setup_pe = sem("setup_pe")
        setup_dve = sem("setup_dve")
        setup_act = sem("setup_act")
        early_ready = sem("early_ready")
        wide_hi = sem("wide_hi")
        wide_ready = sem("wide_ready")
        w2_hi_done = sem("w2_hi_done")
        w2_ready = sem("w2_ready")
        ln1_stats, ln1_aggr, ln1_var, ln1_rstd, ln1_shift, xn1_ready = (sem(n) for n in ("ln1_stats", "ln1_aggr", "ln1_var", "ln1_rstd", "ln1_shift", "xn1_ready"))
        tc_done, tx_done = sem("tc_done"), sem("tx_done")
        c2_ready, r_ready, ret_ready, ret_hi, ret_lo = (sem(n) for n in ("c2_ready", "r_ready", "ret_ready", "ret_hi_ready", "ret_lo_ready"))
        inp_done, gate_done = sem("inp_done"), sem("gate_done")
        gt_ready, inp_ready, cn_ready, cn_hi, cn_lo = (sem(n) for n in ("gt_ready", "inp_ready", "cn_ready", "cn_hi_ready", "cn_lo_ready"))
        bm_done = sem("bm_done")
        ac_done = sem("ac_done")
        uh_ready = [sem(f"uh_ready{t}") for t in range(STEPS)]
        ul_ready = [sem(f"ul_ready{t}") for t in range(STEPS)]
        sum_done = [sem(f"sum_done{t}") for t in range(STEPS)]
        st_ready = [sem(f"st_ready{t}") for t in range(STEPS)]
        st_hi, st_lo = sem("st_hi_ready"), sem("st_lo_ready")
        xr_ready = sem("xr_ready")
        wo_done, x1_ready, ln2_stats, ln2_aggr, ln2_var, ln2_rstd, ln2_shift, xn2_ready = (
            sem(n) for n in ("wo_done", "x1_ready", "ln2_stats", "ln2_aggr", "ln2_var", "ln2_rstd", "ln2_shift", "xn2_ready"))
        t2_done, xn2_hi, xn2_lo = sem("t2_done"), sem("xn2_hi_ready"), sem("xn2_lo_ready")
        sh_done, w1_done = sem("sh_done"), sem("w1_done")
        sil_s_ready, sil_w_ready, hs_ready, hid_ready = (sem(n) for n in ("sil_s_ready", "sil_w_ready", "hs_ready", "hid_ready"))
        hs_hi, hs_lo, hid_hi, hid_lo = (sem(n) for n in ("hs_hi_ready", "hs_lo_ready", "hid_hi_ready", "hid_lo_ready"))
        lg_done, lg_f_ready, lgt_done, lg_ready = (sem(n) for n in ("lg_done", "lg_f_ready", "lgt_done", "lg_ready"))
        lmax_ready, ld_ready, lt_ready = sem("lmax_ready"), sem("ld_ready"), sem("lt_ready")
        numden, rden_ready, ex_ready, esum_ready, rsum_ready, rsg_ready = (
            sem(n) for n in ("numden_ready", "rden_ready", "ex_ready", "esum_ready", "rsum_ready", "rsg_ready"))
        same_ready, samel_ready, beat_ready, rank_ready, picked_ready, wts_ready = (
            sem(n) for n in ("same_ready", "samel_ready", "beat_ready", "rank_ready", "picked_ready", "wts_ready"))
        so_done, acc_ready = sem("so_done"), sem("acc_ready")
        b4_ready, b2_ready = sem("b4_ready"), sem("b2_ready")
        pair_done = [sem(f"pair_done{k}") for k in range(E)]
        pair_half = [sem(f"pair_half{k}") for k in range(E)]
        pair_used = [sem(f"pair_used{k}") for k in range(E)]

        SMALL = 16 * 7

        B_TC, B_TX, B_LGT, B_WO, B_SO, B_INP, B_GATE, B_T2, B_LG = 0, 1, 2, 4, 0, 2, 3, 0, 3
        B_SHA, B_SHB, B_W1A, B_W1B = 0, 1, 4, 5
        B_PAIR = [4, 1, 2, 4, 5, 3, 5, 1]

        def halves(ap):
            return ap.rearrange("p (s b j) -> p s b j", s=HALVES, b=B)

        def by_time(ap):
            return ap.rearrange("p b (j s) -> p s b j", s=HALVES)

        def step_of(t3, t):
            return t3[:, :, :].rearrange("p c (s b j) -> p c s b j", s=HALVES, b=B)[:, :, t % HALVES, :, t // HALVES]

        def flat(t3):
            return t3.rearrange("p a b -> p (a b)")

        class Static:

            def n(self, m):
                return m + 1

            def dma(self, m):
                return 16 * (m // 2 + 1)

            def has(self, m):
                return 0 <= m < TILES

            def tile(self, m):
                return m

        class Looped:

            def __init__(self, eng, reg):
                self.eng, self.reg, self.known = eng, reg, {}

            def kept(self, key, value):
                if key not in self.known:
                    self.known[key] = self.eng.snap(value)
                return self.known[key]

            def n(self, m):
                return self.kept(("n", m), self.reg * 2 + (m + 1))

            def dma(self, m):
                return self.kept(("dma", m // 2), self.reg * 16 + 16 * (m // 2 + 1))

            def has(self, m):
                return True

            def tile(self, m):
                return self.reg * 2 + m

        FIRST_FULL, LAST_FULL = 3, TILES - 4
        HEAD = range(-2, FIRST_FULL)
        TAIL = range(LAST_FULL + 1, TILES + 3)

        def run(eng, iteration, between=lambda i: None):
            for i in HEAD:
                iteration(i, Static())
                between(i)
            with eng.Fori(FIRST_FULL // 2, LAST_FULL // 2) as reg:
                k = Looped(eng, reg)
                iteration(1, k)
                iteration(2, k)
            for i in TAIL:
                iteration(i, Static())

        block = stack.enter_context(nc.Block())

        @block.sync
        def _(sp):
            def part(t2):
                return t2[:, :].rearrange("(b j) e -> b j e", j=J)

            def load_x(m, k):
                sp.dma_start(x_sb[m % 2][:, :], x_tiles[k.tile(m)]).then_inc(x_in[m % 2], 16)

            def load_c(m, k):
                sp.dma_start(c_sb[m % 2][:, :], c_tiles[k.tile(m)]).then_inc(c_in[m % 2], 16)

            with nc.allow_non_contiguous_dma(reason="small vectors"):
                sp.dma_start(raw_sq["Wi"][:, :, :], Wi.rearrange("(k p) i -> p k i", p=P)).then_inc(load["Wi"], 16)
                sp.dma_start(rows[0:2, :], bi.rearrange("(k p) -> k p", p=P)).then_inc(load["small"], 16)
                sp.dma_start(rows[2:4, :], bg.rearrange("(k p) -> k p", p=P)).then_inc(load["small"], 16)
                sp.dma_start(dec8[:, :], decay.rearrange("a (k h) c -> (a k) (h c)", k=KC)).then_inc(load["small"], 16)
                sp.dma_start(gx[:, :], g_xattn.partition_broadcast(P)).then_inc(load["small"], 16)
                sp.dma_start(gf[:, :], g_ffn.partition_broadcast(P)).then_inc(load["small"], 16)
                sp.dma_start(bo_all[:, :], bo.partition_broadcast(P)).then_inc(load["small"], 16)
                sp.dma_start(gb_all[:, :], gate_bias.partition_broadcast(P)).then_inc(load["small"], 16)
                load_x(0, Static())
                for n, w in (("Wg", Wg), ("Bm", Bm), ("A", A), ("Wo", Wo)):
                    sp.dma_start(raw_sq[n][:, :, :], w.rearrange("(k p) i -> p k i", p=P)).then_inc(load[n], 16)
                load_c(0, Static())
                sp.dma_start(raw_wgate[:, :, :], w_gate.rearrange("(k p) e -> p k e", p=P)).then_inc(load["wgate"], 16)
            load_x(1, Static())
            load_c(1, Static())
            sp.dma_start(raw_wide["sh"][:, :, :], w_shared_in.rearrange("(k p) h -> p k h", p=P)).then_inc(load["sh"], 16)
            sp.dma_start(raw_wide["w1"][:, :, :], w1_shared.rearrange("(k p) h -> p k h", p=P)).then_inc(load["w1"], 16)
            sp.dma_start(raw_sq["so"][:, :, :], w_shared_out.rearrange("(k p) i -> p k i", p=P)).then_inc(load["so"], 16)
            sp.wait_ge(early_ready, 1)
            for e in range(E):
                sp.dma_start(raw_w2[e][:, :, :], w2[e].rearrange("(k p) c -> p k c", p=P)).then_inc(load["w2"], 16)

            def iteration(i, k):
                m = i + 3
                if k.has(m) and m >= 2 or k.has(m) and not isinstance(k, Static):
                    sp.wait_ge(xn1_ready, k.n(m - 2))
                    load_x(m, k)
                m = i + 2
                if k.has(m) and m >= 2 or k.has(m) and not isinstance(k, Static):
                    sp.wait_ge(tc_done, k.n(m - 2))
                    load_c(m, k)
                if k.has(i):
                    if k.has(i - 2):
                        sp.wait_ge(x1_ready, k.n(i - 2))
                    sp.dma_start(xr_sb[i % 2][:, :], x_tiles[k.tile(i)]).then_inc(xr_in[i % 2], 16)
                if k.has(i - 3):
                    sp.wait_ge(pair_used[E - 1], k.n(i - 3))
                    sp.dma_start(o_tiles[k.tile(i - 3)], acc[(i - 3) % 2][:, :, :].rearrange("p s d -> p (s d)")).then_inc(out_done[(i - 3) % 2], 16)

            run(sp, iteration)
            for n in range(2):
                sp.wait_ge(out_done[n], 16 * (TILES // 2))

        @block.tensor
        def _(pe):
            def transposed(dst, src):
                for kr in range(KC):
                    for kc in range(KC):
                        last = pe.transpose(dst[:, kc * D + kr * P:kc * D + (kr + 1) * P],
                                            src[:, kr, kc * P:(kc + 1) * P], ident[:, :])
                return last

            def composed(dst, right):
                for kc in range(KC):
                    for mk in range(KC):
                        last = pe.matmul(dst[:, kc * D:(kc + 1) * D], raw_sq["Wi"][:, mk, kc * P:(kc + 1) * P],
                                         right[:, mk, :], start=(kc == 0 and mk == 0), stop=(mk == KC - 1),
                                         skip_group_check=True)
                return last

            pe.wait_ge(consts, 1)
            pe.wait_ge(load["Wi"], 16)
            transposed(bank[0], raw_sq["Wi"]).then_inc(setup_pe, 1)
            pe.wait_ge(load["small"], SMALL)
            pe.wait_ge(zeros, 1)
            pe.transpose(bank[1][:, 0:4], rows[:, :], ident[0:4, 0:4])
            pe.transpose(bank[1][:, 4:6], dec_rows[:, :], ident[0:2, 0:2]).then_inc(setup_pe, 1)
            pe.wait_ge(load["Wg"], 16)
            transposed(bank[2], raw_sq["Wg"]).then_inc(setup_pe, 1)
            pe.wait_ge(load["Bm"], 16)
            transposed(bank[3], raw_sq["Bm"]).then_inc(setup_pe, 1)
            pe.wait_ge(setup_act, 2)
            composed(bank[4], WgT).then_inc(setup_pe, 1)
            pe.wait_ge(setup_act, 3)
            composed(bank[5], BmT).then_inc(setup_pe, 1)
            pe.wait_ge(setup_dve, 2)
            for oc in range(KC):
                for mk in range(KC):
                    pe.matmul(bank[1][:, 256 + oc:257 + oc], WgT[:, mk, oc * P:(oc + 1) * P], bi_wide[:, mk, 0:1],
                              start=(oc == 0 and mk == 0), stop=(mk == KC - 1), skip_group_check=True)
            for mk in range(KC):
                last = pe.matmul(bank[1][:, 0:D], bi_wide[:, mk, :], BmT[:, mk, :], start=False,
                                 stop=(mk == KC - 1), skip_group_check=True)
            last.then_inc(setup_pe, 1)
            pe.wait_ge(load["A"], 16)
            transposed(bank[2], raw_sq["A"]).then_inc(setup_pe, 1)
            pe.wait_ge(load["Wo"], 16)
            transposed(bank[3], raw_sq["Wo"]).then_inc(setup_pe, 1)

            def feature_product(dst, n, acts, start, col=0, done=None):
                w_hi, w_lo = split[n]
                a_hi, a_lo = acts
                first = start
                for oc in range(KC):
                    o = dst[:, oc * TOK:(oc + 1) * TOK]
                    at = slice(col + oc * P, col + (oc + 1) * P)
                    for kc in range(KC):
                        for w, a in ((w_hi, a_hi), (w_hi, a_lo), (w_lo, a_hi)):
                            last = pe.matmul(o, w[:, kc, at], a[:, kc, :], start=first,
                                             stop=(kc == KC - 1 and w is w_lo), skip_group_check=True)
                            first = False
                return last

            def token_product(dst, w, acts, s, start):
                a_hi, a_lo = acts
                first = start
                for kc in range(KC):
                    for a, part in ((a_hi, 0), (a_hi, 1), (a_lo, 0)):
                        last = pe.matmul(dst, a[:, kc, s * P:(s + 1) * P], w(part, kc), start=first,
                                         stop=(kc == KC - 1 and a is a_lo), skip_group_check=True)
                        first = False
                return last

            def recurrence(i, t, k):
                if not k.has(i):
                    return
                o = step_of(rec[i % 2], t)
                pe.wait_ge(uh_ready[t], k.n(i))
                for oc in range(KC):
                    for kc in range(KC):
                        for w in a16:
                            pe.matmul(o[:, oc, :], w[:, kc, oc * P:(oc + 1) * P], u_hi[t % 2][:, kc, :],
                                      start=False, stop=False, skip_group_check=True)
                pe.wait_ge(ul_ready[t], k.n(i))
                for oc in range(KC):
                    for kc in range(KC):
                        last = pe.matmul(o[:, oc, :], a16[0][:, kc, oc * P:(oc + 1) * P], u_lo[t % 2][:, kc, :],
                                         start=False, stop=(kc == KC - 1), skip_group_check=True)
                last.then_inc(sum_done[t], 1)

            def pair(n, m, k):
                q, s = n // 2, n % 2
                last = token_product(bank[B_PAIR[n]][:, :],
                                     lambda part, kc: split["w2"][part][:, kc, 2 * q:2 * q + 2, :].rearrange("p e c -> p (e c)"),
                                     hid_s[m % 2], s, True)
                last.then_inc(pair_done[n], 1)

            def iteration(i, k):
                a, c, d, e = i + 1, i - 1, i - 2, i - 3
                recurrence(i, 0, k)
                if k.has(a):
                    if a == 0:
                        pe.wait_ge(early_ready, 1)
                    if k.has(d):
                        pe.wait_ge(sil_s_ready, k.n(d))
                    pe.wait_ge(c_in[a % 2], k.dma(a))
                    for s in range(HALVES):
                        for kc in range(KC):
                            last = pe.transpose(bank[B_TC][:, kc * TOK + s * P:kc * TOK + (s + 1) * P],
                                                c_sb[a % 2][:, s * D + kc * P:s * D + (kc + 1) * P], ident[:, :])
                    last.then_inc(tc_done, 1)
                    if k.has(d):
                        pe.wait_ge(hs_ready, k.n(d))
                    pe.wait_ge(xn1_ready, k.n(a))
                    for s in range(HALVES):
                        for kc in range(KC):
                            last = pe.transpose(bank[B_TX][:, kc * TOK + s * P:kc * TOK + (s + 1) * P],
                                                xn1[a % 2][:, s, kc * P:(kc + 1) * P], ident[:, :])
                    last.then_inc(tx_done, 1)
                if k.has(d):
                    if k.has(e):
                        pe.wait_ge(pair_used[2], k.n(e))
                    pe.wait_ge(lg_f_ready, k.n(d))
                    for s in range(HALVES):
                        last = pe.transpose(bank[B_LGT][:, s * P:(s + 1) * P], lg_f[:, s * P:(s + 1) * P], ident[:, :])
                    last.then_inc(lgt_done, 1)
                if k.has(e):
                    if not k.has(d) and k.has(e - 1):
                        pe.wait_ge(pair_used[5], k.n(e - 1))
                    pair(5, e, k)
                recurrence(i, 1, k)
                if k.has(c):
                    if k.has(d):
                        pe.wait_ge(sil_w_ready, k.n(d))
                    pe.wait_ge(st_hi, k.n(c))
                    pe.wait_ge(st_lo, k.n(c))
                    for s in range(HALVES):
                        last = token_product(bank[B_WO][:, s * D:(s + 1) * D],
                                             lambda part, kc: split["wo"][part][:, kc, :], st_s[c % 2], s, s == 0)
                    last.then_inc(wo_done, 1)
                if k.has(e):
                    if k.has(d):
                        pe.wait_ge(hid_ready, k.n(d))
                    else:
                        pe.wait_ge(pair_used[4], k.n(e))
                    pair(6, e, k)
                recurrence(i, 2, k)
                if k.has(d):
                    if d == 0:
                        pe.wait_ge(w2_ready, 1)
                    if k.has(a):
                        pe.wait_ge(c2_ready, k.n(a))
                    pe.wait_ge(hs_hi, k.n(d))
                    pe.wait_ge(hs_lo, k.n(d))
                    for s in range(HALVES):
                        last = token_product(bank[B_SO][:, s * D:(s + 1) * D],
                                             lambda part, kc: split["so"][part][:, kc, :], hs_s, s, s == 0)
                    last.then_inc(so_done, 1)
                if k.has(e):
                    if k.has(a):
                        pe.wait_ge(ret_ready, k.n(a))
                    if not k.has(d):
                        pe.wait_ge(pair_used[1], k.n(e))
                    pair(7, e, k)
                recurrence(i, 3, k)
                if k.has(a):
                    if k.has(d):
                        pe.wait_ge(lg_ready, k.n(d))
                    pe.wait_ge(ret_hi, k.n(a))
                    pe.wait_ge(ret_lo, k.n(a))
                    feature_product(bank[B_INP], "inp", ret_s[a % 2], True).then_inc(inp_done, 1)
                    if k.has(e):
                        pe.wait_ge(pair_used[5], k.n(e))
                    feature_product(bank[B_GATE], "gate", ret_s[a % 2], True).then_inc(gate_done, 1)
                if k.has(d):
                    if k.has(c):
                        pe.wait_ge(x1_ready, k.n(c))
                    pe.wait_ge(hid_hi, k.n(d))
                    pe.wait_ge(hid_lo, k.n(d))
                    pair(0, d, k)
                recurrence(i, 4, k)
                if k.has(a):
                    if k.has(c):
                        pe.wait_ge(st_ready[STEPS - 1], k.n(c))
                    rec_flat = rec[a % 2][:, :, :].rearrange("p c n -> p (c n)")
                    feature_product(rec_flat, "bm", ret_s[a % 2], True)
                    for oc in range(KC):
                        last = pe.matmul(rec_flat[:, oc * TOK:(oc + 1) * TOK], cp[:, oc * P:(oc + 1) * P], ones[:, :],
                                         start=False, stop=False, skip_group_check=True)
                    last.then_inc(bm_done, 1)
                if k.has(d):
                    if k.has(e):
                        pe.wait_ge(pair_used[7], k.n(e))
                    pair(1, d, k)
                if k.has(c):
                    if k.has(d):
                        pe.wait_ge(acc_ready, k.n(d))
                    pe.wait_ge(xn2_ready, k.n(c))
                    for s in range(HALVES):
                        for kc in range(KC):
                            last = pe.transpose(bank[B_T2][:, kc * TOK + s * P:kc * TOK + (s + 1) * P],
                                                xn2[c % 2][:, s, kc * P:(kc + 1) * P], ident[:, :])
                    last.then_inc(t2_done, 1)
                recurrence(i, 5, k)
                if k.has(d):
                    if k.has(a):
                        pe.wait_ge(inp_ready, k.n(a))
                    else:
                        pe.wait_ge(lg_ready, k.n(d))
                    pair(2, d, k)
                    pe.wait_ge(pair_used[0], k.n(d))
                    pair(3, d, k)
                    if k.has(e):
                        pe.wait_ge(pair_used[6], k.n(e))
                    pair(4, d, k)
                recurrence(i, 6, k)
                if k.has(c):
                    pe.wait_ge(xn2_hi, k.n(c))
                    pe.wait_ge(xn2_lo, k.n(c))
                    if c == 0:
                        pe.wait_ge(wide_ready, 1)
                    feature_product(bank[B_SHA], "sh", xn2_s[c % 2], True)
                    if k.has(d):
                        pe.wait_ge(pair_used[1], k.n(d))
                    feature_product(bank[B_SHB], "sh", xn2_s[c % 2], True, col=D).then_inc(sh_done, 1)
                    if k.has(a):
                        pe.wait_ge(gt_ready, k.n(a))
                    elif k.has(e):
                        pe.wait_ge(pair_used[5], k.n(e))
                    w_hi, w_lo = split["wgate"]
                    v_hi, v_lo = xn2_s[c % 2]
                    first = True
                    for kc in range(KC):
                        for w, v in ((w_hi, v_hi), (w_hi, v_lo), (w_lo, v_hi)):
                            last = pe.matmul(bank[B_LG][:, 0:TOK], w[:, kc, :], v[:, kc, :], start=first,
                                             stop=(kc == KC - 1 and w is w_lo), skip_group_check=True)
                            first = False
                    last.then_inc(lg_done, 1)
                recurrence(i, 7, k)
                if k.has(a):
                    pe.wait_ge(cn_hi, k.n(a))
                    pe.wait_ge(cn_lo, k.n(a))
                    rec_flat = rec[a % 2][:, :, :].rearrange("p c n -> p (c n)")
                    feature_product(rec_flat, "a", cn_s[a % 2], False).then_inc(ac_done, 1)
                if k.has(c):
                    if k.has(d):
                        pe.wait_ge(pair_used[3], k.n(d))
                    feature_product(bank[B_W1A], "w1", xn2_s[c % 2], True)
                    if k.has(d):
                        pe.wait_ge(pair_used[4], k.n(d))
                    feature_product(bank[B_W1B], "w1", xn2_s[c % 2], True, col=D).then_inc(w1_done, 1)

            run(pe, iteration)

        @block.scalar
        def _(act):
            act.wait_ge(load["small"], SMALL)
            act.activation(tgf[:, :], gx[:, :], ACT.Silu).then_inc(setup_act, 1)
            act.wait_ge(setup_pe, 3)
            act.copy(flat(WgT[:, :, :]), bank[2][:, :]).then_inc(setup_act, 1)
            act.wait_ge(setup_pe, 4)
            act.copy(flat(BmT[:, :, :]), bank[3][:, :]).then_inc(setup_act, 1)
            act.activation(tgx[:, :], gx[:, :], ACT.Tanh)
            act.wait_ge(setup_act, 1)
            act.activation(tgf[:, :], gf[:, :], ACT.Tanh).then_inc(setup_act, 1)
            act.wait_ge(setup_pe, 1)
            act.copy(flat(split["inp"][0][:, :, :]), bank[0][:, :]).then_inc(setup_act, 1)
            act.wait_ge(setup_pe, 5)
            act.copy(flat(split["gate"][0][:, :, :]), bank[4][:, :]).then_inc(setup_act, 1)
            act.wait_ge(setup_dve, 5)
            act.copy(flat(split["bm"][0][:, :, :]), tmp_w[:, :]).then_inc(setup_act, 1)
            act.wait_ge(setup_dve, 7)
            act.copy(cp_hi[:, :], cp_row[:, :]).then_inc(setup_act, 1)
            act.wait_ge(setup_dve, 9)
            act.copy(flat(split["a"][0][:, :, :]), tmp_a[:, :]).then_inc(setup_act, 1)
            act.mul(flat(a16[0][:, :, :]), tmp_a[:, :], -1.0).then_inc(setup_act, 1)
            act.wait_ge(setup_dve, 12)
            act.copy(flat(split["wo"][0][:, :, :]), tmp_s[:, :]).then_inc(setup_act, 1)

            def between(i):
                if i == -1:
                    act.wait_ge(load["sh"], 16)
                    act.copy(flat(split["sh"][0][:, :, :]), flat(raw_wide["sh"][:, :, :])).then_inc(wide_hi, 1)
                    act.wait_ge(load["w1"], 16)
                    act.copy(flat(split["w1"][0][:, :, :]), flat(raw_wide["w1"][:, :, :])).then_inc(wide_hi, 1)
                    act.wait_ge(load["wgate"], 16)
                    act.wait_ge(zeros, 2)
                    act.copy(split["wgate"][0][:, :, 0:E], raw_wgate[:, :, :]).then_inc(wide_hi, 1)
                if i == 0:
                    act.wait_ge(load["so"], 16)
                    act.mul(flat(raw_sq["so"][:, :, :]), flat(raw_sq["so"][:, :, :]), tgf[:, 0:1]).then_inc(w2_hi_done, 1)
                    act.wait_ge(w2_hi_done, 1)
                    act.copy(flat(split["so"][0][:, :, :]), flat(raw_sq["so"][:, :, :])).then_inc(w2_hi_done, 1)
                    act.wait_ge(load["w2"], 16 * E)
                    for e in range(E):
                        act.copy(split["w2"][0][:, :, e, :], raw_w2[e][:, :, :]).then_inc(w2_hi_done, 1)

            def tanh_step(i, t, k):
                if k.has(i):
                    if t == 0 and k.has(i - 2):
                        act.wait_ge(st_lo, k.n(i - 2))
                    act.wait_ge(sum_done[t], k.n(i))
                    act.activation(step_of(state[i % 2], t), step_of(rec[i % 2], t), ACT.Tanh,
                                   scale=1.0 / PSCALE).then_inc(st_ready[t], 1)

            def iteration(i, k):
                a, c, d, f = i + 1, i - 1, i - 2, i + 2
                if k.has(c):
                    if k.has(c - 1):
                        act.wait_ge(wo_done, k.n(c - 1))
                    act.wait_ge(st_ready[STEPS - 1], k.n(c))
                    act.copy(flat(st_s[c % 2][0][:, :, :]), flat(state[c % 2][:, :, :])).then_inc(st_hi, 1)
                tanh_step(i, 0, k)
                if k.has(d):
                    act.wait_ge(w1_done, k.n(d))
                    if k.has(i - 3):
                        act.wait_ge(hid_ready, k.n(i - 3))
                    act.activation(flat(sil_w[:, :, :]), bank[B_W1A][:, :], ACT.Silu).then_inc(sil_w_ready, 1)
                    if k.has(i - 3):
                        act.wait_ge(so_done, k.n(i - 3))
                    act.wait_ge(hs_ready, k.n(d))
                    act.copy(flat(hs_s[0][:, :, :]), flat(hs[:, :, :])).then_inc(hs_hi, 1)
                tanh_step(i, 1, k)
                if k.has(a):
                    act.wait_ge(tc_done, k.n(a))
                    if k.has(a - 1):
                        act.wait_ge(r_ready, k.n(a - 1))
                        act.copy(c2[a % 2][:, :, :, 0], r[(a - 1) % 2][:, :, :, STEPS])
                    for kc in range(KC):
                        last = act.activation(by_time(c2[a % 2][:, kc, :, 1:STEPS + 1]),
                                              halves(bank[B_TC][:, kc * TOK:(kc + 1) * TOK]), ACT.Square)
                    last.then_inc(c2_ready, 1)
                if k.has(d):
                    act.wait_ge(hid_ready, k.n(d))
                    if k.has(d - 2):
                        act.wait_ge(pair_done[E - 1], k.n(d - 2))
                    act.copy(flat(hid_s[d % 2][0][:, :, :]), flat(hid[:, :, :])).then_inc(hid_hi, 1)
                tanh_step(i, 2, k)
                if k.has(a):
                    act.wait_ge(ret_ready, k.n(a))
                    if k.has(a - 1):
                        act.wait_ge(bm_done, k.n(a - 1))
                    act.copy(flat(ret_s[a % 2][0][:, :, :]), flat(ret[a % 2][:, :, :])).then_inc(ret_hi, 1)
                if k.has(d):
                    act.wait_ge(ld_ready, k.n(d))
                    if k.has(d - 1):
                        act.wait_ge(numden, k.n(d - 1))
                    act.activation(flat(lt[:, :, :]), flat(ld[:, :, :]), ACT.Tanh, scale=0.5).then_inc(lt_ready, 1)
                tanh_step(i, 3, k)
                if k.has(c):
                    act.wait_ge(ln2_shift, k.n(c))
                    if k.has(c - 1):
                        act.wait_ge(t2_done, k.n(c - 1))
                    for s in range(HALVES):
                        last = act.activation(xn2[c % 2][:, s, :], x1[c % 2][:, s, :], ACT.Identity,
                                              bias=nr2[c % 2][:, s:s + 1], scale=rs2[c % 2][:, s:s + 1])
                    last.then_inc(xn2_ready, 1)
                tanh_step(i, 4, k)
                if k.has(a):
                    act.wait_ge(inp_done, k.n(a))
                    if k.has(a - 1):
                        act.wait_ge(cn_ready, k.n(a - 1))
                    for kc in range(KC):
                        last = act.activation(inp[a % 2][:, kc, :], bank[B_INP][:, kc * TOK:(kc + 1) * TOK],
                                              ACT.Identity, bias=cols[:, kc:kc + 1])
                    last.then_inc(inp_ready, 1)
                    act.wait_ge(gate_done, k.n(a))
                    if k.has(a - 2):
                        act.wait_ge(uh_ready[STEPS - 1], k.n(a - 2))
                    for kc in range(KC):
                        last = act.activation(gt[a % 2][:, kc, :], bank[B_GATE][:, kc * TOK:(kc + 1) * TOK],
                                              ACT.Tanh, bias=half_gate_bias[:, kc:kc + 1], scale=0.5)
                    last.then_inc(gt_ready, 1)
                tanh_step(i, 5, k)
                if k.has(a):
                    act.wait_ge(cn_ready, k.n(a))
                    if k.has(a - 1):
                        act.wait_ge(ac_done, k.n(a - 1))
                    act.copy(flat(cn_s[a % 2][0][:, :, :]), flat(cn[a % 2][:, :, :])).then_inc(cn_hi, 1)
                if k.has(c):
                    act.wait_ge(t2_done, k.n(c))
                    if k.has(c - 1):
                        act.wait_ge(w1_done, k.n(c - 1))
                    act.copy(flat(xn2_s[c % 2][0][:, :, :]), bank[B_T2][:, :]).then_inc(xn2_hi, 1)
                tanh_step(i, 6, k)
                if k.has(f):
                    act.wait_ge(ln1_shift, k.n(f))
                    if k.has(f - 1):
                        act.wait_ge(tx_done, k.n(f - 1))
                    for s in range(HALVES):
                        last = act.activation(xn1[f % 2][:, s, :], x_sb[f % 2][:, s * D:(s + 1) * D], ACT.Identity,
                                              bias=nr1[f % 2][:, s:s + 1], scale=rs1[f % 2][:, s:s + 1])
                    last.then_inc(xn1_ready, 1)
                tanh_step(i, 7, k)
                if k.has(c):
                    act.wait_ge(sh_done, k.n(c))
                    if k.has(c - 1):
                        act.wait_ge(hs_ready, k.n(c - 1))
                    act.activation(flat(sil_s[:, :, :]), bank[B_SHA][:, :], ACT.Silu).then_inc(sil_s_ready, 1)
                    act.wait_ge(lg_done, k.n(c))
                    if k.has(c - 1):
                        act.wait_ge(lgt_done, k.n(c - 1))
                    act.copy(lg_f[:, :], bank[B_LG][:, 0:TOK]).then_inc(lg_f_ready, 1)

            run(act, iteration, between)

        @block.vector
        def _(dve):
            def low(n, whole, hi, signal):
                dve.tensor_tensor(n, whole, hi.bitcast(F32), ALU.subtract).then_inc(signal, 1)

            dve.wait_ge(load["small"], SMALL)
            dve.tensor_copy(dec_rows[:, :].rearrange("k (h f) -> k h f", f=D // HEADS),
                            dec8[:, :].unsqueeze(2).to_broadcast([2, HEADS // KC, D // HEADS])).then_inc(zeros, 1)
            for part in split["wgate"]:
                dve.memset(part[:, :, :].bitcast(F32), 0.0)
            dve.memset(cp[:, :].bitcast(F32), 0.0)
            dve.memset(c2[0][:, :, :, 0], 0.0)
            dve.memset(ones[:, :].bitcast(F32), 1.0)
            dve.memset(dmask[:, :, :, :], 1.0)
            dve.memset(u_lo[0][:, :, :], 0.0).then_inc(ul_ready[0], 1)
            dve.memset(u_hi[0][:, :, :], 0.0).then_inc(uh_ready[0], 1)
            dve.memset(tri[:, :, :], 0.0).then_inc(zeros, 1)
            dve.wait_ge(zeros, 2)
            dve.memset(dmask[:, :, :, 0], 0.0)
            for e in range(1, E):
                last = dve.memset(tri[:, e, 0:e], 1.0)
            last.then_inc(zeros, 1)
            dve.wait_ge(setup_pe, 2)
            dve.tensor_copy(cols[:, :], bank[1][:, 0:4])
            dve.tensor_copy(dec_cols[:, :], bank[1][:, 4:6]).then_inc(setup_dve, 1)
            dve.wait_ge(setup_dve, 1)
            dve.tensor_copy(bi_wide[:, :, :], cols[:, 0:KC].unsqueeze(2).to_broadcast([P, KC, P])).then_inc(setup_dve, 1)
            for kc in range(KC):
                dve.tensor_scalar(dmask[:, kc, :, :], dmask[:, kc, :, :], dec_cols[:, kc:kc + 1], None, ALU.mult).then_inc(setup_dve, 1)
            dve.wait_ge(setup_pe, 6)
            dve.tensor_scalar(tmp_w[:, :], bank[5][:, :], PSCALE, None, ALU.mult).then_inc(setup_dve, 1)
            dve.wait_ge(setup_pe, 7)
            dve.scalar_tensor_tensor(out=half_gate_bias[:, :], in0=bank[1][:, 256:258], scalar=1.0, in1=cols[:, 2:4],
                                     op0=ALU.mult, op1=ALU.add).then_inc(setup_dve, 1)
            dve.tensor_scalar(cp_row[:, :], bank[1][:, 0:D], PSCALE, None, ALU.mult).then_inc(setup_dve, 1)
            dve.wait_ge(setup_dve, 6)
            dve.tensor_scalar(half_gate_bias[:, :], half_gate_bias[:, :], 0.5, None, ALU.mult).then_inc(setup_dve, 1)
            dve.wait_ge(setup_pe, 8)
            dve.tensor_scalar(tmp_a[:, :], bank[2][:, :], -0.5 * PSCALE, None, ALU.mult).then_inc(setup_dve, 1)
            dve.wait_ge(setup_act, 5)
            low(flat(split["inp"][1][:, :, :]), bank[0][:, :], flat(split["inp"][0][:, :, :]), setup_dve)
            dve.wait_ge(setup_act, 6)
            low(flat(split["gate"][1][:, :, :]), bank[4][:, :], flat(split["gate"][0][:, :, :]), setup_dve)
            dve.wait_ge(setup_pe, 9)
            dve.tensor_scalar(tmp_s[:, :], bank[3][:, :], tgx[:, 0:1], None, ALU.mult).then_inc(setup_dve, 1)
            dve.wait_ge(setup_act, 7)
            low(flat(split["bm"][1][:, :, :]), tmp_w[:, :], flat(split["bm"][0][:, :, :]), setup_dve)
            dve.wait_ge(setup_act, 8)
            dve.tensor_copy(cp[0:1, :], cp_hi[0:1, :].bitcast(F32))
            dve.tensor_tensor(cp[32:33, :], cp_row[32:33, :], cp_hi[32:33, :].bitcast(F32), ALU.subtract).then_inc(setup_dve, 1)
            dve.wait_ge(setup_act, 9)
            low(flat(split["a"][1][:, :, :]), tmp_a[:, :], flat(split["a"][0][:, :, :]), setup_dve)
            dve.wait_ge(setup_act, 10)
            dve.scalar_tensor_tensor(out=flat(a16[1][:, :, :]), in0=tmp_a[:, :], scalar=-1.0, in1=flat(a16[0][:, :, :]),
                                     op0=ALU.mult, op1=ALU.subtract).then_inc(setup_dve, 1)
            dve.tensor_scalar(tgbo[:, :], bo_all[:, :], tgx[:, 0:1], None, ALU.mult).then_inc(setup_dve, 1)
            dve.wait_ge(setup_act, 11)
            low(flat(split["wo"][1][:, :, :]), tmp_s[:, :], flat(split["wo"][0][:, :, :]), early_ready)

            def between(i):
                if i == -1:
                    dve.wait_ge(wide_hi, 3)
                    for n in ("sh", "w1"):
                        dve.tensor_tensor(flat(split[n][1][:, :, :]), flat(raw_wide[n][:, :, :]),
                                          flat(split[n][0][:, :, :]).bitcast(F32), ALU.subtract)
                    dve.tensor_tensor(split["wgate"][1][:, :, 0:E], raw_wgate[:, :, :],
                                      split["wgate"][0][:, :, 0:E].bitcast(F32), ALU.subtract).then_inc(wide_ready, 1)
                if i == 0:
                    dve.wait_ge(w2_hi_done, 2)
                    dve.tensor_tensor(flat(split["so"][1][:, :, :]), flat(raw_sq["so"][:, :, :]),
                                      flat(split["so"][0][:, :, :]).bitcast(F32), ALU.subtract)
                    for e in range(E):
                        dve.wait_ge(w2_hi_done, 3 + e)
                        last = dve.tensor_tensor(split["w2"][1][:, :, e, :], raw_w2[e][:, :, :],
                                                 split["w2"][0][:, :, e, :].bitcast(F32), ALU.subtract)
                    last.then_inc(w2_ready, 1)

            def gated_state(i, t, k):
                if not k.has(i):
                    return
                m, t_next = (i, t + 1) if t + 1 < STEPS else (i + 1, 0)
                if not k.has(m):
                    return
                p = t_next % 2
                old, gate = step_of(state[i % 2], t), step_of(gt[m % 2], t_next)
                if t_next == 0:
                    dve.wait_ge(gt_ready, k.n(m))
                dve.wait_ge(st_ready[t], k.n(i))
                dve.scalar_tensor_tensor(out=u_full[p][:, :, :], in0=gate, scalar=1.0, in1=old,
                                         op0=ALU.add, op1=ALU.mult)
                dve.scalar_tensor_tensor(out=u_hi[p][:, :, :], in0=gate, scalar=1.0, in1=old,
                                         op0=ALU.add, op1=ALU.mult).then_inc(uh_ready[t_next], 1)
                dve.wait_ge(uh_ready[t_next], k.n(m))
                dve.tensor_tensor(u_lo[p][:, :, :], u_full[p][:, :, :], u_hi[p][:, :, :],
                                  ALU.subtract).then_inc(ul_ready[t_next], 1)

            def add_pair(n, m, k):
                if not k.has(m):
                    return
                q, s = n // 2, n % 2
                o = acc[m % 2][:, s, :]
                dve.wait_ge(pair_done[n], k.n(m))
                dve.wait_ge(acc_ready, k.n(m))
                if n >= 2:
                    dve.wait_ge(pair_used[n - 2], k.n(m))
                dve.scalar_tensor_tensor(out=o, in0=bank[B_PAIR[n]][:, 0:D], scalar=wts[m % 2][:, s, 2 * q:2 * q + 1],
                                         in1=o, op0=ALU.mult, op1=ALU.add).then_inc(pair_half[n], 1)
                dve.wait_ge(pair_half[n], k.n(m))
                dve.scalar_tensor_tensor(out=o, in0=bank[B_PAIR[n]][:, D:2 * D], scalar=wts[m % 2][:, s, 2 * q + 1:2 * q + 2],
                                         in1=o, op0=ALU.mult, op1=ALU.add).then_inc(pair_used[n], 1)

            def iteration(i, k):
                a, c, d, e, f = i + 1, i - 1, i - 2, i - 3, i + 2
                gated_state(i, 0, k)
                if k.has(d):
                    dve.wait_ge(sil_w_ready, k.n(d))
                    if k.has(d - 1):
                        dve.wait_ge(hid_hi, k.n(d - 1))
                        dve.wait_ge(hid_lo, k.n(d - 1))
                    dve.tensor_tensor(flat(hid[:, :, :]), bank[B_W1B][:, :], flat(sil_w[:, :, :]),
                                      ALU.mult).then_inc(hid_ready, 1)
                gated_state(i, 1, k)
                if k.has(a):
                    dve.wait_ge(c2_ready, k.n(a))
                    if a == 0:
                        dve.wait_ge(setup_dve, 4)
                    dve.tensor_tensor_scan(r[a % 2][:, :, :, :].rearrange("p c b t -> p (c b t)"),
                                           dmask[:, :, :, :].rearrange("p c b t -> p (c b t)"),
                                           c2[a % 2][:, :, :, :].rearrange("p c b t -> p (c b t)"),
                                           0.0, ALU.mult, ALU.add).then_inc(r_ready, 1)
                if k.has(d):
                    dve.wait_ge(lgt_done, k.n(d))
                    dve.tensor_tensor(lg[:, :, :],
                                      bank[B_LGT][:, 0:TOK].rearrange("p (s n) -> p s n", s=HALVES)[:, :, 0:E],
                                      gb_all[:, :].unsqueeze(1).to_broadcast([P, HALVES, E]), ALU.add).then_inc(lg_ready, 1)
                if k.has(a):
                    dve.wait_ge(r_ready, k.n(a))
                    dve.wait_ge(tx_done, k.n(a))
                    if k.has(a - 1):
                        dve.wait_ge(ret_hi, k.n(a - 1))
                    for kc in range(KC):
                        last = dve.tensor_tensor(halves(ret[a % 2][:, kc, :]), halves(bank[B_TX][:, kc * TOK:(kc + 1) * TOK]),
                                                 by_time(r[a % 2][:, kc, :, 1:STEPS + 1]), ALU.mult)
                    last.then_inc(ret_ready, 1)
                if k.has(d):
                    dve.wait_ge(lg_ready, k.n(d))
                    dve.tensor_reduce(lmax[:, :], lg[:, :, :], AX_X, ALU.max).then_inc(lmax_ready, 1)
                if k.has(d):
                    if k.has(d - 1):
                        dve.wait_ge(beat_ready, k.n(d - 1))
                    mine = lg[:, :, :].unsqueeze(3).to_broadcast([P, HALVES, E, E])
                    others = lg[:, :, :].unsqueeze(2).to_broadcast([P, HALVES, E, E])
                    dve.tensor_tensor(more[:, :, :, :], others, mine, ALU.is_gt)
                    dve.tensor_tensor(same[:, :, :, :], others, mine, ALU.is_equal).then_inc(same_ready, 1)
                add_pair(5, e, k)
                if k.has(d):
                    dve.wait_ge(lmax_ready, k.n(d))
                    dve.tensor_tensor(ld[:, :, :], lg[:, :, :], lmax[:, :].unsqueeze(2).to_broadcast([P, HALVES, E]),
                                      ALU.subtract).then_inc(ld_ready, 1)
                gated_state(i, 2, k)
                if k.has(c):
                    dve.wait_ge(wo_done, k.n(c))
                    dve.wait_ge(xr_ready, k.n(c))
                    dve.tensor_tensor(x1[c % 2][:, :, :].rearrange("p s d -> p (s d)"), bank[B_WO][:, :],
                                      xr_sb[c % 2][:, :], ALU.add).then_inc(x1_ready, 1)
                if k.has(a):
                    dve.wait_ge(ret_hi, k.n(a))
                    dve.wait_ge(ret_ready, k.n(a))
                    if k.has(a - 1):
                        dve.wait_ge(bm_done, k.n(a - 1))
                    low(flat(ret_s[a % 2][1][:, :, :]), flat(ret[a % 2][:, :, :]), flat(ret_s[a % 2][0][:, :, :]), ret_lo)
                if k.has(c):
                    dve.wait_ge(x1_ready, k.n(c))
                    for s in range(HALVES):
                        last = dve.bn_stats(st2[c % 2][:, s, :], x1[c % 2][:, s, :])
                    last.then_inc(ln2_stats, 1)
                    dve.wait_ge(ln2_stats, k.n(c))
                if k.has(d):
                    dve.wait_ge(lt_ready, k.n(d))
                    dve.tensor_scalar(num[:, :, :], lt[:, :, :], 1.0, None, ALU.add)
                    dve.tensor_scalar(den[:, :, :], lt[:, :, :], -1.0, 1.0, ALU.mult, ALU.add).then_inc(numden, 1)
                if k.has(c):
                    for s in range(HALVES):
                        last = dve.bn_aggr(mv2[c % 2][:, s, :], st2[c % 2][:, s, :])
                    last.then_inc(ln2_aggr, 1)
                if k.has(d):
                    dve.wait_ge(numden, k.n(d))
                    dve.reciprocal(rden[:, :, :], den[:, :, :]).then_inc(rden_ready, 1)
                if k.has(c):
                    dve.wait_ge(ln2_aggr, k.n(c))
                    dve.tensor_scalar(ve2[c % 2][:, :], mv2[c % 2][:, :, 1], EPS, None, ALU.add)
                    dve.tensor_scalar(nm2[c % 2][:, :], mv2[c % 2][:, :, 0], -1.0, None, ALU.mult).then_inc(ln2_var, 1)
                add_pair(6, e, k)
                gated_state(i, 3, k)
                if k.has(d):
                    if k.has(d - 2):
                        dve.wait_ge(out_done[d % 2], k.dma(d - 2))
                    dve.wait_ge(so_done, k.n(d))
                    dve.tensor_tensor(acc[d % 2][:, :, :].rearrange("p s d -> p (s d)"), bank[B_SO][:, :],
                                      x1[d % 2][:, :, :].rearrange("p s d -> p (s d)"), ALU.add).then_inc(acc_ready, 1)
                    dve.wait_ge(rden_ready, k.n(d))
                    dve.tensor_tensor(ex[:, :, :], num[:, :, :], rden[:, :, :], ALU.mult).then_inc(ex_ready, 1)
                add_pair(7, e, k)
                if k.has(d):
                    dve.wait_ge(ex_ready, k.n(d))
                    dve.tensor_reduce(esum[:, :], ex[:, :, :], AX_X, ALU.add).then_inc(esum_ready, 1)
                    dve.wait_ge(rank_ready, k.n(d))
                    dve.scalar_tensor_tensor(out=flat(picked[:, :, :]), in0=flat(rank[:, :, :]), scalar=2.0,
                                             in1=flat(ex[:, :, :]), op0=ALU.is_lt, op1=ALU.mult).then_inc(picked_ready, 1)
                    dve.wait_ge(esum_ready, k.n(d))
                    dve.reciprocal(rsum[:, :], esum[:, :]).then_inc(rsum_ready, 1)
                    dve.wait_ge(rsum_ready, k.n(d))
                    dve.tensor_scalar(rsg[:, :], rsum[:, :], tgf[:, 0:1], None, ALU.mult).then_inc(rsg_ready, 1)
                gated_state(i, 4, k)
                if k.has(d):
                    dve.wait_ge(rsg_ready, k.n(d))
                    dve.wait_ge(picked_ready, k.n(d))
                    dve.tensor_tensor(wts[d % 2][:, :, :], picked[:, :, :],
                                      rsg[:, :].unsqueeze(2).to_broadcast([P, HALVES, E]), ALU.mult).then_inc(wts_ready, 1)
                if k.has(f):
                    dve.wait_ge(x_in[f % 2], k.dma(f))
                    for s in range(HALVES):
                        last = dve.bn_stats(st1[f % 2][:, s, :], x_sb[f % 2][:, s * D:(s + 1) * D])
                    last.then_inc(ln1_stats, 1)
                if k.has(d):
                    dve.wait_ge(wts_ready, k.n(d))
                add_pair(0, d, k)
                gated_state(i, 5, k)
                if k.has(f):
                    dve.wait_ge(ln1_stats, k.n(f))
                if k.has(a):
                    dve.wait_ge(inp_ready, k.n(a))
                    dve.wait_ge(gt_ready, k.n(a))
                    if k.has(a - 1):
                        dve.wait_ge(cn_hi, k.n(a - 1))
                        dve.wait_ge(cn_lo, k.n(a - 1))
                    dve.scalar_tensor_tensor(out=flat(cn[a % 2][:, :, :]), in0=flat(gt[a % 2][:, :, :]), scalar=-1.0,
                                             in1=flat(inp[a % 2][:, :, :]), op0=ALU.add, op1=ALU.mult).then_inc(cn_ready, 1)
                if k.has(f):
                    for s in range(HALVES):
                        last = dve.bn_aggr(mv1[f % 2][:, s, :], st1[f % 2][:, s, :])
                    last.then_inc(ln1_aggr, 1)
                if k.has(c):
                    dve.wait_ge(xn2_hi, k.n(c))
                    if k.has(c - 1):
                        dve.wait_ge(w1_done, k.n(c - 1))
                    low(flat(xn2_s[c % 2][1][:, :, :]), bank[B_T2][:, :], flat(xn2_s[c % 2][0][:, :, :]), xn2_lo)
                if k.has(f):
                    dve.wait_ge(ln1_aggr, k.n(f))
                    dve.tensor_scalar(ve1[f % 2][:, :], mv1[f % 2][:, :, 1], EPS, None, ALU.add)
                    dve.tensor_scalar(nm1[f % 2][:, :], mv1[f % 2][:, :, 0], -1.0, None, ALU.mult).then_inc(ln1_var, 1)
                add_pair(1, d, k)
                gated_state(i, 6, k)
                add_pair(2, d, k)
                add_pair(3, d, k)
                gated_state(i, 7, k)
                add_pair(4, d, k)
                if k.has(c):
                    dve.wait_ge(sil_s_ready, k.n(c))
                    if k.has(c - 1):
                        dve.wait_ge(hs_hi, k.n(c - 1))
                        dve.wait_ge(hs_lo, k.n(c - 1))
                    dve.tensor_tensor(flat(hs[:, :, :]), bank[B_SHB][:, :], flat(sil_s[:, :, :]),
                                      ALU.mult).then_inc(hs_ready, 1)

            run(dve, iteration, between)

        @block.gpsimd
        def _(pool):
            pool.memset(minus_half[:, :], -0.5)
            pool.memset(ident[:, :], 0.0).then_inc(zeros_pool := sem("zeros_pool"), 1)
            pool.wait_ge(zeros_pool, 1)
            pool.affine_select(out=ident[:, :], in_=ident[:, :], compare_op=ALU.not_equal, fill=1.0, base=0,
                               pattern=[[-1, P]], channel_multiplier=1).then_inc(consts, 1)

            def low(n, whole, hi, signal):
                pool.tensor_tensor(n, whole, hi.bitcast(F32), ALU.subtract).then_inc(signal, 1)

            def iteration(i, k):
                a, c, d, f = i + 1, i - 1, i - 2, i + 2
                if k.has(c):
                    pool.wait_ge(st_hi, k.n(c))
                    if k.has(c - 1):
                        pool.wait_ge(wo_done, k.n(c - 1))
                    low(flat(st_s[c % 2][1][:, :, :]), flat(state[c % 2][:, :, :]), flat(st_s[c % 2][0][:, :, :]), st_lo)
                if k.has(d):
                    pool.wait_ge(hs_hi, k.n(d))
                    if k.has(d - 1):
                        pool.wait_ge(so_done, k.n(d - 1))
                    low(flat(hs_s[1][:, :, :]), flat(hs[:, :, :]), flat(hs_s[0][:, :, :]), hs_lo)
                    pool.wait_ge(hid_hi, k.n(d))
                    if k.has(d - 2):
                        pool.wait_ge(pair_done[E - 1], k.n(d - 2))
                    low(flat(hid_s[d % 2][1][:, :, :]), flat(hid[:, :, :]), flat(hid_s[d % 2][0][:, :, :]), hid_lo)
                if k.has(d):
                    if d == 0:
                        pool.wait_ge(zeros, 3)
                    pool.wait_ge(same_ready, k.n(d))
                    pool.tensor_tensor(same_l[:, :, :, :].rearrange("p s e f -> p s (e f)"),
                                       same[:, :, :, :].rearrange("p s e f -> p s (e f)"),
                                       tri[:, :, :].rearrange("p e f -> p (e f)").unsqueeze(1).to_broadcast([P, HALVES, E * E]),
                                       ALU.mult).then_inc(samel_ready, 1)
                    pool.wait_ge(samel_ready, k.n(d))
                    pool.tensor_tensor(beat[:, :, :, :].rearrange("p s e f -> p (s e f)"),
                                       more[:, :, :, :].rearrange("p s e f -> p (s e f)"),
                                       same_l[:, :, :, :].rearrange("p s e f -> p (s e f)"), ALU.add).then_inc(beat_ready, 1)
                    if k.has(d - 1):
                        pool.wait_ge(picked_ready, k.n(d - 1))
                    pool.wait_ge(beat_ready, k.n(d))
                    b8 = beat[:, :, :, :].rearrange("p s e f -> p (s e) f")
                    pool.tensor_tensor(b4[:, :, :], b8[:, :, 0:4], b8[:, :, 4:8], ALU.add).then_inc(b4_ready, 1)
                    pool.wait_ge(b4_ready, k.n(d))
                    pool.tensor_tensor(b2[:, :, :], b4[:, :, 0:2], b4[:, :, 2:4], ALU.add).then_inc(b2_ready, 1)
                    pool.wait_ge(b2_ready, k.n(d))
                    pool.tensor_tensor(flat(rank[:, :, :]), b2[:, :, 0], b2[:, :, 1], ALU.add).then_inc(rank_ready, 1)
                if k.has(c):
                    pool.wait_ge(ln2_var, k.n(c))
                    pool.tensor_tensor(rs2[c % 2][:, :], ve2[c % 2][:, :], minus_half[:, :], ALU.pow).then_inc(ln2_rstd, 1)
                    pool.wait_ge(ln2_rstd, k.n(c))
                    pool.tensor_tensor(nr2[c % 2][:, :], nm2[c % 2][:, :], rs2[c % 2][:, :], ALU.mult).then_inc(ln2_shift, 1)
                if k.has(a):
                    pool.wait_ge(cn_hi, k.n(a))
                    if k.has(a - 1):
                        pool.wait_ge(ac_done, k.n(a - 1))
                    low(flat(cn_s[a % 2][1][:, :, :]), flat(cn[a % 2][:, :, :]), flat(cn_s[a % 2][0][:, :, :]), cn_lo)
                if k.has(f):
                    pool.wait_ge(ln1_var, k.n(f))
                    pool.tensor_tensor(rs1[f % 2][:, :], ve1[f % 2][:, :], minus_half[:, :], ALU.pow).then_inc(ln1_rstd, 1)
                    pool.wait_ge(ln1_rstd, k.n(f))
                    pool.tensor_tensor(nr1[f % 2][:, :], nm1[f % 2][:, :], rs1[f % 2][:, :], ALU.mult).then_inc(ln1_shift, 1)
                if k.has(i):
                    if i == 0:
                        pool.wait_ge(setup_dve, 17)
                    pool.wait_ge(xr_in[i % 2], k.dma(i))
                    for s in range(HALVES):
                        last = pool.tensor_tensor(xr_sb[i % 2][:, s * D:(s + 1) * D], xr_sb[i % 2][:, s * D:(s + 1) * D],
                                                  tgbo[:, :], ALU.add)
                    last.then_inc(xr_ready, 1)

            run(pool, iteration)


_INS = ["x", "ctx_1024", "g_xattn", "g_ffn", "L0_xattn_Wi", "L0_xattn_bi", "L0_xattn_Wg", "L0_xattn_bg", "L0_xattn_A",
        "L0_xattn_Bm", "L0_xattn_Wo", "L0_xattn_bo", "L0_xattn_decay", "L0_ffn_w_shared_in", "L0_ffn_w_shared_out",
        "L0_ffn_w1_shared", "L0_ffn_w2", "L0_ffn_w_gate", "L0_ffn_gate_bias"]
_OUTS = [((B, S, D), "float32")]


def kernel(**inputs):
    import numpy as _np
    import concourse.bacc as _bacc
    from concourse import mybir as _mybir
    from concourse.bass_utils import run_bass_kernel_spmd as _run

    nc = _bacc.Bacc("TRN2", target_bir_lowering=False, num_devices=1)
    arrays, args = {}, []
    for name in _INS:
        a = _np.ascontiguousarray(inputs[name])
        arrays[f"in_{name}_dram"] = a
        args.append(nc.dram_tensor(f"in_{name}_dram", a.shape, _mybir.dt.from_np(a.dtype), kind="ExternalInput").ap())
    for i, (shape, dtype) in enumerate(_OUTS):
        dt = _mybir.dt.from_np(_np.dtype(dtype))
        args.append(nc.dram_tensor(f"out_{i}_dram", shape, dt, kind="ExternalOutput").ap())
    gated_layer(nc, *args)
    r = _run(nc, [arrays], core_ids=[0])
    return r.results[0]["out_0_dram"]
```

```python
from contextlib import ExitStack

import concourse.bass as bass
from concourse import mybir

F32 = mybir.dt.float32
F32R = mybir.dt.float32r
F16 = mybir.dt.float16
ALU = mybir.AluOpType
ACT = mybir.ActivationFunctionType
AX_X = mybir.AxisListType.X

P = 128
B, S, D = 32, 128, 256
KC = D // P
HEADS = 16
E = 8
STEPS = 8
HALVES = 2
J = STEPS // HALVES
TOK = STEPS * B
TILES = S // STEPS
EPS = 1e-5
PSCALE = 256.0


def gated_layer(nc, x, ctx_in, g_xattn, g_ffn, Wi, bi, Wg, bg, A, Bm, Wo, bo, decay,
                w_shared_in, w_shared_out, w1_shared, w2, w_gate, gate_bias, out):
    with ExitStack() as stack:
        def sb(name, shape, dt=F32):
            return stack.enter_context(nc.sbuf_tensor(name, shape, dt))

        def two(name, shape, dt=F32):
            return [sb(f"{name}{n}", shape, dt) for n in range(2)]

        def one(name, shape, dt=F32):
            return [sb(name, shape, dt)] * 2

        def sem(name):
            return stack.enter_context(nc.semaphore(name))

        x_tiles = x.rearrange("b (u j s) d -> u b j (s d)", j=J, s=HALVES)
        c_tiles = ctx_in.rearrange("b (u j s) d -> u b j (s d)", j=J, s=HALVES)
        o_tiles = out.rearrange("b (u j s) d -> u b j (s d)", j=J, s=HALVES)

        raw_sq = {n: sb(f"raw_{n}", [P, KC, D]) for n in ("Wi", "Wg", "Bm", "A", "Wo", "so")}
        raw_wide = {n: sb(f"raw_{n}", [P, KC, 2 * D]) for n in ("sh", "w1")}
        raw_wgate = sb("raw_wgate", [P, KC, E])
        cols = sb("cols", [P, 4])
        bi_wide = sb("bi_wide", [P, KC, P])
        WgT = sb("WgT", [P, KC, D])
        BmT = sb("BmT", [P, KC, D])
        split = {}
        for n in ("inp", "gate", "bm", "a", "wo", "so"):
            split[n] = (sb(f"{n}_hi", [P, KC, D], F32R), sb(f"{n}_lo", [P, KC, D], F32R))
        for n in ("sh", "w1"):
            split[n] = (sb(f"{n}_hi", [P, KC, 2 * D], F32R), sb(f"{n}_lo", [P, KC, 2 * D], F32R))
        split["w2"] = (sb("w2_hi", [P, KC, E, D], F32R), sb("w2_lo", [P, KC, E, D], F32R))
        split["wgate"] = (sb("wgate_hi", [P, KC, E], F32R), sb("wgate_lo", [P, KC, E], F32R))
        raw_w2 = [raw_sq[n] for n in ("Wi", "Wg", "Bm", "A")] + [WgT, BmT, sb("raw_w2", [P, KC, D]), raw_sq["Wo"]]
        a16 = (sb("a16_hi", [P, KC, D], F16), sb("a16_lo", [P, KC, D], F16))
        cp = sb("cp", [P, D], F32R)
        cp_hi = sb("cp_hi", [P, D], F32R)
        ones = sb("ones", [P, TOK], F32R)
        ident = sb("ident", [P, P])
        minus_half = sb("minus_half", [P, HALVES])
        half_gate_bias = sb("half_gate_bias", [P, KC])
        gx = sb("gx", [P, 1])
        gf = sb("gf", [P, 1])
        tgx = sb("tgx", [P, 1])
        tgf = sb("tgf", [P, 1])
        bo_all = sb("bo_all", [P, D])
        tgbo = sb("tgbo", [P, D])
        gb_all = sb("gb_all", [P, E])
        dec_cols = sb("dec_cols", [P, KC])
        dmask = sb("dmask", [P, KC, B, STEPS + 1])
        tri = sb("tri", [P, E, E])

        x_sb = two("x_sb", [P, HALVES * D])
        c_sb = two("c_sb", [P, HALVES * D])
        xr_sb = two("xr_sb", [P, HALVES * D])
        xn1 = one("xn1", [P, HALVES, D])
        c2 = one("c2", [P, KC, B, STEPS + 1])
        r = two("r", [P, KC, B, STEPS + 1])
        ret = one("ret", [P, KC, TOK])
        ret_s = [(sb("ret_hi", [P, KC, TOK], F32R), sb("ret_lo", [P, KC, TOK], F32R))] * 2
        gt = two("gt", [P, KC, TOK])
        inp = one("inp_sb", [P, KC, TOK])
        cn = one("cn", [P, KC, TOK])
        cn_s = [(sb("cn_hi", [P, KC, TOK], F32R), sb("cn_lo", [P, KC, TOK], F32R))] * 2
        state = two("state", [P, KC, TOK])
        st_s = [(sb("st_hi", [P, KC, TOK], F32R), sb("st_lo", [P, KC, TOK], F32R))] * 2
        u_hi = two("u_hi", [P, KC, B], F16)
        u_lo = two("u_lo", [P, KC, B], F16)
        u_full = two("u_full", [P, KC, B])
        x1 = two("x1", [P, HALVES, D])
        xn2 = one("xn2", [P, HALVES, D])
        xn2_s = [(sb("xn2_hi", [P, KC, TOK], F32R), sb("xn2_lo", [P, KC, TOK], F32R))] * 2
        sil_s = sb("sil_s", [P, KC, TOK])
        sil_w = sb("sil_w", [P, KC, TOK])
        hs = sb("hs", [P, KC, TOK])
        hid = sb("hid", [P, KC, TOK])
        hs_s = (sb("hs_hi", [P, KC, TOK], F32R), sb("hs_lo", [P, KC, TOK], F32R))
        hid_s = [(sb(f"hid_hi{n}", [P, KC, TOK], F32R), sb(f"hid_lo{n}", [P, KC, TOK], F32R)) for n in range(2)]
        acc = two("acc", [P, HALVES, D])
        st1 = two("st1", [P, HALVES, 6])
        mv1 = two("mv1", [P, HALVES, 2])
        ve1 = two("ve1", [P, HALVES])
        nm1 = two("nm1", [P, HALVES])
        rs1 = two("rs1", [P, HALVES])
        nr1 = two("nr1", [P, HALVES])
        st2 = two("st2", [P, HALVES, 6])
        mv2 = two("mv2", [P, HALVES, 2])
        ve2 = two("ve2", [P, HALVES])
        nm2 = two("nm2", [P, HALVES])
        rs2 = two("rs2", [P, HALVES])
        nr2 = two("nr2", [P, HALVES])
        lg = sb("lg", [P, HALVES, E])
        lmax = sb("lmax", [P, HALVES])
        ld = sb("ld", [P, HALVES, E])
        lt = sb("lt", [P, HALVES, E])
        num = sb("num", [P, HALVES, E])
        den = sb("den", [P, HALVES, E])
        rden = sb("rden", [P, HALVES, E])
        ex = sb("ex", [P, HALVES, E])
        esum = sb("esum", [P, HALVES])
        rsum = sb("rsum", [P, HALVES])
        rsg = sb("rsg", [P, HALVES])
        more = sb("more", [P, HALVES, E, E])
        same = sb("same", [P, HALVES, E, E])
        same_l = sb("same_l", [P, HALVES, E, E])
        beat = sb("beat", [P, HALVES, E, E])
        b4 = sb("b4", [P, HALVES * E, 4])
        b2 = sb("b2", [P, HALVES * E, 2])
        rank = sb("rank", [P, HALVES, E])
        picked = sb("picked", [P, HALVES, E])
        wts = two("wts", [P, HALVES, E])

        rec = [stack.enter_context(nc.psum_tensor(f"rec{n}", [P, KC, TOK], F32)) for n in range(2)]
        bank = [stack.enter_context(nc.psum_tensor(f"bank{n}", [P, 512], F32)) for n in range(6)]

        load = {n: sem(f"load_{n}") for n in
                ("Wi", "Wg", "Bm", "A", "Wo", "so", "sh", "w1", "w2", "wgate", "decay", "biases", "small")}
        x_in = [sem("x_in0"), sem("x_in1")]
        c_in = [sem("c_in0"), sem("c_in1")]
        xr_in = [sem("xr_in0"), sem("xr_in1")]
        out_done = [sem("out_done0"), sem("out_done1")]
        consts = sem("consts")
        table_in = sem("table_in")
        tri_ready = sem("tri_ready")
        setup_pe = sem("setup_pe")
        setup_dve = sem("setup_dve")
        setup_act = sem("setup_act")
        wide_hi = sem("wide_hi")
        wide_lo = sem("wide_lo")
        ffn2_hi = sem("ffn2_hi")
        so_split = sem("so_split")
        w2_lo = sem("w2_lo")
        ln1_stats, ln1_aggr, ln1_var, ln1_rstd, ln1_shift, xn1_ready = (sem(n) for n in ("ln1_stats", "ln1_aggr", "ln1_var", "ln1_rstd", "ln1_shift", "xn1_ready"))
        tc_done, tx_done = sem("tc_done"), sem("tx_done")
        c2_ready, r_ready, ret_ready, ret_hi, ret_lo = (sem(n) for n in ("c2_ready", "r_ready", "ret_ready", "ret_hi_ready", "ret_lo_ready"))
        inp_done, gate_done = sem("inp_done"), sem("gate_done")
        gt_ready, inp_ready, cn_ready, cn_hi, cn_lo = (sem(n) for n in ("gt_ready", "inp_ready", "cn_ready", "cn_hi_ready", "cn_lo_ready"))
        bm_done = sem("bm_done")
        ac_done = sem("ac_done")
        uh_ready = [sem(f"uh_ready{t}") for t in range(STEPS)]
        ul_ready = [sem(f"ul_ready{t}") for t in range(STEPS)]
        sum_done = [sem(f"sum_done{t}") for t in range(STEPS)]
        st_ready = [sem(f"st_ready{t}") for t in range(STEPS)]
        st_hi, st_lo = sem("st_hi_ready"), sem("st_lo_ready")
        xr_ready = sem("xr_ready")
        wo_done, x1_ready, ln2_stats, ln2_aggr, ln2_var, ln2_rstd, ln2_shift, xn2_ready = (
            sem(n) for n in ("wo_done", "x1_ready", "ln2_stats", "ln2_aggr", "ln2_var", "ln2_rstd", "ln2_shift", "xn2_ready"))
        t2_done, xn2_hi, xn2_lo = sem("t2_done"), sem("xn2_hi_ready"), sem("xn2_lo_ready")
        sh_done, w1_done = sem("sh_done"), sem("w1_done")
        sil_s_ready, sil_w_ready, hs_ready, hid_ready = (sem(n) for n in ("sil_s_ready", "sil_w_ready", "hs_ready", "hid_ready"))
        hs_hi, hs_lo, hid_hi, hid_lo = (sem(n) for n in ("hs_hi_ready", "hs_lo_ready", "hid_hi_ready", "hid_lo_ready"))
        lg_done, lg_ready = sem("lg_done"), sem("lg_ready")
        lmax_ready, ld_ready, lt_ready = sem("lmax_ready"), sem("ld_ready"), sem("lt_ready")
        numden, rden_ready, ex_ready, esum_ready, rsum_ready, rsg_ready = (
            sem(n) for n in ("numden_ready", "rden_ready", "ex_ready", "esum_ready", "rsum_ready", "rsg_ready"))
        same_ready, samel_ready, beat_ready, rank_ready, picked_ready, wts_ready = (
            sem(n) for n in ("same_ready", "samel_ready", "beat_ready", "rank_ready", "picked_ready", "wts_ready"))
        so_done, acc_ready = sem("so_done"), sem("acc_ready")
        b4_ready, b2_ready = sem("b4_ready"), sem("b2_ready")
        pair_done = [sem(f"pair_done{k}") for k in range(E)]
        pair_half = [sem(f"pair_half{k}") for k in range(E)]
        pair_used = [sem(f"pair_used{k}") for k in range(E)]

        BIASES = 16 * 2
        SMALL = 16 * 4

        B_TC, B_TX, B_WO, B_SO, B_INP, B_GATE, B_T2, B_LG = 0, 1, 4, 0, 2, 3, 0, 3
        B_SHA, B_SHB, B_W1A, B_W1B = 0, 1, 4, 5
        B_PAIR = [4, 1, 2, 4, 5, 3, 5, 1]

        def halves(ap):
            return ap.rearrange("p (s b j) -> p s b j", s=HALVES, b=B)

        def by_time(ap):
            return ap.rearrange("p b (j s) -> p s b j", s=HALVES)

        def step_of(t3, t):
            return t3[:, :, :].rearrange("p c (s b j) -> p c s b j", s=HALVES, b=B)[:, :, t % HALVES, :, t // HALVES]

        def flat(t3):
            return t3.rearrange("p a b -> p (a b)")

        class Static:
            static = True

            def n(self, m):
                return m + 1

            def dma(self, m):
                return 16 * (m // 2 + 1)

            def has(self, m):
                return 0 <= m < TILES

            def tile(self, m):
                return m

        class Looped:
            static = False

            def __init__(self, eng, reg):
                self.eng, self.reg, self.known = eng, reg, {}

            def kept(self, key, value):
                if key not in self.known:
                    self.known[key] = self.eng.snap(value)
                return self.known[key]

            def n(self, m):
                return self.kept(("n", m), self.reg * 2 + (m + 1))

            def dma(self, m):
                return self.kept(("dma", m // 2), self.reg * 16 + 16 * (m // 2 + 1))

            def has(self, m):
                return True

            def tile(self, m):
                return self.reg * 2 + m

        FIRST_FULL, LAST_FULL = 3, TILES - 4
        TAIL = range(LAST_FULL + 1, TILES + 3)

        def run(eng, iteration):
            for i in range(1, FIRST_FULL):
                iteration(i, Static())
            with eng.Fori(FIRST_FULL // 2, LAST_FULL // 2) as reg:
                k = Looped(eng, reg)
                iteration(1, k)
                iteration(2, k)
            for i in TAIL:
                iteration(i, Static())

        first = Static()

        block = stack.enter_context(nc.Block())

        @block.sync
        def _(sp):
            def part(t2):
                return t2[:, :].rearrange("(b j) e -> b j e", j=J)

            def load_x(m, k):
                sp.dma_start(x_sb[m % 2][:, :], x_tiles[k.tile(m)]).then_inc(x_in[m % 2], 16)

            def load_xr(i, k):
                sp.dma_start(xr_sb[i % 2][:, :], x_tiles[k.tile(i)]).then_inc(xr_in[i % 2], 16)

            def load_c(m, k):
                sp.dma_start(c_sb[m % 2][:, :], c_tiles[k.tile(m)]).then_inc(c_in[m % 2], 16)

            def square(n, w):
                sp.dma_start(raw_sq[n][:, :, :], w.rearrange("(k p) i -> p k i", p=P)).then_inc(load[n], 16)

            load_c(0, first)
            square("Wi", Wi)
            square("Wg", Wg)
            load_x(0, first)
            with nc.allow_non_contiguous_dma(reason="small vectors"):
                for kc in range(KC):
                    sp.dma_start(dec_cols[:, kc:kc + 1],
                                 decay[0, kc * HEADS // KC:(kc + 1) * HEADS // KC, :].unsqueeze(1).to_broadcast([HEADS // KC, D // HEADS, 1])).then_inc(load["decay"], 16)
                square("Bm", Bm)
                sp.dma_start(cols[:, 0:KC], bi.rearrange("(k p) -> p k", p=P)).then_inc(load["biases"], 16)
                sp.dma_start(cols[:, KC:2 * KC], bg.rearrange("(k p) -> p k", p=P)).then_inc(load["biases"], 16)
                square("A", A)
                load_x(1, first)
                load_c(1, first)
                sp.dma_start(gx[:, :], g_xattn.partition_broadcast(P)).then_inc(load["small"], 16)
                sp.dma_start(gf[:, :], g_ffn.partition_broadcast(P)).then_inc(load["small"], 16)
                sp.dma_start(bo_all[:, :], bo.partition_broadcast(P)).then_inc(load["small"], 16)
                sp.dma_start(gb_all[:, :], gate_bias.partition_broadcast(P)).then_inc(load["small"], 16)
                square("Wo", Wo)
                sp.dma_start(raw_wide["sh"][:, :, :], w_shared_in.rearrange("(k p) h -> p k h", p=P)).then_inc(load["sh"], 16)
                sp.dma_start(raw_wgate[:, :, :], w_gate.rearrange("(k p) e -> p k e", p=P)).then_inc(load["wgate"], 16)
                sp.dma_start(raw_wide["w1"][:, :, :], w1_shared.rearrange("(k p) h -> p k h", p=P)).then_inc(load["w1"], 16)
                square("so", w_shared_out)
            load_xr(0, first)
            sp.wait_ge(tc_done, 1)
            load_c(2, first)
            sp.wait_ge(xn1_ready, 1)
            load_x(2, first)
            sp.wait_ge(setup_pe, 7)
            for e in range(E):
                if e == E - 1:
                    sp.wait_ge(setup_pe, 8)
                sp.dma_start(raw_w2[e][:, :, :], w2[e].rearrange("(k p) c -> p k c", p=P)).then_inc(load["w2"], 16)
            sp.wait_ge(xn1_ready, 2)
            load_x(3, first)

            def iteration(i, k):
                m = i + 3
                if k.has(m):
                    sp.wait_ge(xn1_ready, k.n(m - 2))
                    load_x(m, k)
                m = i + 2
                if k.has(m):
                    sp.wait_ge(tc_done, k.n(m - 2))
                    load_c(m, k)
                if k.has(i):
                    if k.has(i - 2):
                        sp.wait_ge(x1_ready, k.n(i - 2))
                    load_xr(i, k)
                if k.has(i - 3):
                    sp.wait_ge(pair_used[E - 1], k.n(i - 3))
                    sp.dma_start(o_tiles[k.tile(i - 3)], acc[(i - 3) % 2][:, :, :].rearrange("p s d -> p (s d)")).then_inc(out_done[(i - 3) % 2], 16)

            run(sp, iteration)
            for n in range(2):
                sp.wait_ge(out_done[n], 16 * (TILES // 2))

        @block.tensor
        def _(pe):
            def transposed(dst, src):
                for kr in range(KC):
                    for kc in range(KC):
                        last = pe.transpose(dst[:, kc * D + kr * P:kc * D + (kr + 1) * P],
                                            src[:, kr, kc * P:(kc + 1) * P], ident[:, :])
                return last

            def composed(dst, right):
                for kc in range(KC):
                    for mk in range(KC):
                        last = pe.matmul(dst[:, kc * D:(kc + 1) * D], raw_sq["Wi"][:, mk, kc * P:(kc + 1) * P],
                                         right[:, mk, :], start=(kc == 0 and mk == 0), stop=(mk == KC - 1),
                                         skip_group_check=True)
                return last

            def feature_product(dst, n, acts, start, col=0, done=None):
                w_hi, w_lo = split[n]
                a_hi, a_lo = acts
                first = start
                for oc in range(KC):
                    o = dst[:, oc * TOK:(oc + 1) * TOK]
                    at = slice(col + oc * P, col + (oc + 1) * P)
                    for kc in range(KC):
                        for w, a in ((w_hi, a_hi), (w_hi, a_lo), (w_lo, a_hi)):
                            last = pe.matmul(o, w[:, kc, at], a[:, kc, :], start=first,
                                             stop=(kc == KC - 1 and w is w_lo), skip_group_check=True)
                            first = False
                return last

            def token_product(dst, w, acts, s, start):
                a_hi, a_lo = acts
                first = start
                for kc in range(KC):
                    for a, part in ((a_hi, 0), (a_hi, 1), (a_lo, 0)):
                        last = pe.matmul(dst, a[:, kc, s * P:(s + 1) * P], w(part, kc), start=first,
                                         stop=(kc == KC - 1 and a is a_lo), skip_group_check=True)
                        first = False
                return last

            def recurrence(i, t, k):
                if not k.has(i):
                    return
                o = step_of(rec[i % 2], t)
                pe.wait_ge(uh_ready[t], k.n(i))
                for oc in range(KC):
                    for kc in range(KC):
                        for w in a16:
                            pe.matmul(o[:, oc, :], w[:, kc, oc * P:(oc + 1) * P], u_hi[t % 2][:, kc, :],
                                      start=False, stop=False, skip_group_check=True)
                pe.wait_ge(ul_ready[t], k.n(i))
                for oc in range(KC):
                    for kc in range(KC):
                        last = pe.matmul(o[:, oc, :], a16[0][:, kc, oc * P:(oc + 1) * P], u_lo[t % 2][:, kc, :],
                                         start=False, stop=(kc == KC - 1), skip_group_check=True)
                last.then_inc(sum_done[t], 1)

            def pair(n, m, k):
                q, s = n // 2, n % 2
                if k.static and m == 0:
                    pe.wait_ge(w2_lo, 2 * q + 2)
                last = token_product(bank[B_PAIR[n]][:, :],
                                     lambda part, kc: split["w2"][part][:, kc, 2 * q:2 * q + 2, :].rearrange("p e c -> p (e c)"),
                                     hid_s[m % 2], s, True)
                last.then_inc(pair_done[n], 1)

            def context_transposed(a, k):
                if not k.has(a):
                    return
                if k.has(a - 3):
                    pe.wait_ge(sil_s_ready, k.n(a - 3))
                pe.wait_ge(c_in[a % 2], k.dma(a))
                for s in range(HALVES):
                    for kc in range(KC):
                        last = pe.transpose(bank[B_TC][:, kc * TOK + s * P:kc * TOK + (s + 1) * P],
                                            c_sb[a % 2][:, s * D + kc * P:s * D + (kc + 1) * P], ident[:, :])
                last.then_inc(tc_done, 1)

            def x_transposed(a, k):
                if not k.has(a):
                    return
                if k.has(a - 3):
                    pe.wait_ge(hs_ready, k.n(a - 3))
                pe.wait_ge(xn1_ready, k.n(a))
                for s in range(HALVES):
                    for kc in range(KC):
                        last = pe.transpose(bank[B_TX][:, kc * TOK + s * P:kc * TOK + (s + 1) * P],
                                            xn1[a % 2][:, s, kc * P:(kc + 1) * P], ident[:, :])
                last.then_inc(tx_done, 1)

            def inp_product(a, k):
                if not k.has(a):
                    return
                if k.has(a - 4):
                    pe.wait_ge(pair_used[2], k.n(a - 4))
                pe.wait_ge(ret_hi, k.n(a))
                pe.wait_ge(ret_lo, k.n(a))
                feature_product(bank[B_INP], "inp", ret_s[a % 2], True).then_inc(inp_done, 1)

            def gate_product(a, k):
                if not k.has(a):
                    return
                if k.has(a - 4):
                    pe.wait_ge(pair_used[5], k.n(a - 4))
                feature_product(bank[B_GATE], "gate", ret_s[a % 2], True).then_inc(gate_done, 1)

            def addend_bm(a, k):
                if not k.has(a):
                    return
                if k.has(a - 2):
                    pe.wait_ge(st_ready[STEPS - 1], k.n(a - 2))
                rec_flat = flat(rec[a % 2][:, :, :])
                feature_product(rec_flat, "bm", ret_s[a % 2], True)
                for oc in range(KC):
                    last = pe.matmul(rec_flat[:, oc * TOK:(oc + 1) * TOK], cp[:, oc * P:(oc + 1) * P], ones[:, :],
                                     start=False, stop=False, skip_group_check=True)
                last.then_inc(bm_done, 1)

            def addend_a(a, k):
                if not k.has(a):
                    return
                pe.wait_ge(cn_hi, k.n(a))
                pe.wait_ge(cn_lo, k.n(a))
                feature_product(flat(rec[a % 2][:, :, :]), "a", cn_s[a % 2], False).then_inc(ac_done, 1)

            pe.wait_ge(consts, 1)
            context_transposed(0, first)
            pe.wait_ge(load["Wi"], 16)
            transposed(bank[3], raw_sq["Wi"]).then_inc(setup_pe, 1)
            pe.wait_ge(load["Wg"], 16)
            transposed(bank[4], raw_sq["Wg"]).then_inc(setup_pe, 1)
            pe.wait_ge(load["Bm"], 16)
            transposed(bank[5], raw_sq["Bm"]).then_inc(setup_pe, 1)
            pe.wait_ge(setup_act, 2)
            composed(flat(rec[1][:, :, :]), WgT).then_inc(setup_pe, 1)
            pe.wait_ge(setup_act, 4)
            composed(flat(rec[0][:, :, :]), BmT).then_inc(setup_pe, 1)
            x_transposed(0, first)
            pe.wait_ge(setup_dve, 2)
            for oc in range(KC):
                for mk in range(KC):
                    pe.matmul(bank[4][:, 256 + oc:257 + oc], WgT[:, mk, oc * P:(oc + 1) * P], bi_wide[:, mk, 0:1],
                              start=(oc == 0 and mk == 0), stop=(mk == KC - 1), skip_group_check=True)
            for mk in range(KC):
                last = pe.matmul(bank[4][:, 0:D], bi_wide[:, mk, :], BmT[:, mk, :], start=False,
                                 stop=(mk == KC - 1), skip_group_check=True)
            last.then_inc(setup_pe, 1)
            pe.wait_ge(load["A"], 16)
            transposed(bank[5], raw_sq["A"]).then_inc(setup_pe, 1)
            pe.wait_ge(setup_dve, 3)
            inp_product(0, first)
            pe.wait_ge(setup_dve, 4)
            gate_product(0, first)
            context_transposed(1, first)
            pe.wait_ge(setup_dve, 5)
            pe.wait_ge(setup_dve, 7)
            addend_bm(0, first)
            x_transposed(1, first)
            pe.wait_ge(load["Wo"], 16)
            transposed(bank[4], raw_sq["Wo"]).then_inc(setup_pe, 1)
            pe.wait_ge(setup_dve, 9)
            addend_a(0, first)
            pe.wait_ge(setup_dve, 10)
            recurrence(0, 0, first)
            inp_product(1, first)
            recurrence(0, 1, first)
            gate_product(1, first)
            recurrence(0, 2, first)
            recurrence(0, 3, first)
            addend_bm(1, first)
            recurrence(0, 4, first)
            recurrence(0, 5, first)
            addend_a(1, first)
            recurrence(0, 6, first)
            recurrence(0, 7, first)

            def iteration(i, k):
                a, c, d, e = i + 1, i - 1, i - 2, i - 3
                recurrence(i, 0, k)
                context_transposed(a, k)
                x_transposed(a, k)
                if k.has(e):
                    if k.has(d):
                        pe.wait_ge(lg_ready, k.n(d))
                    else:
                        pe.wait_ge(pair_used[5], k.n(e - 1))
                    pair(5, e, k)
                recurrence(i, 1, k)
                if k.has(c):
                    if k.has(d):
                        pe.wait_ge(sil_w_ready, k.n(d))
                    pe.wait_ge(st_hi, k.n(c))
                    pe.wait_ge(st_lo, k.n(c))
                    for s in range(HALVES):
                        last = token_product(bank[B_WO][:, s * D:(s + 1) * D],
                                             lambda part, kc: split["wo"][part][:, kc, :], st_s[c % 2], s, s == 0)
                    last.then_inc(wo_done, 1)
                if k.has(e):
                    if k.has(d):
                        pe.wait_ge(hid_ready, k.n(d))
                    else:
                        pe.wait_ge(pair_used[4], k.n(e))
                    pair(6, e, k)
                recurrence(i, 2, k)
                if k.has(d):
                    if k.static and d == 0:
                        pe.wait_ge(so_split, 1)
                    if k.has(a):
                        pe.wait_ge(c2_ready, k.n(a))
                    pe.wait_ge(hs_hi, k.n(d))
                    pe.wait_ge(hs_lo, k.n(d))
                    for s in range(HALVES):
                        last = token_product(bank[B_SO][:, s * D:(s + 1) * D],
                                             lambda part, kc: split["so"][part][:, kc, :], hs_s, s, s == 0)
                    last.then_inc(so_done, 1)
                if k.has(e):
                    if k.has(a):
                        pe.wait_ge(ret_ready, k.n(a))
                    if not k.has(d):
                        pe.wait_ge(pair_used[1], k.n(e))
                    pair(7, e, k)
                recurrence(i, 3, k)
                inp_product(a, k)
                gate_product(a, k)
                if k.has(d):
                    if k.has(c):
                        pe.wait_ge(x1_ready, k.n(c))
                    pe.wait_ge(hid_hi, k.n(d))
                    pe.wait_ge(hid_lo, k.n(d))
                    pair(0, d, k)
                recurrence(i, 4, k)
                addend_bm(a, k)
                if k.has(d):
                    if k.has(e):
                        pe.wait_ge(pair_used[7], k.n(e))
                    pair(1, d, k)
                if k.has(c):
                    if k.has(d):
                        pe.wait_ge(acc_ready, k.n(d))
                    pe.wait_ge(xn2_ready, k.n(c))
                    for s in range(HALVES):
                        for kc in range(KC):
                            last = pe.transpose(bank[B_T2][:, kc * TOK + s * P:kc * TOK + (s + 1) * P],
                                                xn2[c % 2][:, s, kc * P:(kc + 1) * P], ident[:, :])
                    last.then_inc(t2_done, 1)
                recurrence(i, 5, k)
                if k.has(d):
                    if k.has(a):
                        pe.wait_ge(inp_ready, k.n(a))
                    elif k.has(e):
                        pe.wait_ge(pair_used[2], k.n(e))
                    pair(2, d, k)
                    pe.wait_ge(pair_used[0], k.n(d))
                    pair(3, d, k)
                    if k.has(e):
                        pe.wait_ge(pair_used[6], k.n(e))
                    pair(4, d, k)
                recurrence(i, 6, k)
                if k.has(c):
                    pe.wait_ge(xn2_hi, k.n(c))
                    pe.wait_ge(xn2_lo, k.n(c))
                    if k.static and c == 0:
                        pe.wait_ge(wide_lo, 2)
                    feature_product(bank[B_SHA], "sh", xn2_s[c % 2], True)
                    if k.has(d):
                        pe.wait_ge(pair_used[1], k.n(d))
                    feature_product(bank[B_SHB], "sh", xn2_s[c % 2], True, col=D).then_inc(sh_done, 1)
                    if k.has(a):
                        pe.wait_ge(gt_ready, k.n(a))
                    elif k.has(e):
                        pe.wait_ge(pair_used[5], k.n(e))
                    for s in range(HALVES):
                        last = token_product(bank[B_LG][:, s * E:(s + 1) * E],
                                             lambda part, kc: split["wgate"][part][:, kc, :], xn2_s[c % 2], s, s == 0)
                    last.then_inc(lg_done, 1)
                recurrence(i, 7, k)
                addend_a(a, k)
                if k.has(c):
                    if k.has(d):
                        pe.wait_ge(pair_used[3], k.n(d))
                    if k.static and c == 0:
                        pe.wait_ge(wide_lo, 3)
                    feature_product(bank[B_W1A], "w1", xn2_s[c % 2], True)
                    if k.has(d):
                        pe.wait_ge(pair_used[4], k.n(d))
                    feature_product(bank[B_W1B], "w1", xn2_s[c % 2], True, col=D).then_inc(w1_done, 1)

            run(pe, iteration)

        @block.scalar
        def _(act):
            def tanh_step(i, t, k):
                if k.has(i):
                    if t == 0 and k.has(i - 2):
                        act.wait_ge(st_lo, k.n(i - 2))
                    act.wait_ge(sum_done[t], k.n(i))
                    act.activation(step_of(state[i % 2], t), step_of(rec[i % 2], t), ACT.Tanh,
                                   scale=1.0 / PSCALE).then_inc(st_ready[t], 1)

            def context_squares(a, k):
                if not k.has(a):
                    return
                act.wait_ge(tc_done, k.n(a))
                if k.has(a - 1):
                    act.wait_ge(r_ready, k.n(a - 1))
                    act.copy(c2[a % 2][:, :, :, 0], r[(a - 1) % 2][:, :, :, STEPS])
                for kc in range(KC):
                    last = act.activation(by_time(c2[a % 2][:, kc, :, 1:STEPS + 1]),
                                          halves(bank[B_TC][:, kc * TOK:(kc + 1) * TOK]), ACT.Square)
                last.then_inc(c2_ready, 1)

            def ret_high(a, k):
                if not k.has(a):
                    return
                act.wait_ge(ret_ready, k.n(a))
                if k.has(a - 1):
                    act.wait_ge(bm_done, k.n(a - 1))
                act.copy(flat(ret_s[a % 2][0][:, :, :]), flat(ret[a % 2][:, :, :])).then_inc(ret_hi, 1)

            def inp_biased(a, k):
                if not k.has(a):
                    return
                act.wait_ge(inp_done, k.n(a))
                if k.has(a - 1):
                    act.wait_ge(cn_ready, k.n(a - 1))
                for kc in range(KC):
                    last = act.activation(inp[a % 2][:, kc, :], bank[B_INP][:, kc * TOK:(kc + 1) * TOK],
                                          ACT.Identity, bias=cols[:, kc:kc + 1])
                last.then_inc(inp_ready, 1)

            def gate_tanh(a, k):
                if not k.has(a):
                    return
                act.wait_ge(gate_done, k.n(a))
                if k.has(a - 2):
                    act.wait_ge(uh_ready[STEPS - 1], k.n(a - 2))
                for kc in range(KC):
                    last = act.activation(gt[a % 2][:, kc, :], bank[B_GATE][:, kc * TOK:(kc + 1) * TOK],
                                          ACT.Tanh, bias=half_gate_bias[:, kc:kc + 1], scale=0.5)
                last.then_inc(gt_ready, 1)

            def cn_high(a, k):
                if not k.has(a):
                    return
                act.wait_ge(cn_ready, k.n(a))
                if k.has(a - 1):
                    act.wait_ge(ac_done, k.n(a - 1))
                act.copy(flat(cn_s[a % 2][0][:, :, :]), flat(cn[a % 2][:, :, :])).then_inc(cn_hi, 1)

            def x_normalised(f, k):
                if not k.has(f):
                    return
                act.wait_ge(ln1_shift, k.n(f))
                if k.has(f - 1):
                    act.wait_ge(tx_done, k.n(f - 1))
                for s in range(HALVES):
                    last = act.activation(xn1[f % 2][:, s, :], x_sb[f % 2][:, s * D:(s + 1) * D], ACT.Identity,
                                          bias=nr1[f % 2][:, s:s + 1], scale=rs1[f % 2][:, s:s + 1])
                last.then_inc(xn1_ready, 1)

            def w2_high(e):
                act.wait_ge(load["w2"], 16 * E)
                act.copy(split["w2"][0][:, :, e, :], raw_w2[e][:, :, :]).then_inc(ffn2_hi, 1)

            act.wait_ge(table_in, 1)
            act.activation(tgf[:, :], ones[:, 0:1].bitcast(F32), ACT.Silu).then_inc(setup_act, 1)
            context_squares(0, first)
            act.wait_ge(setup_pe, 2)
            act.copy(flat(WgT[:, :, :]), bank[4][:, :]).then_inc(setup_act, 1)
            act.copy(flat(split["inp"][0][:, :, :]), bank[3][:, :]).then_inc(setup_act, 1)
            act.wait_ge(setup_pe, 3)
            act.mul(flat(BmT[:, :, :]), bank[5][:, :], PSCALE).then_inc(setup_act, 1)
            x_normalised(0, first)
            act.wait_ge(setup_pe, 4)
            act.copy(flat(split["gate"][0][:, :, :]), flat(rec[1][:, :, :])).then_inc(setup_act, 1)
            act.wait_ge(setup_pe, 5)
            act.copy(flat(split["bm"][0][:, :, :]), flat(rec[0][:, :, :])).then_inc(setup_act, 1)
            ret_high(0, first)
            act.wait_ge(setup_pe, 6)
            act.copy(cp_hi[:, :], bank[4][:, 0:D]).then_inc(setup_act, 1)
            act.wait_ge(setup_pe, 7)
            act.mul(flat(split["a"][0][:, :, :]), bank[5][:, :], -0.5 * PSCALE).then_inc(setup_act, 1)
            act.mul(flat(a16[0][:, :, :]), bank[5][:, :], 0.5 * PSCALE).then_inc(setup_act, 1)
            x_normalised(1, first)
            act.wait_ge(load["biases"], BIASES)
            inp_biased(0, first)
            act.wait_ge(setup_dve, 8)
            gate_tanh(0, first)
            context_squares(1, first)
            cn_high(0, first)
            ret_high(1, first)
            act.wait_ge(load["small"], SMALL)
            act.activation(tgx[:, :], gx[:, :], ACT.Tanh)
            act.wait_ge(setup_act, 1)
            act.activation(tgf[:, :], gf[:, :], ACT.Tanh).then_inc(setup_act, 1)
            tanh_step(0, 0, first)
            act.wait_ge(load["sh"], 16)
            act.copy(flat(split["sh"][0][:, :, :]), flat(raw_wide["sh"][:, :, :])).then_inc(wide_hi, 1)
            tanh_step(0, 1, first)
            inp_biased(1, first)
            tanh_step(0, 2, first)
            gate_tanh(1, first)
            tanh_step(0, 3, first)
            cn_high(1, first)
            tanh_step(0, 4, first)
            act.wait_ge(load["wgate"], 16)
            act.copy(split["wgate"][0][:, :, :], raw_wgate[:, :, :]).then_inc(wide_hi, 1)
            act.wait_ge(load["w1"], 16)
            act.copy(flat(split["w1"][0][:, :, :]), flat(raw_wide["w1"][:, :, :])).then_inc(wide_hi, 1)
            tanh_step(0, 5, first)
            act.wait_ge(setup_pe, 8)
            act.wait_ge(setup_act, 10)
            act.mul(flat(split["wo"][0][:, :, :]), bank[4][:, :], tgx[:, 0:1]).then_inc(setup_act, 1)
            tanh_step(0, 6, first)
            act.wait_ge(load["so"], 16)
            act.mul(flat(split["so"][0][:, :, :]), flat(raw_sq["so"][:, :, :]), tgf[:, 0:1]).then_inc(ffn2_hi, 1)
            w2_high(0)
            tanh_step(0, 7, first)
            x_normalised(2, first)

            def iteration(i, k):
                a, c, d, f = i + 1, i - 1, i - 2, i + 2
                if k.has(c):
                    if k.has(c - 1):
                        act.wait_ge(wo_done, k.n(c - 1))
                    act.wait_ge(st_ready[STEPS - 1], k.n(c))
                    act.copy(flat(st_s[c % 2][0][:, :, :]), flat(state[c % 2][:, :, :])).then_inc(st_hi, 1)
                tanh_step(i, 0, k)
                if k.has(d):
                    act.wait_ge(w1_done, k.n(d))
                    if k.has(i - 3):
                        act.wait_ge(hid_ready, k.n(i - 3))
                    act.activation(flat(sil_w[:, :, :]), bank[B_W1A][:, :], ACT.Silu).then_inc(sil_w_ready, 1)
                    if k.has(i - 3):
                        act.wait_ge(so_done, k.n(i - 3))
                    act.wait_ge(hs_ready, k.n(d))
                    act.copy(flat(hs_s[0][:, :, :]), flat(hs[:, :, :])).then_inc(hs_hi, 1)
                tanh_step(i, 1, k)
                if k.static and i == 1:
                    w2_high(1)
                context_squares(a, k)
                if k.has(d):
                    act.wait_ge(hid_ready, k.n(d))
                    if k.has(d - 2):
                        act.wait_ge(pair_done[E - 1], k.n(d - 2))
                    act.copy(flat(hid_s[d % 2][0][:, :, :]), flat(hid[:, :, :])).then_inc(hid_hi, 1)
                tanh_step(i, 2, k)
                if k.static and i == 1:
                    w2_high(2)
                ret_high(a, k)
                if k.has(d):
                    act.wait_ge(ld_ready, k.n(d))
                    if k.has(d - 1):
                        act.wait_ge(numden, k.n(d - 1))
                    act.activation(flat(lt[:, :, :]), flat(ld[:, :, :]), ACT.Tanh, scale=0.5).then_inc(lt_ready, 1)
                tanh_step(i, 3, k)
                if k.static and i == 1:
                    w2_high(3)
                if k.has(c):
                    act.wait_ge(ln2_shift, k.n(c))
                    if k.has(c - 1):
                        act.wait_ge(t2_done, k.n(c - 1))
                    for s in range(HALVES):
                        last = act.activation(xn2[c % 2][:, s, :], x1[c % 2][:, s, :], ACT.Identity,
                                              bias=nr2[c % 2][:, s:s + 1], scale=rs2[c % 2][:, s:s + 1])
                    last.then_inc(xn2_ready, 1)
                tanh_step(i, 4, k)
                if k.static and i == 1:
                    w2_high(4)
                inp_biased(a, k)
                gate_tanh(a, k)
                tanh_step(i, 5, k)
                if k.static and i == 1:
                    w2_high(5)
                cn_high(a, k)
                if k.has(c):
                    act.wait_ge(t2_done, k.n(c))
                    if k.has(c - 1):
                        act.wait_ge(w1_done, k.n(c - 1))
                    act.copy(flat(xn2_s[c % 2][0][:, :, :]), bank[B_T2][:, :]).then_inc(xn2_hi, 1)
                tanh_step(i, 6, k)
                if k.static and i == 1:
                    w2_high(6)
                x_normalised(f, k)
                tanh_step(i, 7, k)
                if k.static and i == 1:
                    w2_high(7)
                if k.has(c):
                    act.wait_ge(sh_done, k.n(c))
                    if k.has(c - 1):
                        act.wait_ge(hs_ready, k.n(c - 1))
                    act.activation(flat(sil_s[:, :, :]), bank[B_SHA][:, :], ACT.Silu).then_inc(sil_s_ready, 1)

            run(act, iteration)

        @block.vector
        def _(dve):
            def low(n, whole, hi, signal):
                dve.tensor_tensor(n, whole, hi.bitcast(F32), ALU.subtract).then_inc(signal, 1)

            def gated_state(i, t, k):
                if not k.has(i):
                    return
                m, t_next = (i, t + 1) if t + 1 < STEPS else (i + 1, 0)
                if not k.has(m):
                    return
                p = t_next % 2
                old, gate = step_of(state[i % 2], t), step_of(gt[m % 2], t_next)
                if t_next == 0:
                    dve.wait_ge(gt_ready, k.n(m))
                dve.wait_ge(st_ready[t], k.n(i))
                dve.scalar_tensor_tensor(out=u_full[p][:, :, :], in0=gate, scalar=1.0, in1=old,
                                         op0=ALU.add, op1=ALU.mult)
                dve.scalar_tensor_tensor(out=u_hi[p][:, :, :], in0=gate, scalar=1.0, in1=old,
                                         op0=ALU.add, op1=ALU.mult).then_inc(uh_ready[t_next], 1)
                dve.wait_ge(uh_ready[t_next], k.n(m))
                dve.tensor_tensor(u_lo[p][:, :, :], u_full[p][:, :, :], u_hi[p][:, :, :],
                                  ALU.subtract).then_inc(ul_ready[t_next], 1)

            def add_pair(n, m, k):
                if not k.has(m):
                    return
                q, s = n // 2, n % 2
                o = acc[m % 2][:, s, :]
                dve.wait_ge(pair_done[n], k.n(m))
                dve.wait_ge(acc_ready, k.n(m))
                if n >= 2:
                    dve.wait_ge(pair_used[n - 2], k.n(m))
                dve.scalar_tensor_tensor(out=o, in0=bank[B_PAIR[n]][:, 0:D], scalar=wts[m % 2][:, s, 2 * q:2 * q + 1],
                                         in1=o, op0=ALU.mult, op1=ALU.add).then_inc(pair_half[n], 1)
                dve.wait_ge(pair_half[n], k.n(m))
                dve.scalar_tensor_tensor(out=o, in0=bank[B_PAIR[n]][:, D:2 * D], scalar=wts[m % 2][:, s, 2 * q + 1:2 * q + 2],
                                         in1=o, op0=ALU.mult, op1=ALU.add).then_inc(pair_used[n], 1)

            def scanned(a, k):
                if not k.has(a):
                    return
                dve.wait_ge(c2_ready, k.n(a))
                dve.tensor_tensor_scan(r[a % 2][:, :, :, :].rearrange("p c b t -> p (c b t)"),
                                       dmask[:, :, :, :].rearrange("p c b t -> p (c b t)"),
                                       c2[a % 2][:, :, :, :].rearrange("p c b t -> p (c b t)"),
                                       0.0, ALU.mult, ALU.add).then_inc(r_ready, 1)

            def retained(a, k):
                if not k.has(a):
                    return
                dve.wait_ge(r_ready, k.n(a))
                dve.wait_ge(tx_done, k.n(a))
                if k.has(a - 1):
                    dve.wait_ge(ret_hi, k.n(a - 1))
                for kc in range(KC):
                    last = dve.tensor_tensor(halves(ret[a % 2][:, kc, :]), halves(bank[B_TX][:, kc * TOK:(kc + 1) * TOK]),
                                             by_time(r[a % 2][:, kc, :, 1:STEPS + 1]), ALU.mult)
                last.then_inc(ret_ready, 1)

            def ret_low(a, k):
                if not k.has(a):
                    return
                dve.wait_ge(ret_hi, k.n(a))
                dve.wait_ge(ret_ready, k.n(a))
                if k.has(a - 1):
                    dve.wait_ge(bm_done, k.n(a - 1))
                low(flat(ret_s[a % 2][1][:, :, :]), flat(ret[a % 2][:, :, :]), flat(ret_s[a % 2][0][:, :, :]), ret_lo)

            def blend(a, k):
                if not k.has(a):
                    return
                dve.wait_ge(inp_ready, k.n(a))
                dve.wait_ge(gt_ready, k.n(a))
                if k.has(a - 1):
                    dve.wait_ge(cn_hi, k.n(a - 1))
                    dve.wait_ge(cn_lo, k.n(a - 1))
                dve.scalar_tensor_tensor(out=flat(cn[a % 2][:, :, :]), in0=flat(gt[a % 2][:, :, :]), scalar=-1.0,
                                         in1=flat(inp[a % 2][:, :, :]), op0=ALU.add, op1=ALU.mult).then_inc(cn_ready, 1)

            def cn_low(a):
                dve.wait_ge(cn_hi, first.n(a))
                if a > 0:
                    dve.wait_ge(ac_done, first.n(a - 1))
                dve.wait_ge(cn_ready, first.n(a))
                low(flat(cn_s[a % 2][1][:, :, :]), flat(cn[a % 2][:, :, :]), flat(cn_s[a % 2][0][:, :, :]), cn_lo)

            def x_stats(f, k):
                if not k.has(f):
                    return
                dve.wait_ge(x_in[f % 2], k.dma(f))
                for s in range(HALVES):
                    last = dve.bn_stats(st1[f % 2][:, s, :], x_sb[f % 2][:, s * D:(s + 1) * D])
                last.then_inc(ln1_stats, 1)

            def x_aggregate(f, k):
                if not k.has(f):
                    return
                for s in range(HALVES):
                    last = dve.bn_aggr(mv1[f % 2][:, s, :], st1[f % 2][:, s, :])
                last.then_inc(ln1_aggr, 1)

            def x_variance(f, k):
                if not k.has(f):
                    return
                dve.wait_ge(ln1_aggr, k.n(f))
                dve.tensor_scalar(ve1[f % 2][:, :], mv1[f % 2][:, :, 1], EPS, None, ALU.add)
                dve.tensor_scalar(nm1[f % 2][:, :], mv1[f % 2][:, :, 0], -1.0, None, ALU.mult).then_inc(ln1_var, 1)

            def first_moments(f):
                x_stats(f, first)
                dve.wait_ge(ln1_stats, first.n(f))
                x_aggregate(f, first)
                x_variance(f, first)

            dve.memset(ones[:, :].bitcast(F32), 1.0).then_inc(table_in, 1)
            dve.memset(c2[0][:, :, :, 0], 0.0)
            dve.memset(dmask[:, :, :, 0], 0.0)
            dve.memset(cp[:, :].bitcast(F32), 0.0).then_inc(tri_ready, 1)
            dve.memset(u_lo[0][:, :, :], 0.0).then_inc(ul_ready[0], 1)
            dve.memset(u_hi[0][:, :, :], 0.0).then_inc(uh_ready[0], 1)
            dve.wait_ge(load["decay"], 16 * KC)
            for kc in range(KC):
                last = dve.tensor_copy(dmask[:, kc, :, 1:STEPS + 1],
                                       dec_cols[:, kc:kc + 1].unsqueeze(2).to_broadcast([P, B, STEPS]))
            last.then_inc(setup_dve, 1)
            dve.wait_ge(setup_dve, 1)
            first_moments(0)
            scanned(0, first)
            dve.wait_ge(load["biases"], BIASES)
            dve.tensor_copy(bi_wide[:, :, :], cols[:, 0:KC].unsqueeze(2).to_broadcast([P, KC, P])).then_inc(setup_dve, 1)
            dve.wait_ge(setup_act, 3)
            low(flat(split["inp"][1][:, :, :]), bank[3][:, :], flat(split["inp"][0][:, :, :]), setup_dve)
            retained(0, first)
            dve.wait_ge(setup_act, 5)
            low(flat(split["gate"][1][:, :, :]), flat(rec[1][:, :, :]), flat(split["gate"][0][:, :, :]), setup_dve)
            ret_low(0, first)
            dve.wait_ge(setup_act, 6)
            low(flat(split["bm"][1][:, :, :]), flat(rec[0][:, :, :]), flat(split["bm"][0][:, :, :]), setup_dve)
            first_moments(1)
            dve.wait_ge(setup_act, 7)
            dve.wait_ge(tri_ready, 1)
            dve.scalar_tensor_tensor(out=half_gate_bias[:, :], in0=bank[4][:, 256:258], scalar=1.0, in1=cols[:, 2:4],
                                     op0=ALU.mult, op1=ALU.add).then_inc(setup_dve, 1)
            dve.tensor_copy(cp[0:1, :], cp_hi[0:1, :].bitcast(F32))
            dve.tensor_tensor(cp[32:33, :], bank[4][32:33, 0:D], cp_hi[32:33, :].bitcast(F32), ALU.subtract).then_inc(setup_dve, 1)
            dve.wait_ge(setup_dve, 6)
            dve.tensor_scalar(half_gate_bias[:, :], half_gate_bias[:, :], 0.5, None, ALU.mult).then_inc(setup_dve, 1)
            dve.wait_ge(setup_act, 9)
            dve.scalar_tensor_tensor(out=flat(split["a"][1][:, :, :]), in0=bank[5][:, :], scalar=-0.5 * PSCALE,
                                     in1=flat(split["a"][0][:, :, :]).bitcast(F32),
                                     op0=ALU.mult, op1=ALU.subtract).then_inc(setup_dve, 1)
            dve.scalar_tensor_tensor(out=flat(a16[1][:, :, :]), in0=bank[5][:, :], scalar=0.5 * PSCALE,
                                     in1=flat(a16[0][:, :, :]), op0=ALU.mult, op1=ALU.subtract).then_inc(setup_dve, 1)
            blend(0, first)
            scanned(1, first)
            cn_low(0)
            retained(1, first)
            ret_low(1, first)
            gated_state(0, 0, first)
            dve.wait_ge(setup_act, 10)
            dve.tensor_scalar(tgbo[:, :], bo_all[:, :], tgx[:, 0:1], None, ALU.mult).then_inc(setup_dve, 1)
            gated_state(0, 1, first)
            first_moments(2)
            gated_state(0, 2, first)
            blend(1, first)
            gated_state(0, 3, first)
            cn_low(1)
            gated_state(0, 4, first)
            for e in range(E):
                dve.memset(tri[:, e, e:E], 0.0)
                if e > 0:
                    last = dve.memset(tri[:, e, 0:e], 1.0)
            last.then_inc(tri_ready, 1)
            gated_state(0, 5, first)
            dve.wait_ge(setup_act, 11)
            dve.scalar_tensor_tensor(out=flat(split["wo"][1][:, :, :]), in0=bank[4][:, :], scalar=tgx[:, 0:1],
                                     in1=flat(split["wo"][0][:, :, :]).bitcast(F32),
                                     op0=ALU.mult, op1=ALU.subtract).then_inc(setup_dve, 1)
            gated_state(0, 6, first)
            dve.wait_ge(ffn2_hi, 1)
            dve.scalar_tensor_tensor(out=flat(split["so"][1][:, :, :]), in0=flat(raw_sq["so"][:, :, :]), scalar=tgf[:, 0:1],
                                     in1=flat(split["so"][0][:, :, :]).bitcast(F32),
                                     op0=ALU.mult, op1=ALU.subtract).then_inc(so_split, 1)
            gated_state(0, 7, first)

            def iteration(i, k):
                a, c, d, e, f = i + 1, i - 1, i - 2, i - 3, i + 2
                gated_state(i, 0, k)
                if k.has(d):
                    dve.wait_ge(sil_w_ready, k.n(d))
                    if k.has(d - 1):
                        dve.wait_ge(hid_hi, k.n(d - 1))
                        dve.wait_ge(hid_lo, k.n(d - 1))
                    dve.tensor_tensor(flat(hid[:, :, :]), bank[B_W1B][:, :], flat(sil_w[:, :, :]),
                                      ALU.mult).then_inc(hid_ready, 1)
                gated_state(i, 1, k)
                scanned(a, k)
                retained(a, k)
                if k.has(d):
                    dve.wait_ge(lg_ready, k.n(d))
                    dve.tensor_reduce(lmax[:, :], lg[:, :, :], AX_X, ALU.max).then_inc(lmax_ready, 1)
                if k.has(d):
                    if k.has(d - 1):
                        dve.wait_ge(beat_ready, k.n(d - 1))
                    mine = lg[:, :, :].unsqueeze(3).to_broadcast([P, HALVES, E, E])
                    others = lg[:, :, :].unsqueeze(2).to_broadcast([P, HALVES, E, E])
                    dve.tensor_tensor(more[:, :, :, :], others, mine, ALU.is_gt)
                    dve.tensor_tensor(same[:, :, :, :], others, mine, ALU.is_equal).then_inc(same_ready, 1)
                add_pair(5, e, k)
                if k.has(d):
                    dve.wait_ge(lmax_ready, k.n(d))
                    dve.tensor_tensor(ld[:, :, :], lg[:, :, :], lmax[:, :].unsqueeze(2).to_broadcast([P, HALVES, E]),
                                      ALU.subtract).then_inc(ld_ready, 1)
                gated_state(i, 2, k)
                if k.has(c):
                    dve.wait_ge(wo_done, k.n(c))
                    dve.wait_ge(xr_ready, k.n(c))
                    dve.tensor_tensor(x1[c % 2][:, :, :].rearrange("p s d -> p (s d)"), bank[B_WO][:, :],
                                      xr_sb[c % 2][:, :], ALU.add).then_inc(x1_ready, 1)
                ret_low(a, k)
                if k.has(c):
                    dve.wait_ge(x1_ready, k.n(c))
                    for s in range(HALVES):
                        last = dve.bn_stats(st2[c % 2][:, s, :], x1[c % 2][:, s, :])
                    last.then_inc(ln2_stats, 1)
                    dve.wait_ge(ln2_stats, k.n(c))
                if k.has(d):
                    dve.wait_ge(lt_ready, k.n(d))
                    dve.tensor_scalar(num[:, :, :], lt[:, :, :], 1.0, None, ALU.add)
                    dve.tensor_scalar(den[:, :, :], lt[:, :, :], -1.0, 1.0, ALU.mult, ALU.add).then_inc(numden, 1)
                if k.has(c):
                    for s in range(HALVES):
                        last = dve.bn_aggr(mv2[c % 2][:, s, :], st2[c % 2][:, s, :])
                    last.then_inc(ln2_aggr, 1)
                if k.has(d):
                    dve.wait_ge(numden, k.n(d))
                    dve.reciprocal(rden[:, :, :], den[:, :, :]).then_inc(rden_ready, 1)
                if k.has(c):
                    dve.wait_ge(ln2_aggr, k.n(c))
                    dve.tensor_scalar(ve2[c % 2][:, :], mv2[c % 2][:, :, 1], EPS, None, ALU.add)
                    dve.tensor_scalar(nm2[c % 2][:, :], mv2[c % 2][:, :, 0], -1.0, None, ALU.mult).then_inc(ln2_var, 1)
                add_pair(6, e, k)
                gated_state(i, 3, k)
                if k.has(d):
                    if k.has(d - 2):
                        dve.wait_ge(out_done[d % 2], k.dma(d - 2))
                    dve.wait_ge(so_done, k.n(d))
                    dve.tensor_tensor(acc[d % 2][:, :, :].rearrange("p s d -> p (s d)"), bank[B_SO][:, :],
                                      x1[d % 2][:, :, :].rearrange("p s d -> p (s d)"), ALU.add).then_inc(acc_ready, 1)
                    dve.wait_ge(rden_ready, k.n(d))
                    dve.tensor_tensor(ex[:, :, :], num[:, :, :], rden[:, :, :], ALU.mult).then_inc(ex_ready, 1)
                add_pair(7, e, k)
                if k.has(d):
                    dve.wait_ge(ex_ready, k.n(d))
                    dve.tensor_reduce(esum[:, :], ex[:, :, :], AX_X, ALU.add).then_inc(esum_ready, 1)
                    dve.wait_ge(rank_ready, k.n(d))
                    dve.scalar_tensor_tensor(out=flat(picked[:, :, :]), in0=flat(rank[:, :, :]), scalar=2.0,
                                             in1=flat(ex[:, :, :]), op0=ALU.is_lt, op1=ALU.mult).then_inc(picked_ready, 1)
                    dve.wait_ge(esum_ready, k.n(d))
                    dve.reciprocal(rsum[:, :], esum[:, :]).then_inc(rsum_ready, 1)
                    dve.wait_ge(rsum_ready, k.n(d))
                    dve.tensor_scalar(rsg[:, :], rsum[:, :], tgf[:, 0:1], None, ALU.mult).then_inc(rsg_ready, 1)
                gated_state(i, 4, k)
                if k.has(d):
                    dve.wait_ge(rsg_ready, k.n(d))
                    dve.wait_ge(picked_ready, k.n(d))
                    dve.tensor_tensor(wts[d % 2][:, :, :], picked[:, :, :],
                                      rsg[:, :].unsqueeze(2).to_broadcast([P, HALVES, E]), ALU.mult).then_inc(wts_ready, 1)
                x_stats(f, k)
                if k.has(d):
                    dve.wait_ge(wts_ready, k.n(d))
                add_pair(0, d, k)
                gated_state(i, 5, k)
                if k.has(f):
                    dve.wait_ge(ln1_stats, k.n(f))
                blend(a, k)
                x_aggregate(f, k)
                if k.has(c):
                    dve.wait_ge(xn2_hi, k.n(c))
                    if k.has(c - 1):
                        dve.wait_ge(w1_done, k.n(c - 1))
                    low(flat(xn2_s[c % 2][1][:, :, :]), bank[B_T2][:, :], flat(xn2_s[c % 2][0][:, :, :]), xn2_lo)
                x_variance(f, k)
                add_pair(1, d, k)
                gated_state(i, 6, k)
                add_pair(2, d, k)
                add_pair(3, d, k)
                gated_state(i, 7, k)
                if k.has(c):
                    dve.wait_ge(lg_done, k.n(c))
                    dve.tensor_tensor(lg[:, :, :], bank[B_LG][:, 0:HALVES * E].rearrange("p (s e) -> p s e", s=HALVES),
                                      gb_all[:, :].unsqueeze(1).to_broadcast([P, HALVES, E]), ALU.add).then_inc(lg_ready, 1)
                add_pair(4, d, k)
                if k.has(c):
                    dve.wait_ge(sil_s_ready, k.n(c))
                    if k.has(c - 1):
                        dve.wait_ge(hs_hi, k.n(c - 1))
                        dve.wait_ge(hs_lo, k.n(c - 1))
                    dve.tensor_tensor(flat(hs[:, :, :]), bank[B_SHB][:, :], flat(sil_s[:, :, :]),
                                      ALU.mult).then_inc(hs_ready, 1)

            run(dve, iteration)

        @block.gpsimd
        def _(pool):
            pool.memset(minus_half[:, :], -0.5)
            pool.memset(ident[:, :], 0.0).then_inc(zeros_pool := sem("zeros_pool"), 1)
            pool.wait_ge(zeros_pool, 1)
            pool.affine_select(out=ident[:, :], in_=ident[:, :], compare_op=ALU.not_equal, fill=1.0, base=0,
                               pattern=[[-1, P]], channel_multiplier=1).then_inc(consts, 1)

            def low(n, whole, hi, signal):
                pool.tensor_tensor(n, whole, hi.bitcast(F32), ALU.subtract).then_inc(signal, 1)

            def x_rstd(f, k):
                if not k.has(f):
                    return
                pool.wait_ge(ln1_var, k.n(f))
                pool.tensor_tensor(rs1[f % 2][:, :], ve1[f % 2][:, :], minus_half[:, :], ALU.pow).then_inc(ln1_rstd, 1)
                pool.wait_ge(ln1_rstd, k.n(f))
                pool.tensor_tensor(nr1[f % 2][:, :], nm1[f % 2][:, :], rs1[f % 2][:, :], ALU.mult).then_inc(ln1_shift, 1)

            def residual(i, k):
                if not k.has(i):
                    return
                pool.wait_ge(xr_in[i % 2], k.dma(i))
                for s in range(HALVES):
                    last = pool.tensor_tensor(xr_sb[i % 2][:, s * D:(s + 1) * D], xr_sb[i % 2][:, s * D:(s + 1) * D],
                                              tgbo[:, :], ALU.add)
                last.then_inc(xr_ready, 1)

            def w2_low(e):
                pool.wait_ge(ffn2_hi, e + 2)
                low(split["w2"][1][:, :, e, :], raw_w2[e][:, :, :], split["w2"][0][:, :, e, :], w2_lo)

            x_rstd(0, first)
            x_rstd(1, first)
            pool.wait_ge(wide_hi, 1)
            low(flat(split["sh"][1][:, :, :]), flat(raw_wide["sh"][:, :, :]), flat(split["sh"][0][:, :, :]), wide_lo)
            x_rstd(2, first)
            pool.wait_ge(wide_hi, 2)
            low(split["wgate"][1][:, :, :], raw_wgate[:, :, :], split["wgate"][0][:, :, :], wide_lo)
            pool.wait_ge(setup_dve, 11)
            residual(0, first)
            pool.wait_ge(wide_hi, 3)
            low(flat(split["w1"][1][:, :, :]), flat(raw_wide["w1"][:, :, :]), flat(split["w1"][0][:, :, :]), wide_lo)
            w2_low(0)

            def iteration(i, k):
                a, c, d, f = i + 1, i - 1, i - 2, i + 2
                if k.has(c):
                    pool.wait_ge(st_hi, k.n(c))
                    if k.has(c - 1):
                        pool.wait_ge(wo_done, k.n(c - 1))
                    low(flat(st_s[c % 2][1][:, :, :]), flat(state[c % 2][:, :, :]), flat(st_s[c % 2][0][:, :, :]), st_lo)
                if k.has(d):
                    pool.wait_ge(hs_hi, k.n(d))
                    if k.has(d - 1):
                        pool.wait_ge(so_done, k.n(d - 1))
                    low(flat(hs_s[1][:, :, :]), flat(hs[:, :, :]), flat(hs_s[0][:, :, :]), hs_lo)
                    pool.wait_ge(hid_hi, k.n(d))
                    if k.has(d - 2):
                        pool.wait_ge(pair_done[E - 1], k.n(d - 2))
                    low(flat(hid_s[d % 2][1][:, :, :]), flat(hid[:, :, :]), flat(hid_s[d % 2][0][:, :, :]), hid_lo)
                if k.has(d):
                    if k.static and d == 0:
                        pool.wait_ge(tri_ready, 2)
                    pool.wait_ge(same_ready, k.n(d))
                    pool.tensor_tensor(same_l[:, :, :, :].rearrange("p s e f -> p s (e f)"),
                                       same[:, :, :, :].rearrange("p s e f -> p s (e f)"),
                                       tri[:, :, :].rearrange("p e f -> p (e f)").unsqueeze(1).to_broadcast([P, HALVES, E * E]),
                                       ALU.mult).then_inc(samel_ready, 1)
                    pool.wait_ge(samel_ready, k.n(d))
                    pool.tensor_tensor(beat[:, :, :, :].rearrange("p s e f -> p (s e f)"),
                                       more[:, :, :, :].rearrange("p s e f -> p (s e f)"),
                                       same_l[:, :, :, :].rearrange("p s e f -> p (s e f)"), ALU.add).then_inc(beat_ready, 1)
                    if k.has(d - 1):
                        pool.wait_ge(picked_ready, k.n(d - 1))
                    pool.wait_ge(beat_ready, k.n(d))
                    b8 = beat[:, :, :, :].rearrange("p s e f -> p (s e) f")
                    pool.tensor_tensor(b4[:, :, :], b8[:, :, 0:4], b8[:, :, 4:8], ALU.add).then_inc(b4_ready, 1)
                    pool.wait_ge(b4_ready, k.n(d))
                    pool.tensor_tensor(b2[:, :, :], b4[:, :, 0:2], b4[:, :, 2:4], ALU.add).then_inc(b2_ready, 1)
                    pool.wait_ge(b2_ready, k.n(d))
                    pool.tensor_tensor(flat(rank[:, :, :]), b2[:, :, 0], b2[:, :, 1], ALU.add).then_inc(rank_ready, 1)
                if k.static and i == 1:
                    w2_low(1)
                if k.has(c):
                    pool.wait_ge(ln2_var, k.n(c))
                    pool.tensor_tensor(rs2[c % 2][:, :], ve2[c % 2][:, :], minus_half[:, :], ALU.pow).then_inc(ln2_rstd, 1)
                    pool.wait_ge(ln2_rstd, k.n(c))
                    pool.tensor_tensor(nr2[c % 2][:, :], nm2[c % 2][:, :], rs2[c % 2][:, :], ALU.mult).then_inc(ln2_shift, 1)
                if k.static and i == 1:
                    for expert in range(2, 5):
                        w2_low(expert)
                if k.has(a):
                    pool.wait_ge(cn_hi, k.n(a))
                    if k.has(a - 1):
                        pool.wait_ge(ac_done, k.n(a - 1))
                    low(flat(cn_s[a % 2][1][:, :, :]), flat(cn[a % 2][:, :, :]), flat(cn_s[a % 2][0][:, :, :]), cn_lo)
                x_rstd(f, k)
                residual(i, k)
                if k.static and i == 1:
                    for expert in range(5, E):
                        w2_low(expert)

            run(pool, iteration)


_INS = ["x", "ctx_1024", "g_xattn", "g_ffn", "L0_xattn_Wi", "L0_xattn_bi", "L0_xattn_Wg", "L0_xattn_bg", "L0_xattn_A",
        "L0_xattn_Bm", "L0_xattn_Wo", "L0_xattn_bo", "L0_xattn_decay", "L0_ffn_w_shared_in", "L0_ffn_w_shared_out",
        "L0_ffn_w1_shared", "L0_ffn_w2", "L0_ffn_w_gate", "L0_ffn_gate_bias"]
_OUTS = [((B, S, D), "float32")]


def kernel(**inputs):
    import numpy as _np
    import concourse.bacc as _bacc
    from concourse import mybir as _mybir
    from concourse.bass_utils import run_bass_kernel_spmd as _run

    nc = _bacc.Bacc("TRN2", target_bir_lowering=False, num_devices=1)
    arrays, args = {}, []
    for name in _INS:
        a = _np.ascontiguousarray(inputs[name])
        arrays[f"in_{name}_dram"] = a
        args.append(nc.dram_tensor(f"in_{name}_dram", a.shape, _mybir.dt.from_np(a.dtype), kind="ExternalInput").ap())
    for i, (shape, dtype) in enumerate(_OUTS):
        dt = _mybir.dt.from_np(_np.dtype(dtype))
        args.append(nc.dram_tensor(f"out_{i}_dram", shape, dt, kind="ExternalOutput").ap())
    gated_layer(nc, *args)
    r = _run(nc, [arrays], core_ids=[0])
    return r.results[0]["out_0_dram"]
```

```python
from contextlib import ExitStack

import concourse.bass as bass
from concourse import mybir

F32 = mybir.dt.float32
F32R = mybir.dt.float32r
F16 = mybir.dt.float16
ALU = mybir.AluOpType
ACT = mybir.ActivationFunctionType
AX_X = mybir.AxisListType.X

P = 128
B, S, D = 32, 128, 256
KC = D // P
BLOCKS = P // 32
HEADS = 16
E = 8
STEPS = 8
HALVES = 2
J = STEPS // HALVES
TOK = STEPS * B
TILES = S // STEPS
EPS = 1e-5
WARMUP = 6
PSCALE = 256.0


def gated_layer(nc, x, ctx_in, g_xattn, g_ffn, Wi, bi, Wg, bg, A, Bm, Wo, bo, decay,
                w_shared_in, w_shared_out, w1_shared, w2, w_gate, gate_bias, out):
    with ExitStack() as stack:
        def sb(name, shape, dt=F32):
            return stack.enter_context(nc.sbuf_tensor(name, shape, dt))

        def two(name, shape, dt=F32):
            return [sb(f"{name}{n}", shape, dt) for n in range(2)]

        def one(name, shape, dt=F32):
            return [sb(name, shape, dt)] * 2

        def sem(name):
            return stack.enter_context(nc.semaphore(name))

        x_tiles = x.rearrange("b (u j s) d -> u b j (s d)", j=J, s=HALVES)
        c_tiles = ctx_in.rearrange("b (u t) (k i r) -> u i b (t k) r", t=STEPS, k=KC, i=BLOCKS)
        o_tiles = out.rearrange("b (u j s) d -> u b j (s d)", j=J, s=HALVES)

        raw_sq = {n: sb(f"raw_{n}", [P, KC, D]) for n in ("Wi", "Wg", "Bm", "A", "Wo", "so")}
        raw_wide = {n: sb(f"raw_{n}", [P, KC, 2 * D]) for n in ("sh", "w1")}
        raw_wgate = sb("raw_wgate", [P, KC, E])
        cols = sb("cols", [P, 4])
        WgT = sb("WgT", [P, KC, D])
        BmT = sb("BmT", [P, KC, D])
        split = {}
        for n in ("inp", "gate", "bm", "a", "wo", "so"):
            split[n] = (sb(f"{n}_hi", [P, KC, D], F32R), sb(f"{n}_lo", [P, KC, D], F32R))
        for n in ("sh", "w1"):
            split[n] = (sb(f"{n}_hi", [P, KC, 2 * D], F32R), sb(f"{n}_lo", [P, KC, 2 * D], F32R))
        split["w2"] = (sb("w2_hi", [P, KC, E, D], F32R), sb("w2_lo", [P, KC, E, D], F32R))
        wgate_s = sb("wgate_s", [P, KC, BLOCKS, 32], F32R)
        raw_w2 = [raw_sq[n] for n in ("Wi", "Wg", "Bm", "A")] + [WgT, BmT, sb("raw_w2", [P, KC, D]), raw_sq["Wo"]]
        a16 = (sb("a16_hi", [P, KC, D], F16), sb("a16_lo", [P, KC, D], F16))
        bm_bias = sb("bm_bias", [P, KC, TOK])
        ident = sb("ident", [P, P])
        minus_half = sb("minus_half", [P, HALVES])
        half_gate_bias = sb("half_gate_bias", [P, KC])
        gx = sb("gx", [P, 1])
        gf = sb("gf", [P, 1])
        tgx = sb("tgx", [P, 1])
        tgf = sb("tgf", [P, 1])
        bo_all = sb("bo_all", [P, D])
        tgbo = sb("tgbo", [P, D])
        gb_all = sb("gb_all", [P, E])
        dec_cols = sb("dec_cols", [P, KC])
        dmask = sb("dmask", [P, KC, B, STEPS + 1])
        tri = sb("tri", [P, E, E])

        x_sb = two("x_sb", [P, HALVES * D])
        c_sb = two("c_sb", [P, STEPS * KC, 32])
        c_turned = sb("c_turned", [P, STEPS * KC, B])
        xr_sb = two("xr_sb", [P, HALVES * D])
        xn1 = one("xn1", [P, HALVES, D])
        c2 = one("c2", [P, KC, B, STEPS + 1])
        r = two("r", [P, KC, B, STEPS + 1])
        ret = one("ret", [P, KC, TOK])
        ret_s = [(sb("ret_hi", [P, KC, TOK], F32R), sb("ret_lo", [P, KC, TOK], F32R))] * 2
        gt = two("gt", [P, KC, TOK])
        inp = one("inp_sb", [P, KC, TOK])
        cn = one("cn", [P, KC, TOK])
        cn_s = [(sb("cn_hi", [P, KC, TOK], F32R), sb("cn_lo", [P, KC, TOK], F32R))] * 2
        state = two("state", [P, KC, TOK])
        st_s = [(sb("st_hi", [P, KC, TOK], F32R), sb("st_lo", [P, KC, TOK], F32R))] * 2
        u_hi = two("u_hi", [P, KC, B], F16)
        u_lo = two("u_lo", [P, KC, B], F16)
        u_full = two("u_full", [P, KC, B])
        x1 = two("x1", [P, HALVES, D])
        xn2 = one("xn2", [P, HALVES, D])
        xn2_s = [(sb("xn2_hi", [P, KC, TOK], F32R), sb("xn2_lo", [P, KC, TOK], F32R))] * 2
        sil_s = sb("sil_s", [P, KC, TOK])
        sil_w = sb("sil_w", [P, KC, TOK])
        hs = sb("hs", [P, KC, TOK])
        hid = sb("hid", [P, KC, TOK])
        hs_s = (sb("hs_hi", [P, KC, TOK], F32R), sb("hs_lo", [P, KC, TOK], F32R))
        hid_s = [(sb(f"hid_hi{n}", [P, KC, TOK], F32R), sb(f"hid_lo{n}", [P, KC, TOK], F32R)) for n in range(2)]
        acc = two("acc", [P, HALVES, D])
        st1 = two("st1", [P, HALVES, 6])
        mv1 = two("mv1", [P, HALVES, 2])
        ve1 = two("ve1", [P, HALVES])
        nm1 = two("nm1", [P, HALVES])
        rs1 = two("rs1", [P, HALVES])
        nr1 = two("nr1", [P, HALVES])
        st2 = two("st2", [P, HALVES, 6])
        mv2 = two("mv2", [P, HALVES, 2])
        ve2 = two("ve2", [P, HALVES])
        nm2 = two("nm2", [P, HALVES])
        rs2 = two("rs2", [P, HALVES])
        nr2 = two("nr2", [P, HALVES])
        lg_t = sb("lg_t", [P, HALVES, 32])
        lg_b = sb("lg_b", [P, HALVES, E])
        lg = sb("lg", [P, HALVES, E])
        lmax = sb("lmax", [P, HALVES])
        ld = sb("ld", [P, HALVES, E])
        lt = sb("lt", [P, HALVES, E])
        num = sb("num", [P, HALVES, E])
        den = sb("den", [P, HALVES, E])
        rden = sb("rden", [P, HALVES, E])
        ex = sb("ex", [P, HALVES, E])
        esum = sb("esum", [P, HALVES])
        rsum = sb("rsum", [P, HALVES])
        rsg = sb("rsg", [P, HALVES])
        more = sb("more", [P, HALVES, E, E])
        same = sb("same", [P, HALVES, E, E])
        same_l = sb("same_l", [P, HALVES, E, E])
        beat = sb("beat", [P, HALVES, E, E])
        b4 = sb("b4", [P, HALVES * E, 4])
        b2 = sb("b2", [P, HALVES * E, 2])
        rank = sb("rank", [P, HALVES, E])
        picked = sb("picked", [P, HALVES, E])
        wts = two("wts", [P, HALVES, E])

        rec = [stack.enter_context(nc.psum_tensor(f"rec{n}", [P, KC, TOK], F32)) for n in range(2)]
        bank = [stack.enter_context(nc.psum_tensor(f"bank{n}", [P, 512], F32)) for n in range(6)]

        load = {n: sem(f"load_{n}") for n in
                ("Wi", "Wg", "Bm", "A", "Wo", "so", "sh", "w1", "w2", "wgate", "decay", "biases", "small")}
        x_in = [sem("x_in0"), sem("x_in1")]
        c_in = [sem("c_in0"), sem("c_in1")]
        xr_in = [sem("xr_in0"), sem("xr_in1")]
        out_done = [sem("out_done0"), sem("out_done1")]
        consts = sem("consts")
        setup_pe = sem("setup_pe")
        setup_dve = sem("setup_dve")
        setup_act = sem("setup_act")
        wide_hi = sem("wide_hi")
        wide_lo = sem("wide_lo")
        ffn2_hi = sem("ffn2_hi")
        so_split = sem("so_split")
        w2_lo = sem("w2_lo")
        ln1_stats, ln1_aggr, ln1_var, ln1_rstd, ln1_shift, xn1_ready = (sem(n) for n in ("ln1_stats", "ln1_aggr", "ln1_var", "ln1_rstd", "ln1_shift", "xn1_ready"))
        turned, tx_done = sem("turned"), sem("tx_done")
        c2_ready, r_ready, ret_ready, ret_hi, ret_lo = (sem(n) for n in ("c2_ready", "r_ready", "ret_ready", "ret_hi_ready", "ret_lo_ready"))
        inp_done, gate_done = sem("inp_done"), sem("gate_done")
        gt_ready, inp_ready, cn_ready, cn_hi, cn_lo = (sem(n) for n in ("gt_ready", "inp_ready", "cn_ready", "cn_hi_ready", "cn_lo_ready"))
        bias_in = sem("bias_in")
        bm_done = sem("bm_done")
        ac_done = sem("ac_done")
        uh_ready = [sem(f"uh_ready{t}") for t in range(STEPS)]
        uf_ready = sem("uf_ready")
        ul_ready = [sem(f"ul_ready{t}") for t in range(STEPS)]
        sum_done = [sem(f"sum_done{t}") for t in range(STEPS)]
        st_ready = [sem(f"st_ready{t}") for t in range(STEPS)]
        st_hi, st_lo = sem("st_hi_ready"), sem("st_lo_ready")
        xr_ready = sem("xr_ready")
        wo_done, x1_ready, ln2_stats, ln2_aggr, ln2_var, ln2_rstd, ln2_shift, xn2_ready = (
            sem(n) for n in ("wo_done", "x1_ready", "ln2_stats", "ln2_aggr", "ln2_var", "ln2_rstd", "ln2_shift", "xn2_ready"))
        t2_done, xn2_hi, xn2_lo = sem("t2_done"), sem("xn2_hi_ready"), sem("xn2_lo_ready")
        sh_done, w1_done = sem("sh_done"), sem("w1_done")
        sil_s_ready, sil_w_ready, hs_ready, hid_ready = (sem(n) for n in ("sil_s_ready", "sil_w_ready", "hs_ready", "hid_ready"))
        hs_hi, hs_lo, hid_hi, hid_lo = (sem(n) for n in ("hs_hi_ready", "hs_lo_ready", "hid_hi_ready", "hid_lo_ready"))
        lg_done, lg_t_ready, lg_b_ready, lg_ready = (
            sem(n) for n in ("lg_done", "lg_t_ready", "lg_b_ready", "lg_ready"))
        lmax_ready, ld_ready, lt_ready = sem("lmax_ready"), sem("ld_ready"), sem("lt_ready")
        numden, rden_ready, ex_ready, esum_ready, rsum_ready, rsg_ready = (
            sem(n) for n in ("numden_ready", "rden_ready", "ex_ready", "esum_ready", "rsum_ready", "rsg_ready"))
        same_ready, samel_ready, beat_ready, rank_ready, picked_ready, wts_ready = (
            sem(n) for n in ("same_ready", "samel_ready", "beat_ready", "rank_ready", "picked_ready", "wts_ready"))
        so_done, acc_ready = sem("so_done"), sem("acc_ready")
        b4_ready, b2_ready = sem("b4_ready"), sem("b2_ready")
        pair_done = [sem(f"pair_done{k}") for k in range(E)]
        pair_half = sem("pair_half")
        pair_used = [sem(f"pair_used{k}") for k in range(E)]

        BIASES = 16 * 2
        SMALL = 16 * 4

        B_TX, B_WO, B_SO, B_INP, B_GATE, B_T2, B_LG = 1, 4, 0, 2, 3, 0, 3
        B_SHA, B_SHB, B_W1A, B_W1B = 0, 1, 4, 5
        B_PAIR = [4, 1, 2, 4, 5, 3, 5, 1]

        def halves(ap):
            return ap.rearrange("p (s b j) -> p s b j", s=HALVES, b=B)

        def by_time(ap):
            return ap.rearrange("p b (j s) -> p s b j", s=HALVES)

        def step_of(t3, t):
            return t3[:, :, :].rearrange("p c (s b j) -> p c s b j", s=HALVES, b=B)[:, :, t % HALVES, :, t // HALVES]

        def flat(t3):
            return t3.rearrange("p a b -> p (a b)")

        class Static:
            static = True

            def n(self, m):
                return m + 1

            def steps(self, m, t):
                return STEPS * m + t

            def dma(self, m):
                return 16 * (m // 2 + 1)

            def pairs(self, m, n):
                return E * m + n + 1

            def context(self, m):
                return 16 * BLOCKS * (m // 2 + 1)

            def has(self, m):
                return 0 <= m < TILES

            def tile(self, m):
                return m

        class Looped:
            static = False

            def __init__(self, eng, reg):
                self.eng, self.reg, self.known = eng, reg, {}

            def kept(self, key, value):
                if key not in self.known:
                    self.known[key] = self.eng.snap(value)
                return self.known[key]

            def n(self, m):
                return self.kept(("n", m), self.reg * 2 + (m + 1))

            def steps(self, m, t):
                return self.kept(("steps", m, t), self.reg * (2 * STEPS) + (STEPS * m + t))

            def dma(self, m):
                return self.kept(("dma", m // 2), self.reg * 16 + 16 * (m // 2 + 1))

            def pairs(self, m, n):
                return self.kept(("pairs", m, n), self.reg * (2 * E) + (E * m + n + 1))

            def context(self, m):
                return self.kept(("context", m // 2), self.reg * (16 * BLOCKS) + 16 * BLOCKS * (m // 2 + 1))

            def has(self, m):
                return True

            def tile(self, m):
                return self.reg * 2 + m

        FIRST_FULL, LAST_FULL = 3, TILES - 4
        TAIL = range(LAST_FULL + 1, TILES + 3)

        def run(eng, iteration):
            for i in range(1, FIRST_FULL):
                iteration(i, Static())
            with eng.Fori(FIRST_FULL // 2, LAST_FULL // 2) as reg:
                k = Looped(eng, reg)
                iteration(1, k)
                iteration(2, k)
            for i in TAIL:
                iteration(i, Static())

        first = Static()

        block = stack.enter_context(nc.Block())

        @block.sync
        def _(sp):
            def part(t2):
                return t2[:, :].rearrange("(b j) e -> b j e", j=J)

            def load_x(m, k):
                sp.dma_start(x_sb[m % 2][:, :], x_tiles[k.tile(m)]).then_inc(x_in[m % 2], 16)

            def load_xr(i, k):
                sp.dma_start(xr_sb[i % 2][:, :], x_tiles[k.tile(i)]).then_inc(xr_in[i % 2], 16)

            def load_c(m, k):
                for i in range(BLOCKS):
                    sp.dma_start(c_sb[m % 2][32 * i:32 * (i + 1), :, :], c_tiles[k.tile(m), i]).then_inc(c_in[m % 2], 16)

            def square(n, w):
                sp.dma_start(raw_sq[n][:, :, :], w.rearrange("(k p) i -> p k i", p=P)).then_inc(load[n], 16)

            load_x(0, first)
            square("Wi", Wi)
            square("Wg", Wg)
            load_c(0, first)
            with nc.allow_non_contiguous_dma(reason="small vectors"):
                square("Bm", Bm)
                load_x(1, first)
                square("A", A)
                load_c(1, first)
                sp.dma_start(gx[:, :], g_xattn.partition_broadcast(P)).then_inc(load["small"], 16)
                sp.dma_start(gf[:, :], g_ffn.partition_broadcast(P)).then_inc(load["small"], 16)
                sp.dma_start(bo_all[:, :], bo.partition_broadcast(P)).then_inc(load["small"], 16)
                sp.dma_start(gb_all[:, :], gate_bias.partition_broadcast(P)).then_inc(load["small"], 16)
                square("Wo", Wo)
                sp.dma_start(raw_wide["sh"][:, :, :], w_shared_in.rearrange("(k p) h -> p k h", p=P)).then_inc(load["sh"], 16)
                sp.dma_start(raw_wgate[:, :, :], w_gate.rearrange("(k p) e -> p k e", p=P)).then_inc(load["wgate"], 16)
                sp.dma_start(raw_wide["w1"][:, :, :], w1_shared.rearrange("(k p) h -> p k h", p=P)).then_inc(load["w1"], 16)
                square("so", w_shared_out)
            load_xr(0, first)
            sp.wait_ge(turned, 1)
            load_c(2, first)
            sp.wait_ge(xn1_ready, 1)
            load_x(2, first)
            sp.wait_ge(setup_pe, 7)
            for e in range(E):
                if e == E - 1:
                    sp.wait_ge(setup_pe, 8)
                sp.dma_start(raw_w2[e][:, :, :], w2[e].rearrange("(k p) c -> p k c", p=P)).then_inc(load["w2"], 16)
            sp.wait_ge(xn1_ready, 2)
            load_x(3, first)

            def iteration(i, k):
                m = i + 3
                if k.has(m):
                    sp.wait_ge(xn1_ready, k.n(m - 2))
                    load_x(m, k)
                m = i + 2
                if k.has(m):
                    sp.wait_ge(turned, k.n(m - 2))
                    load_c(m, k)
                if k.has(i):
                    if k.has(i - 2):
                        sp.wait_ge(x1_ready, k.n(i - 2))
                    load_xr(i, k)
                if k.has(i - 3):
                    sp.wait_ge(pair_used[E - 1], k.n(i - 3))
                    sp.dma_start(o_tiles[k.tile(i - 3)], acc[(i - 3) % 2][:, :, :].rearrange("p s d -> p (s d)")).then_inc(out_done[(i - 3) % 2], 16)

            run(sp, iteration)
            for n in range(2):
                sp.wait_ge(out_done[n], 16 * (TILES // 2))

        @block.tensor
        def _(pe):
            def transposed(dst, src):
                for kr in range(KC):
                    for kc in range(KC):
                        last = pe.transpose(dst[:, kc * D + kr * P:kc * D + (kr + 1) * P],
                                            src[:, kr, kc * P:(kc + 1) * P], ident[:, :])
                return last

            def composed(dst, right):
                for kc in range(KC):
                    for mk in range(KC):
                        last = pe.matmul(dst[:, kc * D:(kc + 1) * D], raw_sq["Wi"][:, mk, kc * P:(kc + 1) * P],
                                         right[:, mk, :], start=(kc == 0 and mk == 0), stop=(mk == KC - 1),
                                         skip_group_check=True)
                return last

            def feature_product(dst, n, acts, start, col=0, done=None):
                w_hi, w_lo = split[n]
                a_hi, a_lo = acts
                first = start
                for oc in range(KC):
                    o = dst[:, oc * TOK:(oc + 1) * TOK]
                    at = slice(col + oc * P, col + (oc + 1) * P)
                    for kc in range(KC):
                        for w, a in ((w_hi, a_hi), (w_hi, a_lo), (w_lo, a_hi)):
                            last = pe.matmul(o, w[:, kc, at], a[:, kc, :], start=first,
                                             stop=(kc == KC - 1 and w is w_lo), skip_group_check=True)
                            first = False
                return last

            def token_product(dst, w, acts, s, start):
                a_hi, a_lo = acts
                first = start
                for kc in range(KC):
                    for a, part in ((a_hi, 0), (a_hi, 1), (a_lo, 0)):
                        last = pe.matmul(dst, a[:, kc, s * P:(s + 1) * P], w(part, kc), start=first,
                                         stop=(kc == KC - 1 and a is a_lo), skip_group_check=True)
                        first = False
                return last

            def recurrence(i, t, k):
                if not k.has(i):
                    return
                o = step_of(rec[i % 2], t)
                pe.wait_ge(uh_ready[t], k.n(i))
                for oc in range(KC):
                    for kc in range(KC):
                        for w in a16:
                            pe.matmul(o[:, oc, :], w[:, kc, oc * P:(oc + 1) * P], u_hi[t % 2][:, kc, :],
                                      start=False, stop=False, skip_group_check=True)
                pe.wait_ge(ul_ready[t], k.n(i))
                for oc in range(KC):
                    for kc in range(KC):
                        last = pe.matmul(o[:, oc, :], a16[0][:, kc, oc * P:(oc + 1) * P], u_lo[t % 2][:, kc, :],
                                         start=False, stop=(kc == KC - 1), skip_group_check=True)
                last.then_inc(sum_done[t], 1)

            def pair(n, m, k):
                q, s = n // 2, n % 2
                if k.static and m == 0:
                    pe.wait_ge(w2_lo, 2 * q + 2)
                last = token_product(bank[B_PAIR[n]][:, :],
                                     lambda part, kc: split["w2"][part][:, kc, 2 * q:2 * q + 2, :].rearrange("p e c -> p (e c)"),
                                     hid_s[m % 2], s, True)
                last.then_inc(pair_done[n], 1)

            def kept_warm(n):
                for _ in range(n):
                    pe.matmul(bank[5][:, 0:P], ident[:, :], ident[:, :], start=True, stop=True)

            def x_transposed(a, k):
                if not k.has(a):
                    return
                if k.has(a - 3):
                    pe.wait_ge(hs_ready, k.n(a - 3))
                pe.wait_ge(xn1_ready, k.n(a))
                for s in range(HALVES):
                    for kc in range(KC):
                        last = pe.transpose(bank[B_TX][:, kc * TOK + s * P:kc * TOK + (s + 1) * P],
                                            xn1[a % 2][:, s, kc * P:(kc + 1) * P], ident[:, :])
                last.then_inc(tx_done, 1)

            def x1_transposed(c, k):
                if not k.has(c):
                    return
                if k.has(c - 1):
                    pe.wait_ge(acc_ready, k.n(c - 1))
                pe.wait_ge(xn2_ready, k.n(c))
                for s in range(HALVES):
                    for kc in range(KC):
                        last = pe.transpose(bank[B_T2][:, kc * TOK + s * P:kc * TOK + (s + 1) * P],
                                            xn2[c % 2][:, s, kc * P:(kc + 1) * P], ident[:, :])
                last.then_inc(t2_done, 1)

            def inp_product(a, k):
                if not k.has(a):
                    return
                if k.has(a - 4):
                    pe.wait_ge(pair_used[2], k.n(a - 4))
                pe.wait_ge(ret_hi, k.n(a))
                pe.wait_ge(ret_lo, k.n(a))
                feature_product(bank[B_INP], "inp", ret_s[a % 2], True).then_inc(inp_done, 1)

            def gate_product(a, k):
                if not k.has(a):
                    return
                if k.has(a - 4):
                    pe.wait_ge(pair_used[5], k.n(a - 4))
                feature_product(bank[B_GATE], "gate", ret_s[a % 2], True).then_inc(gate_done, 1)

            def addend_bm(a, k):
                if not k.has(a):
                    return
                pe.wait_ge(bias_in, k.n(a))
                rec_flat = flat(rec[a % 2][:, :, :])
                feature_product(rec_flat, "bm", ret_s[a % 2], False).then_inc(bm_done, 1)

            def addend_a(a, k):
                if not k.has(a):
                    return
                pe.wait_ge(cn_hi, k.n(a))
                pe.wait_ge(cn_lo, k.n(a))
                feature_product(flat(rec[a % 2][:, :, :]), "a", cn_s[a % 2], False).then_inc(ac_done, 1)

            pe.wait_ge(consts, 1)
            for n in range(WARMUP):
                at = slice((n * P) % (KC * TOK), (n * P) % (KC * TOK) + P)
                pe.matmul(flat(rec[0][:, :, :])[:, at], ident[:, :], ident[:, :], start=(n == 0),
                          stop=(n == WARMUP - 1), skip_group_check=True)
            pe.wait_ge(load["Wi"], 16)
            transposed(bank[3], raw_sq["Wi"]).then_inc(setup_pe, 1)
            pe.wait_ge(load["Wg"], 16)
            transposed(bank[4], raw_sq["Wg"]).then_inc(setup_pe, 1)
            pe.wait_ge(load["Bm"], 16)
            transposed(bank[5], raw_sq["Bm"]).then_inc(setup_pe, 1)
            x_transposed(0, first)
            pe.wait_ge(setup_act, 3)
            composed(flat(rec[1][:, :, :]), WgT).then_inc(setup_pe, 1)
            pe.wait_ge(setup_dve, 2)
            inp_product(0, first)
            pe.wait_ge(load["biases"], BIASES)
            pe.wait_ge(setup_act, 4)
            for n, m in enumerate((WgT, BmT)):
                for oc in range(KC):
                    for mk in range(KC):
                        last = pe.matmul(bank[4][:, n * KC + oc:n * KC + oc + 1], m[:, mk, oc * P:(oc + 1) * P],
                                         cols[:, mk:mk + 1], start=(n == 0 and oc == 0 and mk == 0),
                                         stop=(mk == KC - 1), skip_group_check=True)
            last.then_inc(setup_pe, 1)
            pe.wait_ge(setup_dve, 3)
            gate_product(0, first)
            pe.wait_ge(load["A"], 16)
            transposed(bank[5], raw_sq["A"]).then_inc(setup_pe, 1)
            composed(flat(rec[1][:, :, :]), BmT).then_inc(setup_pe, 1)
            x_transposed(1, first)
            pe.wait_ge(load["Wo"], 16)
            pe.wait_ge(setup_dve, 6)
            transposed(bank[4], raw_sq["Wo"]).then_inc(setup_pe, 1)
            pe.wait_ge(setup_dve, 8)
            addend_bm(0, first)
            addend_a(0, first)
            pe.wait_ge(setup_dve, 9)
            recurrence(0, 0, first)
            inp_product(1, first)
            recurrence(0, 1, first)
            gate_product(1, first)
            recurrence(0, 2, first)
            recurrence(0, 3, first)
            addend_bm(1, first)
            recurrence(0, 4, first)
            x_transposed(2, first)
            recurrence(0, 5, first)
            addend_a(1, first)
            recurrence(0, 6, first)
            recurrence(0, 7, first)
            inp_product(2, first)

            def iteration(i, k):
                a, c, d, e = i + 1, i - 1, i - 2, i - 3
                ahead = k.static and i == 1
                recurrence(i, 0, k)
                if ahead:
                    gate_product(a, k)
                else:
                    x_transposed(a, k)
                if k.has(e):
                    if k.has(d):
                        pe.wait_ge(lg_ready, k.n(d))
                    else:
                        pe.wait_ge(pair_used[5], k.n(e - 1))
                    pair(5, e, k)
                recurrence(i, 1, k)
                if k.has(c):
                    if k.has(d):
                        pe.wait_ge(sil_w_ready, k.n(d))
                    pe.wait_ge(st_hi, k.n(c))
                    pe.wait_ge(st_lo, k.n(c))
                    for s in range(HALVES):
                        last = token_product(bank[B_WO][:, s * D:(s + 1) * D],
                                             lambda part, kc: split["wo"][part][:, kc, :], st_s[c % 2], s, s == 0)
                    last.then_inc(wo_done, 1)
                if k.has(e):
                    if k.has(d):
                        pe.wait_ge(hid_ready, k.n(d))
                    else:
                        pe.wait_ge(pair_used[4], k.n(e))
                    pair(6, e, k)
                recurrence(i, 2, k)
                if ahead:
                    addend_bm(a, k)
                if k.has(d):
                    if k.static and d == 0:
                        pe.wait_ge(so_split, 1)
                    pe.wait_ge(hs_hi, k.n(d))
                    pe.wait_ge(hs_lo, k.n(d))
                    for s in range(HALVES):
                        last = token_product(bank[B_SO][:, s * D:(s + 1) * D],
                                             lambda part, kc: split["so"][part][:, kc, :], hs_s, s, s == 0)
                    last.then_inc(so_done, 1)
                if k.has(e):
                    if k.has(a):
                        pe.wait_ge(ret_ready, k.n(a))
                    if not k.has(d):
                        pe.wait_ge(pair_used[1], k.n(e))
                    pair(7, e, k)
                recurrence(i, 3, k)
                if ahead:
                    kept_warm(3)
                if k.has(d):
                    if k.has(c):
                        pe.wait_ge(x1_ready, k.n(c))
                    pe.wait_ge(hid_hi, k.n(d))
                    pe.wait_ge(hid_lo, k.n(d))
                    pair(0, d, k)
                if not ahead:
                    inp_product(a, k)
                    gate_product(a, k)
                recurrence(i, 4, k)
                if ahead:
                    addend_a(a, k)
                else:
                    addend_bm(a, k)
                if k.has(d):
                    if k.has(e):
                        pe.wait_ge(pair_used[7], k.n(e))
                    pair(1, d, k)
                if not ahead:
                    x1_transposed(c, k)
                recurrence(i, 5, k)
                if ahead:
                    kept_warm(2)
                    x1_transposed(c, k)
                if k.has(d):
                    if k.has(a):
                        pe.wait_ge(inp_ready, k.n(a))
                    elif k.has(e):
                        pe.wait_ge(pair_used[2], k.n(e))
                    pair(2, d, k)
                    pe.wait_ge(pair_used[0], k.n(d))
                    pair(3, d, k)
                    if k.has(e):
                        pe.wait_ge(pair_used[6], k.n(e))
                    pair(4, d, k)
                recurrence(i, 6, k)
                if ahead:
                    kept_warm(2)
                if k.has(c):
                    pe.wait_ge(xn2_hi, k.n(c))
                    pe.wait_ge(xn2_lo, k.n(c))
                    if k.static and c == 0:
                        pe.wait_ge(wide_lo, 2)
                    feature_product(bank[B_SHA], "sh", xn2_s[c % 2], True)
                    if k.has(d):
                        pe.wait_ge(pair_used[1], k.n(d))
                    feature_product(bank[B_SHB], "sh", xn2_s[c % 2], True, col=D).then_inc(sh_done, 1)
                    if k.has(a):
                        pe.wait_ge(gt_ready, k.n(a))
                    elif k.has(e):
                        pe.wait_ge(pair_used[5], k.n(e))
                    for kc in range(KC):
                        for v in xn2_s[c % 2]:
                            last = pe.matmul(bank[B_LG][:, 0:TOK], wgate_s[:, kc, :, :].rearrange("p g e -> p (g e)"),
                                             v[:, kc, :], start=(kc == 0 and v is xn2_s[c % 2][0]),
                                             stop=(kc == KC - 1), skip_group_check=True)
                    last.then_inc(lg_done, 1)
                recurrence(i, 7, k)
                if not ahead:
                    addend_a(a, k)
                if k.has(c):
                    if k.has(d):
                        pe.wait_ge(pair_used[3], k.n(d))
                    if k.static and i == 2:
                        pe.wait_ge(w2_lo, E)
                    if k.static and c == 0:
                        pe.wait_ge(wide_lo, 3)
                    feature_product(bank[B_W1A], "w1", xn2_s[c % 2], True)
                    if k.has(d):
                        pe.wait_ge(pair_used[4], k.n(d))
                    feature_product(bank[B_W1B], "w1", xn2_s[c % 2], True, col=D).then_inc(w1_done, 1)

            run(pe, iteration)

        @block.scalar
        def _(act):
            def tanh_step(i, t, k):
                if k.has(i):
                    if t == 0 and k.has(i - 2):
                        act.wait_ge(st_lo, k.n(i - 2))
                    act.wait_ge(sum_done[t], k.n(i))
                    act.activation(step_of(state[i % 2], t), step_of(rec[i % 2], t), ACT.Tanh,
                                   scale=1.0 / PSCALE).then_inc(st_ready[t], 1)

            def context_squares(a, k):
                if not k.has(a):
                    return
                act.wait_ge(turned, k.n(a))
                if k.has(a - 1):
                    act.wait_ge(r_ready, k.n(a - 1))
                    act.copy(c2[a % 2][:, :, :, 0], r[(a - 1) % 2][:, :, :, STEPS])
                for kc in range(KC):
                    last = act.activation(c2[a % 2][:, kc, :, 1:STEPS + 1],
                                          c_turned[:, :, :].rearrange("p (t k) b -> p k b t", k=KC)[:, kc], ACT.Square)
                last.then_inc(c2_ready, 1)

            def bias_set(a, k):
                if not k.has(a):
                    return
                if k.static and a == 0:
                    act.wait_ge(setup_dve, 6)
                if k.static and a == 1:
                    act.wait_ge(setup_dve, 8)
                if k.has(a - 2):
                    act.wait_ge(st_ready[STEPS - 1], k.n(a - 2))
                act.copy(flat(rec[a % 2][:, :, :]), flat(bm_bias[:, :, :])).then_inc(bias_in, 1)

            def ret_high(a, k):
                if not k.has(a):
                    return
                act.wait_ge(ret_ready, k.n(a))
                if k.has(a - 1):
                    act.wait_ge(bm_done, k.n(a - 1))
                act.copy(flat(ret_s[a % 2][0][:, :, :]), flat(ret[a % 2][:, :, :])).then_inc(ret_hi, 1)

            def inp_biased(a, k):
                if not k.has(a):
                    return
                act.wait_ge(inp_done, k.n(a))
                if k.has(a - 1):
                    act.wait_ge(cn_ready, k.n(a - 1))
                for kc in range(KC):
                    last = act.activation(inp[a % 2][:, kc, :], bank[B_INP][:, kc * TOK:(kc + 1) * TOK],
                                          ACT.Identity, bias=cols[:, kc:kc + 1])
                last.then_inc(inp_ready, 1)

            def gate_tanh(a, k):
                if not k.has(a):
                    return
                act.wait_ge(gate_done, k.n(a))
                if k.has(a - 2):
                    act.wait_ge(uh_ready[STEPS - 1], k.n(a - 2))
                for kc in range(KC):
                    last = act.activation(gt[a % 2][:, kc, :], bank[B_GATE][:, kc * TOK:(kc + 1) * TOK],
                                          ACT.Tanh, bias=half_gate_bias[:, kc:kc + 1], scale=0.5)
                last.then_inc(gt_ready, 1)

            def cn_high(a, k):
                if not k.has(a):
                    return
                act.wait_ge(cn_ready, k.n(a))
                if k.has(a - 1):
                    act.wait_ge(ac_done, k.n(a - 1))
                act.copy(flat(cn_s[a % 2][0][:, :, :]), flat(cn[a % 2][:, :, :])).then_inc(cn_hi, 1)

            def x_normalised(f, k):
                if not k.has(f):
                    return
                act.wait_ge(ln1_shift, k.n(f))
                if k.has(f - 1):
                    act.wait_ge(tx_done, k.n(f - 1))
                for s in range(HALVES):
                    last = act.activation(xn1[f % 2][:, s, :], x_sb[f % 2][:, s * D:(s + 1) * D], ACT.Identity,
                                          bias=nr1[f % 2][:, s:s + 1], scale=rs1[f % 2][:, s:s + 1])
                last.then_inc(xn1_ready, 1)

            def x1_normalised(c, k):
                if not k.has(c):
                    return
                act.wait_ge(ln2_shift, k.n(c))
                if k.has(c - 1):
                    act.wait_ge(t2_done, k.n(c - 1))
                for s in range(HALVES):
                    last = act.activation(xn2[c % 2][:, s, :], x1[c % 2][:, s, :], ACT.Identity,
                                          bias=nr2[c % 2][:, s:s + 1], scale=rs2[c % 2][:, s:s + 1])
                last.then_inc(xn2_ready, 1)

            def w2_high(e):
                act.wait_ge(load["w2"], 16 * E)
                act.copy(split["w2"][0][:, :, e, :], raw_w2[e][:, :, :]).then_inc(ffn2_hi, 1)

            act.wait_ge(consts, 1)
            act.activation(tgf[:, :], minus_half[:, 0:1], ACT.Silu).then_inc(setup_act, 1)
            x_normalised(0, first)
            context_squares(0, first)
            act.wait_ge(setup_pe, 1)
            act.copy(flat(split["inp"][0][:, :, :]), bank[3][:, :]).then_inc(setup_act, 1)
            act.wait_ge(setup_pe, 2)
            act.copy(flat(WgT[:, :, :]), bank[4][:, :]).then_inc(setup_act, 1)
            act.wait_ge(setup_pe, 3)
            act.mul(flat(BmT[:, :, :]), bank[5][:, :], PSCALE).then_inc(setup_act, 1)
            ret_high(0, first)
            act.wait_ge(setup_pe, 4)
            act.copy(flat(split["gate"][0][:, :, :]), flat(rec[1][:, :, :])).then_inc(setup_act, 1)
            x_normalised(1, first)
            act.wait_ge(load["biases"], BIASES)
            inp_biased(0, first)
            bias_set(0, first)
            act.wait_ge(setup_dve, 5)
            gate_tanh(0, first)
            act.wait_ge(setup_pe, 6)
            act.mul(flat(split["a"][0][:, :, :]), bank[5][:, :], -0.5 * PSCALE).then_inc(setup_act, 1)
            act.mul(flat(a16[0][:, :, :]), bank[5][:, :], 0.5 * PSCALE).then_inc(setup_act, 1)
            cn_high(0, first)
            act.wait_ge(setup_pe, 7)
            act.copy(flat(split["bm"][0][:, :, :]), flat(rec[1][:, :, :])).then_inc(setup_act, 1)
            context_squares(1, first)
            bias_set(1, first)
            ret_high(1, first)
            act.wait_ge(load["small"], SMALL)
            act.activation(tgx[:, :], gx[:, :], ACT.Tanh)
            act.wait_ge(setup_act, 1)
            act.activation(tgf[:, :], gf[:, :], ACT.Tanh).then_inc(setup_act, 1)
            tanh_step(0, 0, first)
            act.wait_ge(load["sh"], 16)
            act.copy(flat(split["sh"][0][:, :, :]), flat(raw_wide["sh"][:, :, :])).then_inc(wide_hi, 1)
            tanh_step(0, 1, first)
            inp_biased(1, first)
            tanh_step(0, 2, first)
            gate_tanh(1, first)
            tanh_step(0, 3, first)
            cn_high(1, first)
            x_normalised(2, first)
            tanh_step(0, 4, first)
            context_squares(2, first)
            act.wait_ge(load["wgate"], 16)
            act.wait_ge(setup_dve, 1)
            act.copy(wgate_s[:, :, :, 0:E], raw_wgate[:, :, :].unsqueeze(2).to_broadcast([P, KC, BLOCKS, E])).then_inc(wide_hi, 1)
            tanh_step(0, 5, first)
            act.wait_ge(load["w1"], 16)
            act.copy(flat(split["w1"][0][:, :, :]), flat(raw_wide["w1"][:, :, :])).then_inc(wide_hi, 1)
            tanh_step(0, 6, first)
            ret_high(2, first)
            act.wait_ge(setup_pe, 8)
            act.wait_ge(setup_act, 9)
            act.mul(flat(split["wo"][0][:, :, :]), bank[4][:, :], tgx[:, 0:1]).then_inc(setup_act, 1)
            tanh_step(0, 7, first)
            act.wait_ge(load["so"], 16)
            act.mul(flat(split["so"][0][:, :, :]), flat(raw_sq["so"][:, :, :]), tgf[:, 0:1]).then_inc(ffn2_hi, 1)
            w2_high(0)

            def iteration(i, k):
                a, c, d, f = i + 1, i - 1, i - 2, i + 2
                ahead = k.static and i == 1
                if k.has(c):
                    if k.has(c - 1):
                        act.wait_ge(wo_done, k.n(c - 1))
                    act.wait_ge(st_ready[STEPS - 1], k.n(c))
                    act.copy(flat(st_s[c % 2][0][:, :, :]), flat(state[c % 2][:, :, :])).then_inc(st_hi, 1)
                tanh_step(i, 0, k)
                if ahead:
                    inp_biased(a, k)
                if k.has(d):
                    act.wait_ge(w1_done, k.n(d))
                    if k.has(i - 3):
                        act.wait_ge(hid_ready, k.n(i - 3))
                    act.activation(flat(sil_w[:, :, :]), bank[B_W1A][:, :], ACT.Silu).then_inc(sil_w_ready, 1)
                    if k.has(i - 3):
                        act.wait_ge(so_done, k.n(i - 3))
                    act.wait_ge(hs_ready, k.n(d))
                    act.copy(flat(hs_s[0][:, :, :]), flat(hs[:, :, :])).then_inc(hs_hi, 1)
                tanh_step(i, 1, k)
                if ahead:
                    gate_tanh(a, k)
                else:
                    context_squares(a, k)
                bias_set(a, k)
                if k.has(d):
                    act.wait_ge(hid_ready, k.n(d))
                    if k.has(d - 2):
                        act.wait_ge(pair_done[E - 1], k.n(d - 2))
                    act.copy(flat(hid_s[d % 2][0][:, :, :]), flat(hid[:, :, :])).then_inc(hid_hi, 1)
                if ahead:
                    w2_high(1)
                tanh_step(i, 2, k)
                if ahead:
                    cn_high(a, k)
                if not ahead:
                    ret_high(a, k)
                if k.has(d):
                    act.wait_ge(ld_ready, k.n(d))
                    if k.has(d - 1):
                        act.wait_ge(numden, k.n(d - 1))
                    act.activation(flat(lt[:, :, :]), flat(ld[:, :, :]), ACT.Tanh, scale=0.5).then_inc(lt_ready, 1)
                if ahead:
                    w2_high(2)
                tanh_step(i, 3, k)
                if not ahead:
                    x1_normalised(c, k)
                if ahead:
                    w2_high(3)
                tanh_step(i, 4, k)
                if ahead:
                    x1_normalised(c, k)
                if not ahead:
                    inp_biased(a, k)
                    gate_tanh(a, k)
                if ahead:
                    w2_high(4)
                tanh_step(i, 5, k)
                if k.has(c):
                    act.wait_ge(t2_done, k.n(c))
                    if k.has(c - 1):
                        act.wait_ge(w1_done, k.n(c - 1))
                    act.copy(flat(xn2_s[c % 2][0][:, :, :]), bank[B_T2][:, :]).then_inc(xn2_hi, 1)
                if not ahead:
                    cn_high(a, k)
                if ahead:
                    w2_high(5)
                tanh_step(i, 6, k)
                x_normalised(f, k)
                if ahead:
                    w2_high(6)
                tanh_step(i, 7, k)
                if k.has(c):
                    act.wait_ge(sh_done, k.n(c))
                    if k.has(c - 1):
                        act.wait_ge(hs_ready, k.n(c - 1))
                    act.activation(flat(sil_s[:, :, :]), bank[B_SHA][:, :], ACT.Silu).then_inc(sil_s_ready, 1)
                if ahead:
                    w2_high(7)

            run(act, iteration)

        @block.vector
        def _(dve):
            def low(n, whole, hi, signal):
                dve.tensor_tensor(n, whole, hi.bitcast(F32), ALU.subtract).then_inc(signal, 1)

            def gated_state(i, t, k):
                if not k.has(i):
                    return
                m, t_next = (i, t + 1) if t + 1 < STEPS else (i + 1, 0)
                if not k.has(m):
                    return
                p = t_next % 2
                old, gate = step_of(state[i % 2], t), step_of(gt[m % 2], t_next)
                if t_next == 0:
                    dve.wait_ge(gt_ready, k.n(m))
                dve.wait_ge(st_ready[t], k.n(i))
                dve.scalar_tensor_tensor(out=u_hi[p][:, :, :], in0=gate, scalar=1.0, in1=old,
                                         op0=ALU.add, op1=ALU.mult).then_inc(uh_ready[t_next], 1)
                dve.scalar_tensor_tensor(out=u_full[p][:, :, :], in0=gate, scalar=1.0, in1=old,
                                         op0=ALU.add, op1=ALU.mult).then_inc(uf_ready, 1)
                dve.wait_ge(uf_ready, k.steps(m, t_next))
                dve.tensor_tensor(u_lo[p][:, :, :], u_full[p][:, :, :], u_hi[p][:, :, :],
                                  ALU.subtract).then_inc(ul_ready[t_next], 1)

            def add_pair(n, m, k):
                if not k.has(m):
                    return
                q, s = n // 2, n % 2
                o = acc[m % 2][:, s, :]
                dve.wait_ge(pair_done[n], k.n(m))
                dve.wait_ge(acc_ready, k.n(m))
                if n >= 2:
                    dve.wait_ge(pair_used[n - 2], k.n(m))
                dve.scalar_tensor_tensor(out=o, in0=bank[B_PAIR[n]][:, 0:D], scalar=wts[m % 2][:, s, 2 * q:2 * q + 1],
                                         in1=o, op0=ALU.mult, op1=ALU.add).then_inc(pair_half, 1)
                dve.wait_ge(pair_half, k.pairs(m, n))
                dve.scalar_tensor_tensor(out=o, in0=bank[B_PAIR[n]][:, D:2 * D], scalar=wts[m % 2][:, s, 2 * q + 1:2 * q + 2],
                                         in1=o, op0=ALU.mult, op1=ALU.add).then_inc(pair_used[n], 1)

            def context_turned(a, k):
                if not k.has(a):
                    return
                if k.has(a - 1):
                    dve.wait_ge(c2_ready, k.n(a - 1))
                dve.wait_ge(c_in[a % 2], k.context(a))
                dve.transpose(flat(c_turned[:, :, :]), flat(c_sb[a % 2][:, :, :])).then_inc(turned, 1)

            def scanned(a, k):
                if not k.has(a):
                    return
                dve.wait_ge(c2_ready, k.n(a))
                dve.tensor_tensor_scan(r[a % 2][:, :, :, :].rearrange("p c b t -> p (c b t)"),
                                       dmask[:, :, :, :].rearrange("p c b t -> p (c b t)"),
                                       c2[a % 2][:, :, :, :].rearrange("p c b t -> p (c b t)"),
                                       0.0, ALU.mult, ALU.add).then_inc(r_ready, 1)

            def retained(a, k):
                if not k.has(a):
                    return
                dve.wait_ge(r_ready, k.n(a))
                dve.wait_ge(tx_done, k.n(a))
                if k.has(a - 1):
                    dve.wait_ge(ret_hi, k.n(a - 1))
                for kc in range(KC):
                    last = dve.tensor_tensor(halves(ret[a % 2][:, kc, :]), halves(bank[B_TX][:, kc * TOK:(kc + 1) * TOK]),
                                             by_time(r[a % 2][:, kc, :, 1:STEPS + 1]), ALU.mult)
                last.then_inc(ret_ready, 1)

            def ret_low(a, k):
                if not k.has(a):
                    return
                dve.wait_ge(ret_hi, k.n(a))
                dve.wait_ge(ret_ready, k.n(a))
                if k.has(a - 1):
                    dve.wait_ge(bm_done, k.n(a - 1))
                low(flat(ret_s[a % 2][1][:, :, :]), flat(ret[a % 2][:, :, :]), flat(ret_s[a % 2][0][:, :, :]), ret_lo)

            def blend(a, k):
                if not k.has(a):
                    return
                dve.wait_ge(inp_ready, k.n(a))
                dve.wait_ge(gt_ready, k.n(a))
                if k.has(a - 1):
                    dve.wait_ge(cn_hi, k.n(a - 1))
                    dve.wait_ge(cn_lo, k.n(a - 1))
                dve.scalar_tensor_tensor(out=flat(cn[a % 2][:, :, :]), in0=flat(gt[a % 2][:, :, :]), scalar=-1.0,
                                         in1=flat(inp[a % 2][:, :, :]), op0=ALU.add, op1=ALU.mult).then_inc(cn_ready, 1)

            def cn_low(a):
                dve.wait_ge(cn_hi, first.n(a))
                if a > 0:
                    dve.wait_ge(ac_done, first.n(a - 1))
                dve.wait_ge(cn_ready, first.n(a))
                low(flat(cn_s[a % 2][1][:, :, :]), flat(cn[a % 2][:, :, :]), flat(cn_s[a % 2][0][:, :, :]), cn_lo)

            def projected(c, k):
                if not k.has(c):
                    return
                dve.wait_ge(wo_done, k.n(c))
                dve.wait_ge(xr_ready, k.n(c))
                dve.tensor_tensor(x1[c % 2][:, :, :].rearrange("p s d -> p (s d)"), bank[B_WO][:, :],
                                  xr_sb[c % 2][:, :], ALU.add).then_inc(x1_ready, 1)

            def x_stats(f, k):
                if not k.has(f):
                    return
                dve.wait_ge(x_in[f % 2], k.dma(f))
                for s in range(HALVES):
                    last = dve.bn_stats(st1[f % 2][:, s, :], x_sb[f % 2][:, s * D:(s + 1) * D])
                last.then_inc(ln1_stats, 1)

            def x_aggregate(f, k):
                if not k.has(f):
                    return
                for s in range(HALVES):
                    last = dve.bn_aggr(mv1[f % 2][:, s, :], st1[f % 2][:, s, :])
                last.then_inc(ln1_aggr, 1)

            def x_variance(f, k):
                if not k.has(f):
                    return
                dve.wait_ge(ln1_aggr, k.n(f))
                dve.tensor_scalar(ve1[f % 2][:, :], mv1[f % 2][:, :, 1], EPS, None, ALU.add)
                dve.tensor_scalar(nm1[f % 2][:, :], mv1[f % 2][:, :, 0], -1.0, None, ALU.mult).then_inc(ln1_var, 1)

            def first_moments(f):
                x_stats(f, first)
                dve.wait_ge(ln1_stats, first.n(f))
                x_aggregate(f, first)
                x_variance(f, first)

            dve.memset(c2[0][:, :, :, 0], 0.0)
            dve.memset(wgate_s[:, :, :, :].bitcast(F32), 0.0)
            dve.memset(dmask[:, :, :, 0], 0.0)
            dve.memset(u_lo[0][:, :, :], 0.0).then_inc(ul_ready[0], 1)
            dve.memset(u_hi[0][:, :, :], 0.0).then_inc(uh_ready[0], 1)
            first_moments(0)
            context_turned(0, first)
            dve.wait_ge(load["decay"], 16 * KC)
            for kc in range(KC):
                last = dve.tensor_copy(dmask[:, kc, :, 1:STEPS + 1],
                                       dec_cols[:, kc:kc + 1].unsqueeze(2).to_broadcast([P, B, STEPS]))
            last.then_inc(setup_dve, 1)
            dve.wait_ge(setup_dve, 1)
            scanned(0, first)
            retained(0, first)
            dve.wait_ge(setup_act, 2)
            low(flat(split["inp"][1][:, :, :]), bank[3][:, :], flat(split["inp"][0][:, :, :]), setup_dve)
            ret_low(0, first)
            first_moments(1)
            dve.wait_ge(setup_act, 5)
            low(flat(split["gate"][1][:, :, :]), flat(rec[1][:, :, :]), flat(split["gate"][0][:, :, :]), setup_dve)
            dve.wait_ge(load["biases"], BIASES)
            dve.wait_ge(setup_pe, 5)
            dve.tensor_tensor(half_gate_bias[:, :], bank[4][:, 0:KC], cols[:, KC:2 * KC], ALU.add).then_inc(setup_dve, 1)
            dve.wait_ge(setup_dve, 4)
            dve.tensor_scalar(half_gate_bias[:, :], half_gate_bias[:, :], 0.5, None, ALU.mult).then_inc(setup_dve, 1)
            dve.tensor_copy(bm_bias[:, :, :], bank[4][:, KC:2 * KC].unsqueeze(2).to_broadcast([P, KC, TOK])).then_inc(setup_dve, 1)
            context_turned(1, first)
            blend(0, first)
            dve.wait_ge(setup_act, 7)
            dve.scalar_tensor_tensor(out=flat(split["a"][1][:, :, :]), in0=bank[5][:, :], scalar=-0.5 * PSCALE,
                                     in1=flat(split["a"][0][:, :, :]).bitcast(F32),
                                     op0=ALU.mult, op1=ALU.subtract).then_inc(setup_dve, 1)
            cn_low(0)
            dve.wait_ge(setup_act, 8)
            low(flat(split["bm"][1][:, :, :]), flat(rec[1][:, :, :]), flat(split["bm"][0][:, :, :]), setup_dve)
            dve.scalar_tensor_tensor(out=flat(a16[1][:, :, :]), in0=bank[5][:, :], scalar=0.5 * PSCALE,
                                     in1=flat(a16[0][:, :, :]), op0=ALU.mult, op1=ALU.subtract).then_inc(setup_dve, 1)
            scanned(1, first)
            retained(1, first)
            ret_low(1, first)
            gated_state(0, 0, first)
            dve.wait_ge(setup_act, 9)
            dve.tensor_scalar(tgbo[:, :], bo_all[:, :], tgx[:, 0:1], None, ALU.mult).then_inc(setup_dve, 1)
            for e in range(E):
                dve.memset(tri[:, e, e:E], 0.0)
                if e > 0:
                    last = dve.memset(tri[:, e, 0:e], 1.0)
            last.then_inc(setup_dve, 1)
            gated_state(0, 1, first)
            first_moments(2)
            gated_state(0, 2, first)
            context_turned(2, first)
            blend(1, first)
            gated_state(0, 3, first)
            cn_low(1)
            gated_state(0, 4, first)
            scanned(2, first)
            gated_state(0, 5, first)
            retained(2, first)
            gated_state(0, 6, first)
            ret_low(2, first)
            dve.wait_ge(setup_act, 10)
            dve.scalar_tensor_tensor(out=flat(split["wo"][1][:, :, :]), in0=bank[4][:, :], scalar=tgx[:, 0:1],
                                     in1=flat(split["wo"][0][:, :, :]).bitcast(F32),
                                     op0=ALU.mult, op1=ALU.subtract).then_inc(setup_dve, 1)
            gated_state(0, 7, first)
            dve.wait_ge(ffn2_hi, 1)
            dve.scalar_tensor_tensor(out=flat(split["so"][1][:, :, :]), in0=flat(raw_sq["so"][:, :, :]), scalar=tgf[:, 0:1],
                                     in1=flat(split["so"][0][:, :, :]).bitcast(F32),
                                     op0=ALU.mult, op1=ALU.subtract).then_inc(so_split, 1)

            def iteration(i, k):
                a, c, d, e, f = i + 1, i - 1, i - 2, i - 3, i + 2
                ahead = k.static and i == 1
                sparse = k.static and i <= 2
                early = k.static and i == 2
                gated_state(i, 0, k)
                if k.has(d):
                    dve.wait_ge(sil_w_ready, k.n(d))
                    if k.has(d - 1):
                        dve.wait_ge(hid_hi, k.n(d - 1))
                        dve.wait_ge(hid_lo, k.n(d - 1))
                    dve.tensor_tensor(flat(hid[:, :, :]), bank[B_W1B][:, :], flat(sil_w[:, :, :]),
                                      ALU.mult).then_inc(hid_ready, 1)
                if not ahead:
                    context_turned(a, k)
                gated_state(i, 1, k)
                if ahead:
                    blend(a, k)
                if not ahead:
                    scanned(a, k)
                if not ahead:
                    retained(a, k)
                if early:
                    gated_state(i, 2, k)
                    projected(c, k)
                if k.has(d):
                    dve.wait_ge(lg_ready, k.n(d))
                    dve.tensor_reduce(lmax[:, :], lg[:, :, :], AX_X, ALU.max).then_inc(lmax_ready, 1)
                if k.has(d):
                    if k.has(d - 1):
                        dve.wait_ge(beat_ready, k.n(d - 1))
                    mine = lg[:, :, :].unsqueeze(3).to_broadcast([P, HALVES, E, E])
                    others = lg[:, :, :].unsqueeze(2).to_broadcast([P, HALVES, E, E])
                    dve.tensor_tensor(more[:, :, :, :], others, mine, ALU.is_gt)
                    dve.tensor_tensor(same[:, :, :, :], others, mine, ALU.is_equal).then_inc(same_ready, 1)
                add_pair(5, e, k)
                if k.has(d):
                    dve.wait_ge(lmax_ready, k.n(d))
                    dve.tensor_tensor(ld[:, :, :], lg[:, :, :], lmax[:, :].unsqueeze(2).to_broadcast([P, HALVES, E]),
                                      ALU.subtract).then_inc(ld_ready, 1)
                if not early:
                    gated_state(i, 2, k)
                if not early:
                    projected(c, k)
                if not ahead:
                    ret_low(a, k)
                if k.has(c):
                    dve.wait_ge(x1_ready, k.n(c))
                    for s in range(HALVES):
                        last = dve.bn_stats(st2[c % 2][:, s, :], x1[c % 2][:, s, :])
                    last.then_inc(ln2_stats, 1)
                    if sparse:
                        gated_state(i, 3, k)
                    dve.wait_ge(ln2_stats, k.n(c))
                if k.has(d):
                    dve.wait_ge(lt_ready, k.n(d))
                    dve.tensor_scalar(num[:, :, :], lt[:, :, :], 1.0, None, ALU.add)
                    dve.tensor_scalar(den[:, :, :], lt[:, :, :], -1.0, 1.0, ALU.mult, ALU.add).then_inc(numden, 1)
                if k.has(c):
                    for s in range(HALVES):
                        last = dve.bn_aggr(mv2[c % 2][:, s, :], st2[c % 2][:, s, :])
                    last.then_inc(ln2_aggr, 1)
                if k.has(d):
                    dve.wait_ge(numden, k.n(d))
                    dve.reciprocal(rden[:, :, :], den[:, :, :]).then_inc(rden_ready, 1)
                if k.has(c):
                    dve.wait_ge(ln2_aggr, k.n(c))
                    dve.tensor_scalar(ve2[c % 2][:, :], mv2[c % 2][:, :, 1], EPS, None, ALU.add)
                    dve.tensor_scalar(nm2[c % 2][:, :], mv2[c % 2][:, :, 0], -1.0, None, ALU.mult).then_inc(ln2_var, 1)
                add_pair(6, e, k)
                if not sparse:
                    gated_state(i, 3, k)
                if k.has(d):
                    if k.has(d - 2):
                        dve.wait_ge(out_done[d % 2], k.dma(d - 2))
                    dve.wait_ge(so_done, k.n(d))
                    dve.tensor_tensor(acc[d % 2][:, :, :].rearrange("p s d -> p (s d)"), bank[B_SO][:, :],
                                      x1[d % 2][:, :, :].rearrange("p s d -> p (s d)"), ALU.add).then_inc(acc_ready, 1)
                    dve.wait_ge(rden_ready, k.n(d))
                    dve.tensor_tensor(ex[:, :, :], num[:, :, :], rden[:, :, :], ALU.mult).then_inc(ex_ready, 1)
                add_pair(7, e, k)
                if k.has(d):
                    dve.wait_ge(ex_ready, k.n(d))
                    dve.tensor_reduce(esum[:, :], ex[:, :, :], AX_X, ALU.add).then_inc(esum_ready, 1)
                    dve.wait_ge(rank_ready, k.n(d))
                    dve.scalar_tensor_tensor(out=flat(picked[:, :, :]), in0=flat(rank[:, :, :]), scalar=2.0,
                                             in1=flat(ex[:, :, :]), op0=ALU.is_lt, op1=ALU.mult).then_inc(picked_ready, 1)
                    dve.wait_ge(esum_ready, k.n(d))
                    dve.reciprocal(rsum[:, :], esum[:, :]).then_inc(rsum_ready, 1)
                    dve.wait_ge(rsum_ready, k.n(d))
                    dve.tensor_scalar(rsg[:, :], rsum[:, :], tgf[:, 0:1], None, ALU.mult).then_inc(rsg_ready, 1)
                gated_state(i, 4, k)
                if k.has(d):
                    dve.wait_ge(rsg_ready, k.n(d))
                    dve.wait_ge(picked_ready, k.n(d))
                    dve.tensor_tensor(wts[d % 2][:, :, :], picked[:, :, :],
                                      rsg[:, :].unsqueeze(2).to_broadcast([P, HALVES, E]), ALU.mult).then_inc(wts_ready, 1)
                x_stats(f, k)
                if k.has(d):
                    dve.wait_ge(wts_ready, k.n(d))
                add_pair(0, d, k)
                gated_state(i, 5, k)
                if k.has(f):
                    dve.wait_ge(ln1_stats, k.n(f))
                if not ahead:
                    blend(a, k)
                x_aggregate(f, k)
                if k.has(c):
                    dve.wait_ge(xn2_hi, k.n(c))
                    if k.has(c - 1):
                        dve.wait_ge(w1_done, k.n(c - 1))
                    low(flat(xn2_s[c % 2][1][:, :, :]), bank[B_T2][:, :], flat(xn2_s[c % 2][0][:, :, :]), xn2_lo)
                x_variance(f, k)
                add_pair(1, d, k)
                gated_state(i, 6, k)
                add_pair(2, d, k)
                add_pair(3, d, k)
                gated_state(i, 7, k)
                add_pair(4, d, k)
                if k.has(c):
                    dve.wait_ge(lg_done, k.n(c))
                    product = bank[B_LG][:, 0:TOK].rearrange("p (s g q) -> p s g q", s=HALVES, g=BLOCKS)
                    for g in range(BLOCKS):
                        last = dve.transpose(lg_t[32 * g:32 * (g + 1), :, :], product[32 * g:32 * (g + 1), :, g, :])
                    last.then_inc(lg_t_ready, 1)
                    dve.wait_ge(lg_t_ready, k.n(c))
                    dve.tensor_tensor(lg_b[:, :, :], lg_t[:, :, 0:E],
                                      gb_all[:, :].unsqueeze(1).to_broadcast([P, HALVES, E]), ALU.add).then_inc(lg_b_ready, 1)
                    dve.wait_ge(lg_b_ready, k.n(c))
                    dve.tensor_tensor(lg[:, :, :], lg_t[:, :, E:2 * E], lg_b[:, :, :], ALU.add).then_inc(lg_ready, 1)
                if k.has(c):
                    dve.wait_ge(sil_s_ready, k.n(c))
                    if k.has(c - 1):
                        dve.wait_ge(hs_hi, k.n(c - 1))
                        dve.wait_ge(hs_lo, k.n(c - 1))
                    dve.tensor_tensor(flat(hs[:, :, :]), bank[B_SHB][:, :], flat(sil_s[:, :, :]),
                                      ALU.mult).then_inc(hs_ready, 1)

            run(dve, iteration)

        @block.gpsimd
        def _(pool):
            pool.memset(minus_half[:, :], -0.5)
            pool.memset(ident[:, :], 0.0).then_inc(zeros_pool := sem("zeros_pool"), 1)
            pool.wait_ge(zeros_pool, 1)
            pool.affine_select(out=ident[:, :], in_=ident[:, :], compare_op=ALU.not_equal, fill=1.0, base=0,
                               pattern=[[-1, P]], channel_multiplier=1).then_inc(consts, 1)

            def low(n, whole, hi, signal):
                pool.tensor_tensor(n, whole, hi.bitcast(F32), ALU.subtract).then_inc(signal, 1)

            def x_rstd(f, k):
                if not k.has(f):
                    return
                pool.wait_ge(ln1_var, k.n(f))
                pool.tensor_tensor(rs1[f % 2][:, :], ve1[f % 2][:, :], minus_half[:, :], ALU.pow).then_inc(ln1_rstd, 1)
                pool.wait_ge(ln1_rstd, k.n(f))
                pool.tensor_tensor(nr1[f % 2][:, :], nm1[f % 2][:, :], rs1[f % 2][:, :], ALU.mult).then_inc(ln1_shift, 1)

            def residual(i, k):
                if not k.has(i):
                    return
                pool.wait_ge(xr_in[i % 2], k.dma(i))
                for s in range(HALVES):
                    last = pool.tensor_tensor(xr_sb[i % 2][:, s * D:(s + 1) * D], xr_sb[i % 2][:, s * D:(s + 1) * D],
                                              tgbo[:, :], ALU.add)
                last.then_inc(xr_ready, 1)

            def w2_low(e):
                pool.wait_ge(ffn2_hi, e + 2)
                low(split["w2"][1][:, :, e, :], raw_w2[e][:, :, :], split["w2"][0][:, :, e, :], w2_lo)

            with nc.allow_non_contiguous_dma(reason="small vectors"):
                for kc in range(KC):
                    pool.dma_start(dec_cols[:, kc:kc + 1],
                                 decay[0, kc * HEADS // KC:(kc + 1) * HEADS // KC, :].unsqueeze(1).to_broadcast([HEADS // KC, D // HEADS, 1])).then_inc(load["decay"], 16)
            x_rstd(0, first)
            with nc.allow_non_contiguous_dma(reason="small vectors"):
                pool.dma_start(cols[:, 0:KC], bi.rearrange("(k p) -> p k", p=P)).then_inc(load["biases"], 16)
                pool.dma_start(cols[:, KC:2 * KC], bg.rearrange("(k p) -> p k", p=P)).then_inc(load["biases"], 16)
            x_rstd(1, first)
            pool.wait_ge(wide_hi, 1)
            low(flat(split["sh"][1][:, :, :]), flat(raw_wide["sh"][:, :, :]), flat(split["sh"][0][:, :, :]), wide_lo)
            x_rstd(2, first)
            pool.wait_ge(wide_hi, 2)
            low(wgate_s[:, :, :, E:2 * E], raw_wgate[:, :, :].unsqueeze(2).to_broadcast([P, KC, BLOCKS, E]),
                wgate_s[:, :, :, 0:E], wide_lo)
            pool.wait_ge(setup_dve, 10)
            residual(0, first)
            pool.wait_ge(wide_hi, 3)
            low(flat(split["w1"][1][:, :, :]), flat(raw_wide["w1"][:, :, :]), flat(split["w1"][0][:, :, :]), wide_lo)

            def cn_low(a, k):
                if not k.has(a):
                    return
                pool.wait_ge(cn_hi, k.n(a))
                if k.has(a - 1):
                    pool.wait_ge(ac_done, k.n(a - 1))
                low(flat(cn_s[a % 2][1][:, :, :]), flat(cn[a % 2][:, :, :]), flat(cn_s[a % 2][0][:, :, :]), cn_lo)

            def iteration(i, k):
                a, c, d, f = i + 1, i - 1, i - 2, i + 2
                ahead = k.static and i == 1
                if k.has(c):
                    pool.wait_ge(st_hi, k.n(c))
                    if k.has(c - 1):
                        pool.wait_ge(wo_done, k.n(c - 1))
                    low(flat(st_s[c % 2][1][:, :, :]), flat(state[c % 2][:, :, :]), flat(st_s[c % 2][0][:, :, :]), st_lo)
                if k.has(d):
                    pool.wait_ge(hs_hi, k.n(d))
                    if k.has(d - 1):
                        pool.wait_ge(so_done, k.n(d - 1))
                    low(flat(hs_s[1][:, :, :]), flat(hs[:, :, :]), flat(hs_s[0][:, :, :]), hs_lo)
                    pool.wait_ge(hid_hi, k.n(d))
                    if k.has(d - 2):
                        pool.wait_ge(pair_done[E - 1], k.n(d - 2))
                    low(flat(hid_s[d % 2][1][:, :, :]), flat(hid[:, :, :]), flat(hid_s[d % 2][0][:, :, :]), hid_lo)
                if k.has(d):
                    if k.static and d == 0:
                        pool.wait_ge(setup_dve, 11)
                    pool.wait_ge(same_ready, k.n(d))
                    pool.tensor_tensor(same_l[:, :, :, :].rearrange("p s e f -> p s (e f)"),
                                       same[:, :, :, :].rearrange("p s e f -> p s (e f)"),
                                       tri[:, :, :].rearrange("p e f -> p (e f)").unsqueeze(1).to_broadcast([P, HALVES, E * E]),
                                       ALU.mult).then_inc(samel_ready, 1)
                    pool.wait_ge(samel_ready, k.n(d))
                    pool.tensor_tensor(beat[:, :, :, :].rearrange("p s e f -> p (s e f)"),
                                       more[:, :, :, :].rearrange("p s e f -> p (s e f)"),
                                       same_l[:, :, :, :].rearrange("p s e f -> p (s e f)"), ALU.add).then_inc(beat_ready, 1)
                    if k.has(d - 1):
                        pool.wait_ge(picked_ready, k.n(d - 1))
                    pool.wait_ge(beat_ready, k.n(d))
                    b8 = beat[:, :, :, :].rearrange("p s e f -> p (s e) f")
                    pool.tensor_tensor(b4[:, :, :], b8[:, :, 0:4], b8[:, :, 4:8], ALU.add).then_inc(b4_ready, 1)
                    pool.wait_ge(b4_ready, k.n(d))
                    pool.tensor_tensor(b2[:, :, :], b4[:, :, 0:2], b4[:, :, 2:4], ALU.add).then_inc(b2_ready, 1)
                    pool.wait_ge(b2_ready, k.n(d))
                    pool.tensor_tensor(flat(rank[:, :, :]), b2[:, :, 0], b2[:, :, 1], ALU.add).then_inc(rank_ready, 1)
                if ahead:
                    w2_low(0)
                    cn_low(a, k)
                if k.has(c):
                    pool.wait_ge(ln2_var, k.n(c))
                    pool.tensor_tensor(rs2[c % 2][:, :], ve2[c % 2][:, :], minus_half[:, :], ALU.pow).then_inc(ln2_rstd, 1)
                    pool.wait_ge(ln2_rstd, k.n(c))
                    pool.tensor_tensor(nr2[c % 2][:, :], nm2[c % 2][:, :], rs2[c % 2][:, :], ALU.mult).then_inc(ln2_shift, 1)
                if ahead:
                    for expert in range(1, 5):
                        w2_low(expert)
                if k.static and i == 2:
                    for expert in range(6, E):
                        w2_low(expert)
                if not ahead:
                    cn_low(a, k)
                x_rstd(f, k)
                residual(i, k)
                if ahead:
                    w2_low(5)

            run(pool, iteration)


_INS = ["x", "ctx_1024", "g_xattn", "g_ffn", "L0_xattn_Wi", "L0_xattn_bi", "L0_xattn_Wg", "L0_xattn_bg", "L0_xattn_A",
        "L0_xattn_Bm", "L0_xattn_Wo", "L0_xattn_bo", "L0_xattn_decay", "L0_ffn_w_shared_in", "L0_ffn_w_shared_out",
        "L0_ffn_w1_shared", "L0_ffn_w2", "L0_ffn_w_gate", "L0_ffn_gate_bias"]
_OUTS = [((B, S, D), "float32")]


def kernel(**inputs):
    import numpy as _np
    import concourse.bacc as _bacc
    from concourse import mybir as _mybir
    from concourse.bass_utils import run_bass_kernel_spmd as _run

    nc = _bacc.Bacc("TRN2", target_bir_lowering=False, num_devices=1)
    arrays, args = {}, []
    for name in _INS:
        a = _np.ascontiguousarray(inputs[name])
        arrays[f"in_{name}_dram"] = a
        args.append(nc.dram_tensor(f"in_{name}_dram", a.shape, _mybir.dt.from_np(a.dtype), kind="ExternalInput").ap())
    for i, (shape, dtype) in enumerate(_OUTS):
        dt = _mybir.dt.from_np(_np.dtype(dtype))
        args.append(nc.dram_tensor(f"out_{i}_dram", shape, dt, kind="ExternalOutput").ap())
    gated_layer(nc, *args)
    r = _run(nc, [arrays], core_ids=[0])
    return r.results[0]["out_0_dram"]
```
